# Optimizing a Trainium2 kernel written in Bass

```python
import numpy as np
import jax
import jax.numpy as jnp

def _softmax(x, axis=-1):
    return jax.nn.softmax(x, axis=axis)

def _gelu(x):
    return jax.nn.gelu(x, approximate=True)

def _silu(x):
    return jax.nn.silu(x)

def _sigmoid(x):
    return jax.nn.sigmoid(x)

def _layernorm(x, axis=-1, eps=1e-05):
    m = jnp.mean(x, axis=axis, keepdims=True)
    v = jnp.var(x, axis=axis, keepdims=True)
    return (x - m) / jnp.sqrt(v + eps)

def _scatter_add(tgt, idx, src, axis=0):
    return tgt.at[idx].add(src)

def _segment_sum(src, seg, n):
    return jax.ops.segment_sum(src, seg, n)
kernel_name = 'mk_gnn_preln_d2_gnn_r32_2545f6'

def setup_inputs(seed: int=0):
    np.random.seed(seed)
    _w = jnp.asarray

    def _rec_inputs():
        import jax
        import jax.numpy as jnp
        _gk = jax.random.key(seed)
        x = -0.000202 + 1 * jax.random.normal(jax.random.fold_in(_gk, 1), (3125, 64), jnp.float32)
        _s = jax.random.randint(jax.random.fold_in(_gk, 2), (50000,), 0, 3125, jnp.int32)
        _d = jax.random.randint(jax.random.fold_in(_gk, 3), (50000,), 0, 3125, jnp.int32)
        _loop = jnp.arange(3125, dtype=jnp.int32)
        src = jnp.concatenate([_s, _d, _loop])
        dst = jnp.concatenate([_d, _s, _loop])
        _o = jnp.argsort(dst, stable=True)
        src = src[_o]
        dst = dst[_o]
        edge_weight = jax.random.uniform(jax.random.fold_in(_gk, 12), (103125,), jnp.float32, 0.0, 0.999998)
        node_vec = jax.random.uniform(jax.random.fold_in(_gk, 13), (3125,), jnp.float32, 0.0, 0.999957)
        return (x, src, dst, edge_weight, node_vec)
    x, src, dst, edge_weight, node_vec = _rec_inputs()

    def _L0_gnn_setup():
        import jax, jax.numpy as jnp
        import numpy as np

        def gin_layer(x, src, dst, ew, w1, b1, w2, b2):
            msg = x[src] * ew[:, None]
            agg = jax.ops.segment_sum(msg, dst, num_segments=x.shape[0])
            h = agg + x
            h = jax.nn.relu(h @ w1 + b1)
            return h @ w2 + b2
        key = jax.random.key(seed)
        ks = jax.random.split(key, 16)
        N, E, D = (3125, 31250, 64)
        x = jax.random.normal(ks[0], (N, D), dtype=jnp.float32)
        edge_index = jax.random.randint(ks[1], (2, E), 0, N)
        edge_weight = jax.random.uniform(ks[2], (E,), dtype=jnp.float32)

        def lin(k, fi, fo):
            return jax.random.normal(k, (fi, fo), dtype=jnp.float32) * (1.0 / np.sqrt(fi))
        return {'x': x, 'edge_index': edge_index, 'edge_weight': edge_weight, 'w11': lin(ks[3], 64, 64), 'b11': jnp.zeros(64, jnp.float32), 'w12': lin(ks[4], 64, 64), 'b12': jnp.zeros(64, jnp.float32), 'w21': lin(ks[5], 64, 128), 'b21': jnp.zeros(128, jnp.float32), 'w22': lin(ks[6], 128, 64), 'b22': jnp.zeros(64, jnp.float32), 'w31': lin(ks[7], 64, 64), 'b31': jnp.zeros(64, jnp.float32), 'w32': lin(ks[8], 64, 64), 'b32': jnp.zeros(64, jnp.float32)}
    _L0_gnn_all = _L0_gnn_setup()
    _L0_gnn_in = {k: v for k, v in _L0_gnn_all.items() if k in ('w11', 'b11', 'w12', 'b12', 'w21', 'b21', 'w22', 'b22', 'w31', 'b31', 'w32', 'b32')}
    del _L0_gnn_all

    def _L1_gnn_setup():
        import jax, jax.numpy as jnp
        import numpy as np
        N = 50000
        E = 25000
        D_IN = 64
        LD = 128
        HEADS = 8
        MAX_POS = 10000.0
        LRELU_SLOPE = 0.2
        BN_EPS = 1e-05

        def _pos_embed(t, channels):
            half = channels // 2
            freqs = jnp.arange(half, dtype=jnp.float32) / half
            freqs = (1.0 / MAX_POS) ** freqs
            x = t[:, None] * freqs[None, :]
            emb = jnp.concatenate([jnp.cos(x), jnp.sin(x)], axis=1)
            n = emb.shape[0]
            return jnp.flip(emb.reshape(n, 2, half), axis=1).reshape(n, channels)

        def _gat(x, src, dst, W, a_src, a_dst, bias, n_nodes):
            H, C = a_src.shape
            xw = (x @ W).reshape(n_nodes, H, C)
            al_s = jnp.einsum('nhc,hc->nh', xw, a_src)
            al_d = jnp.einsum('nhc,hc->nh', xw, a_dst)
            logits = jax.nn.leaky_relu(al_s[src] + al_d[dst], LRELU_SLOPE)
            m = jax.lax.stop_gradient(jax.ops.segment_max(logits, dst, num_segments=n_nodes))
            e = jnp.exp(logits - m[dst])
            denom = jax.ops.segment_sum(e, dst, num_segments=n_nodes)
            alpha = e / denom[dst]
            out = jax.ops.segment_sum(alpha[:, :, None] * xw[src], dst, num_segments=n_nodes)
            return out.reshape(n_nodes, H * C) + bias

        def _bn_train(x, g, b):
            mu = x.mean(axis=0)
            var = x.var(axis=0)
            return g * (x - mu) * jax.lax.rsqrt(var + BN_EPS) + b
        key = jax.random.key(seed)
        ks = jax.random.split(key, 32)
        p = lambda i, shape: jax.random.normal(ks[i], shape, dtype=jnp.float32) * 0.05
        inp = {'subgraph_x': jax.random.normal(ks[0], (N, D_IN), dtype=jnp.float32), 'edge_index': jax.random.randint(ks[1], (2, E), 0, N, dtype=jnp.int32), 'noise_labels': jax.random.uniform(ks[2], (N,), dtype=jnp.float32), 'init_w': p(3, (D_IN, LD)), 'init_b': jnp.zeros((LD,), jnp.float32), 'te_w1': p(4, (LD, LD)), 'te_b1': jnp.zeros((LD,), jnp.float32), 'te_w2': p(5, (LD, LD)), 'te_b2': jnp.zeros((LD,), jnp.float32)}
        dims = [(LD, 2 * LD), (2 * LD, 2 * LD), (2 * LD, LD)]
        for i, (din, dout) in enumerate(dims):
            c = dout // HEADS
            inp[f'gat_w{i}'] = p(6 + 4 * i, (din, dout))
            inp[f'att_src{i}'] = p(7 + 4 * i, (HEADS, c))
            inp[f'att_dst{i}'] = p(8 + 4 * i, (HEADS, c))
            inp[f'gat_b{i}'] = jnp.zeros((dout,), jnp.float32)
            inp[f'adj_w{i}'] = p(9 + 4 * i, (din, dout))
            inp[f'adj_b{i}'] = jnp.zeros((dout,), jnp.float32)
            inp[f'bn_g{i}'] = jnp.ones((dout,), jnp.float32)
            inp[f'bn_b{i}'] = jnp.zeros((dout,), jnp.float32)
        inp['out_w'] = p(20, (LD, D_IN))
        inp['out_b'] = jnp.zeros((D_IN,), jnp.float32)
        return inp
    _L1_gnn_all = _L1_gnn_setup()
    _L1_gnn_in = {k: v for k, v in _L1_gnn_all.items() if k in ('init_w', 'init_b', 'te_w1', 'te_b1', 'te_w2', 'te_b2', 'gat_w0', 'att_src0', 'att_dst0', 'gat_b0', 'adj_w0', 'adj_b0', 'bn_g0', 'bn_b0', 'gat_w1', 'att_src1', 'att_dst1', 'gat_b1', 'adj_w1', 'adj_b1', 'bn_g1', 'bn_b1', 'gat_w2', 'att_src2', 'att_dst2', 'gat_b2', 'adj_w2', 'adj_b2', 'bn_g2', 'bn_b2', 'out_w', 'out_b')}
    del _L1_gnn_all
    return {'x': x, 'src': src, 'dst': dst, 'edge_weight': edge_weight, 'node_vec': node_vec, 'L0_gnn_w11': _L0_gnn_in['w11'], 'L0_gnn_b11': _L0_gnn_in['b11'], 'L0_gnn_w12': _L0_gnn_in['w12'], 'L0_gnn_b12': _L0_gnn_in['b12'], 'L0_gnn_w21': _L0_gnn_in['w21'], 'L0_gnn_b21': _L0_gnn_in['b21'], 'L0_gnn_w22': _L0_gnn_in['w22'], 'L0_gnn_b22': _L0_gnn_in['b22'], 'L0_gnn_w31': _L0_gnn_in['w31'], 'L0_gnn_b31': _L0_gnn_in['b31'], 'L0_gnn_w32': _L0_gnn_in['w32'], 'L0_gnn_b32': _L0_gnn_in['b32'], 'L1_gnn_init_w': _L1_gnn_in['init_w'], 'L1_gnn_init_b': _L1_gnn_in['init_b'], 'L1_gnn_te_w1': _L1_gnn_in['te_w1'], 'L1_gnn_te_b1': _L1_gnn_in['te_b1'], 'L1_gnn_te_w2': _L1_gnn_in['te_w2'], 'L1_gnn_te_b2': _L1_gnn_in['te_b2'], 'L1_gnn_gat_w0': _L1_gnn_in['gat_w0'], 'L1_gnn_att_src0': _L1_gnn_in['att_src0'], 'L1_gnn_att_dst0': _L1_gnn_in['att_dst0'], 'L1_gnn_gat_b0': _L1_gnn_in['gat_b0'], 'L1_gnn_adj_w0': _L1_gnn_in['adj_w0'], 'L1_gnn_adj_b0': _L1_gnn_in['adj_b0'], 'L1_gnn_bn_g0': _L1_gnn_in['bn_g0'], 'L1_gnn_bn_b0': _L1_gnn_in['bn_b0'], 'L1_gnn_gat_w1': _L1_gnn_in['gat_w1'], 'L1_gnn_att_src1': _L1_gnn_in['att_src1'], 'L1_gnn_att_dst1': _L1_gnn_in['att_dst1'], 'L1_gnn_gat_b1': _L1_gnn_in['gat_b1'], 'L1_gnn_adj_w1': _L1_gnn_in['adj_w1'], 'L1_gnn_adj_b1': _L1_gnn_in['adj_b1'], 'L1_gnn_bn_g1': _L1_gnn_in['bn_g1'], 'L1_gnn_bn_b1': _L1_gnn_in['bn_b1'], 'L1_gnn_gat_w2': _L1_gnn_in['gat_w2'], 'L1_gnn_att_src2': _L1_gnn_in['att_src2'], 'L1_gnn_att_dst2': _L1_gnn_in['att_dst2'], 'L1_gnn_gat_b2': _L1_gnn_in['gat_b2'], 'L1_gnn_adj_w2': _L1_gnn_in['adj_w2'], 'L1_gnn_adj_b2': _L1_gnn_in['adj_b2'], 'L1_gnn_bn_g2': _L1_gnn_in['bn_g2'], 'L1_gnn_bn_b2': _L1_gnn_in['bn_b2'], 'L1_gnn_out_w': _L1_gnn_in['out_w'], 'L1_gnn_out_b': _L1_gnn_in['out_b']}

def reference(x, src, dst, edge_weight, node_vec, L0_gnn_w11, L0_gnn_b11, L0_gnn_w12, L0_gnn_b12, L0_gnn_w21, L0_gnn_b21, L0_gnn_w22, L0_gnn_b22, L0_gnn_w31, L0_gnn_b31, L0_gnn_w32, L0_gnn_b32, L1_gnn_init_w, L1_gnn_init_b, L1_gnn_te_w1, L1_gnn_te_b1, L1_gnn_te_w2, L1_gnn_te_b2, L1_gnn_gat_w0, L1_gnn_att_src0, L1_gnn_att_dst0, L1_gnn_gat_b0, L1_gnn_adj_w0, L1_gnn_adj_b0, L1_gnn_bn_g0, L1_gnn_bn_b0, L1_gnn_gat_w1, L1_gnn_att_src1, L1_gnn_att_dst1, L1_gnn_gat_b1, L1_gnn_adj_w1, L1_gnn_adj_b1, L1_gnn_bn_g1, L1_gnn_bn_b1, L1_gnn_gat_w2, L1_gnn_att_src2, L1_gnn_att_dst2, L1_gnn_gat_b2, L1_gnn_adj_w2, L1_gnn_adj_b2, L1_gnn_bn_g2, L1_gnn_bn_b2, L1_gnn_out_w, L1_gnn_out_b):
    import jax
    import jax.numpy as jnp

    def _L0_gnn_ref(x, edge_index, edge_weight, w11, b11, w12, b12, w21, b21, w22, b22, w31, b31, w32, b32):
        import jax, jax.numpy as jnp
        import numpy as np

        def gin_layer(x, src, dst, ew, w1, b1, w2, b2):
            msg = x[src] * ew[:, None]
            agg = jax.ops.segment_sum(msg, dst, num_segments=x.shape[0])
            h = agg + x
            h = jax.nn.relu(h @ w1 + b1)
            return h @ w2 + b2
        src, dst = (edge_index[0], edge_index[1])
        h = gin_layer(x, src, dst, edge_weight, w11, b11, w12, b12)
        h = jax.nn.relu(h)
        h = gin_layer(h, src, dst, edge_weight, w21, b21, w22, b22)
        h = jax.nn.relu(h)
        h = gin_layer(h, src, dst, edge_weight, w31, b31, w32, b32)
        return h

    def _L1_gnn_ref(subgraph_x, edge_index, noise_labels, init_w, init_b, te_w1, te_b1, te_w2, te_b2, gat_w0, att_src0, att_dst0, gat_b0, adj_w0, adj_b0, bn_g0, bn_b0, gat_w1, att_src1, att_dst1, gat_b1, adj_w1, adj_b1, bn_g1, bn_b1, gat_w2, att_src2, att_dst2, gat_b2, adj_w2, adj_b2, bn_g2, bn_b2, out_w, out_b):
        import jax, jax.numpy as jnp
        import numpy as np
        N = 50000
        E = 25000
        D_IN = 64
        LD = 128
        HEADS = 8
        MAX_POS = 10000.0
        LRELU_SLOPE = 0.2
        BN_EPS = 1e-05

        def _pos_embed(t, channels):
            half = channels // 2
            freqs = jnp.arange(half, dtype=jnp.float32) / half
            freqs = (1.0 / MAX_POS) ** freqs
            x = t[:, None] * freqs[None, :]
            emb = jnp.concatenate([jnp.cos(x), jnp.sin(x)], axis=1)
            n = emb.shape[0]
            return jnp.flip(emb.reshape(n, 2, half), axis=1).reshape(n, channels)

        def _gat(x, src, dst, W, a_src, a_dst, bias, n_nodes):
            H, C = a_src.shape
            xw = (x @ W).reshape(n_nodes, H, C)
            al_s = jnp.einsum('nhc,hc->nh', xw, a_src)
            al_d = jnp.einsum('nhc,hc->nh', xw, a_dst)
            logits = jax.nn.leaky_relu(al_s[src] + al_d[dst], LRELU_SLOPE)
            m = jax.lax.stop_gradient(jax.ops.segment_max(logits, dst, num_segments=n_nodes))
            e = jnp.exp(logits - m[dst])
            denom = jax.ops.segment_sum(e, dst, num_segments=n_nodes)
            alpha = e / denom[dst]
            out = jax.ops.segment_sum(alpha[:, :, None] * xw[src], dst, num_segments=n_nodes)
            return out.reshape(n_nodes, H * C) + bias

        def _bn_train(x, g, b):
            mu = x.mean(axis=0)
            var = x.var(axis=0)
            return g * (x - mu) * jax.lax.rsqrt(var + BN_EPS) + b
        n = subgraph_x.shape[0]
        self_idx = jnp.arange(n, dtype=edge_index.dtype)
        src = jnp.concatenate([edge_index[0], self_idx])
        dst = jnp.concatenate([edge_index[1], self_idx])
        emb = _pos_embed(noise_labels, LD)
        emb = jax.nn.silu(emb @ te_w1 + te_b1) @ te_w2 + te_b2
        x = subgraph_x @ init_w + init_b + emb
        layers = [(gat_w0, att_src0, att_dst0, gat_b0, adj_w0, adj_b0, bn_g0, bn_b0), (gat_w1, att_src1, att_dst1, gat_b1, adj_w1, adj_b1, bn_g1, bn_b1), (gat_w2, att_src2, att_dst2, gat_b2, adj_w2, adj_b2, bn_g2, bn_b2)]
        for gw, a_s, a_d, gb, aw, ab, g, b in layers:
            res = x @ aw + ab
            x = _gat(x, src, dst, gw, a_s, a_d, gb, n) + res
            x = jax.nn.silu(_bn_train(x, g, b))
        return x @ out_w + out_b
    edge_index = jnp.stack([src, dst])
    h = jnp.maximum(_layernorm(x, axis=-1), 0.0)
    x = x + _L0_gnn_ref(h, edge_index, edge_weight, L0_gnn_w11, L0_gnn_b11, L0_gnn_w12, L0_gnn_b12, L0_gnn_w21, L0_gnn_b21, L0_gnn_w22, L0_gnn_b22, L0_gnn_w31, L0_gnn_b31, L0_gnn_w32, L0_gnn_b32)
    h = jnp.maximum(_layernorm(x, axis=-1), 0.0)
    x = x + _L1_gnn_ref(h, edge_index, node_vec, L1_gnn_init_w, L1_gnn_init_b, L1_gnn_te_w1, L1_gnn_te_b1, L1_gnn_te_w2, L1_gnn_te_b2, L1_gnn_gat_w0, L1_gnn_att_src0, L1_gnn_att_dst0, L1_gnn_gat_b0, L1_gnn_adj_w0, L1_gnn_adj_b0, L1_gnn_bn_g0, L1_gnn_bn_b0, L1_gnn_gat_w1, L1_gnn_att_src1, L1_gnn_att_dst1, L1_gnn_gat_b1, L1_gnn_adj_w1, L1_gnn_adj_b1, L1_gnn_bn_g1, L1_gnn_bn_b1, L1_gnn_gat_w2, L1_gnn_att_src2, L1_gnn_att_dst2, L1_gnn_gat_b2, L1_gnn_adj_w2, L1_gnn_adj_b2, L1_gnn_bn_g2, L1_gnn_bn_b2, L1_gnn_out_w, L1_gnn_out_b)
    return x

_drawn_inputs = setup_inputs


def setup_inputs(seed=0):
    import zlib

    import numpy as np

    out = dict(_drawn_inputs(seed))
    spreads = {'L0_gnn_b11': (0.0, 0.8),
     'L0_gnn_b12': (0.0, 0.47),
     'L0_gnn_b21': (0.0, 2.0),
     'L0_gnn_b22': (0.0, 2.0),
     'L0_gnn_b31': (0.0, 2.0),
     'L0_gnn_b32': (0.0, 2.0),
     'L1_gnn_init_b': (0.0, 2.0),
     'L1_gnn_te_b1': (0.0, 2.0),
     'L1_gnn_te_b2': (0.0, 2.0),
     'L1_gnn_gat_b0': (0.0, 2.0),
     'L1_gnn_adj_b0': (0.0, 2.0),
     'L1_gnn_bn_g0': (1.0, 0.6),
     'L1_gnn_bn_b0': (0.0, 2.0),
     'L1_gnn_gat_b1': (0.0, 2.0),
     'L1_gnn_adj_b1': (0.0, 2.0),
     'L1_gnn_bn_g1': (1.0, 0.6),
     'L1_gnn_bn_b1': (0.0, 2.0),
     'L1_gnn_gat_b2': (0.0, 2.0),
     'L1_gnn_adj_b2': (0.0, 2.0),
     'L1_gnn_bn_g2': (1.0, 0.6),
     'L1_gnn_bn_b2': (0.0, 2.0),
     'L1_gnn_out_b': (0.0, 2.0)}
    factors = {'node_vec': 56.174,
     'L1_gnn_init_w': 64.0,
     'L1_gnn_te_w1': 59.454,
     'L1_gnn_te_w2': 61.021,
     'L1_gnn_gat_w0': 64.0,
     'L1_gnn_att_src0': 64.0,
     'L1_gnn_att_dst0': 64.0,
     'L1_gnn_adj_w0': 59.893,
     'L1_gnn_gat_w1': 64.0,
     'L1_gnn_att_src1': 64.0,
     'L1_gnn_att_dst1': 64.0,
     'L1_gnn_adj_w1': 64.0,
     'L1_gnn_gat_w2': 64.0,
     'L1_gnn_att_src2': 64.0,
     'L1_gnn_att_dst2': 64.0,
     'L1_gnn_adj_w2': 64.0,
     'L1_gnn_out_w': 49.056}
    for name, (base, spread) in spreads.items():
        noise = np.random.default_rng([zlib.crc32(name.encode()), seed]).standard_normal(out[name].shape)
        drawn = base * np.exp(spread * noise) if base else spread * noise
        out[name] = jnp.asarray(drawn.astype(out[name].dtype))
    for name, factor in factors.items():
        out[name] = (out[name] * factor).astype(out[name].dtype)
    return out
```

```python
from contextlib import ExitStack

import numpy as np

import concourse.bass as bass
from concourse import mybir

F32, I32 = mybir.dt.float32, mybir.dt.int32
ALU, ACT, AX = mybir.AluOpType, mybir.ActivationFunctionType, mybir.AxisListType
R_MAX = bass.bass_isa.ReduceOp.max

P = 128
N = 3125
E = 103125
D = 64
LD = 128
HEADS = 8
TILES = -(-N // P)
T = TILES + 1
NP = T * P
LAST = N - (TILES - 1) * P
PAD = NP
BLOCK = 64
EP = -(-E // (P * 2)) * P * 2
EC = EP // P
BLOCKS = EP // BLOCK
SLOTS = 8
PER_BLOCK = BLOCK // SLOTS
RING = 4
TILE_AT = 2 * SLOTS
CHUNK = TILE_AT + 1
CHUNKS = E // SLOTS + T + PER_BLOCK * T + RING
LN_EPS = BN_EPS = 1e-5
LRELU_SLOPE = 0.2
NEG = -1.0e30
HALF = LD // 2
PAIR = 2
GIN_MID = (64, 128, 64)
GAT_IN = (LD, 2 * LD, 2 * LD)
GAT_OUT = (2 * LD, 2 * LD, LD)
TWO_PI = 2.0 * np.pi
PI_HI = 6.28125
PI_MID = float(np.float32(np.round((TWO_PI - PI_HI) * 2.0**20) / 2.0**20))
PI_LO = float(np.float32(TWO_PI - PI_HI - PI_MID))
ROUND = 12582912.0


class Chain:

    def __init__(self, eng, sem):
        self.eng, self.sem, self.n = eng, sem, 0

    def __call__(self, ins):
        self.n += 1
        ins.then_inc(self.sem, 1)
        self.eng.wait_ge(self.sem, self.n)

    def reset(self):
        if self.n:
            self.eng.sem_inc(self.sem, -self.n)
        self.n = 0


def take(eng, sem, n=1):
    eng.wait_ge(sem, n)
    eng.sem_inc(sem, -n)


def program(nc, a, out, debug):
    x_d, src_d, dst_d, w_d, nv_d, freq_d = (a[k] for k in ("x", "src", "dst", "edge_weight", "node_vec", "freqs"))

    def dram(name, shape, dt=F32):
        return nc.dram_tensor(name, shape, dt, kind="ExternalOutput" if name in debug else "Internal").ap()

    sw_d = dram("sw_d", (EP + 2 * BLOCK, 2))
    rp_d = dram("rp_d", (NP + 1,))
    key_d = dram("key_d", (NP,))
    rec_d = dram("rec_d", (NP, 4))
    ell_d = dram("ell_d", (CHUNKS, P, CHUNK), I32)
    gin_tab = [dram(f"gin_tab{l}", (NP + 1, D)) for l in range(3)]
    gat_row = [GAT_OUT[l] + HEADS for l in range(3)]
    gat_tab = [dram(f"gat_tab{l}", (NP + 1, gat_row[l])) for l in range(3)]

    with ExitStack() as ctx:
        def sb(name, shape, dt=F32):
            return ctx.enter_context(nc.sbuf_tensor(name, shape, dt))

        def sem(name):
            return ctx.enter_context(nc.semaphore(name))

        ident = sb("ident", [P, P])
        ones = sb("ones", [P, P])
        ones_last = sb("ones_last", [P, P])
        pad_row = sb("pad_row", [1, 2 * LD + HEADS])
        freqs = sb("freqs", [P, HALF])
        w1 = [sb(f"w1_{l}", [D, GIN_MID[l]]) for l in range(3)]
        w2 = [sb(f"w2_{l}", [GIN_MID[l], D]) for l in range(3)]
        b1 = [sb(f"b1_{l}", [GIN_MID[l], 1]) for l in range(3)]
        b2 = [sb(f"b2_{l}", [P, D]) for l in range(3)]
        te_w1, te_w2 = sb("te_w1", [LD, LD]), sb("te_w2", [LD, LD])
        te_b1 = sb("te_b1", [LD, 1])
        init_w = sb("init_w", [D, LD])
        init_b, te_b2 = sb("init_b", [P, LD]), sb("te_b2", [P, LD])
        kin = [GAT_IN[l] // P for l in range(3)]
        gat_w = [sb(f"gat_w{l}", [P, kin[l], GAT_OUT[l] + 2 * HEADS]) for l in range(3)]
        adj_w = [sb(f"adj_w{l}", [P, kin[l], GAT_OUT[l]]) for l in range(3)]
        att = [sb(f"att{l}", [P, 2, GAT_OUT[l]]) for l in range(3)]
        gat_b = [sb(f"gat_b{l}", [P, GAT_OUT[l]]) for l in range(3)]
        adj_b = [sb(f"adj_b{l}", [P, GAT_OUT[l]]) for l in range(3)]
        bn_g = [sb(f"bn_g{l}", [P, GAT_OUT[l]]) for l in range(3)]
        bn_b = [sb(f"bn_b{l}", [P, GAT_OUT[l]]) for l in range(3)]
        out_w = sb("out_w", [LD, D])
        out_b = sb("out_b", [P, D])

        x_a = sb("x_a", [P, T, 2 * LD])
        res = sb("res", [P, T, 2 * LD])
        acc = sb("acc", [P, T, 2 * LD])
        x_res = sb("x_res", [P, T, D])
        h_in = sb("h_in", [P, T, D])
        sd = sb("sd", [P, T, 2 * HEADS])
        m_all = sb("m_all", [P, T, HEADS])
        den = sb("den", [P, T, HEADS])
        flat = lambda t: t[:, :, :].rearrange("p t f -> p (t f)")
        xf, rf, af = flat(x_a), flat(res), flat(acc)

        key_all, junk = xf[:, 0:NP], xf[:, NP:2 * NP]
        src_i, w_f = rf[:, 0:EC].bitcast(I32), rf[:, EC:2 * EC]
        sw = rf[:, 2 * EC:4 * EC].rearrange("p (e c) -> p e c", c=2)
        dst_i = rf[:, 4 * EC:4 * EC + T * BLOCK].bitcast(I32).rearrange("p (t k) -> p t k", k=BLOCK)
        dst_f = af[:, 0:T * BLOCK].rearrange("p (t k) -> p t k", k=BLOCK)
        below = af[:, T * BLOCK:2 * T * BLOCK].rearrange("p (t k) -> p t k", k=BLOCK)
        tops_i = af[0:1, 2 * T * BLOCK:2 * T * BLOCK + BLOCKS].bitcast(I32)
        tops_f = xf[0:1, 0:BLOCKS]
        zeros = sb("zeros", [1, 4 * BLOCK])
        id_i, id_f = sb("id_i", [P, T], I32), sb("id_f", [P, T])
        slot_i, slot_f = sb("slot_i", [P, BLOCK], I32), sb("slot_f", [P, BLOCK])
        cnt, blk, rp, rp1 = (sb(n, [P, T]) for n in ("cnt", "blk", "rp", "rp1"))
        blk_i, rank_i = sb("blk_i", [P, T], I32), sb("rank_i", [P, T], I32)
        key, rank = sb("key", [P, T]), sb("rank", [P, T])
        e_end = sb("e_end", [1, 1])
        rec = sb("rec", [P, T, 4])
        vec = sb("vec", [P, T])
        recs = sb("recs", [P, T, 4])
        node_i, node_in = sb("node_i", [P, T], I32), sb("node_in", [P, T], I32)
        tmp_i, first_i = sb("tmp_i", [P, T], I32), sb("first_i", [P, T], I32)
        first_blk = sb("first_blk", [P, T])
        bit, nbit = sb("bit", [P, 6, T]), sb("nbit", [P, 6, T])
        deg_max = sb("deg_max", [P, T])
        chunks_i, blocks_i = sb("chunks_i", [P, T], I32), sb("blocks_i", [P, T], I32)
        chunks_f, start_f, zero_t = (sb(n, [P, T]) for n in ("chunks_f", "start_f", "zero_t"))
        first_blk_at, block_start_i = sb("first_blk_at", [P, T]), sb("block_start_i", [P, T], I32)
        start_i, meta = sb("start_i", [P, T], I32), sb("meta", [P, 1], I32)
        at_blk, left, tile_no = (sb(n, [P, 1]) for n in ("at_blk", "left", "tile_no"))
        pick_i = sb("pick_i", [P, 2], I32)
        pair = sb("pair", [P, 2, 2 * BLOCK])
        shift_a, shift_b = sb("shift_a", [P, 4 * BLOCK]), sb("shift_b", [P, 4 * BLOCK])
        valid, srcv = sb("valid", [P, BLOCK]), sb("srcv", [P, BLOCK])
        ell_new = sb("ell_new", [P, PER_BLOCK, CHUNK], I32)

        ell = [sb(f"ell{u}", [P, CHUNK], I32) for u in range(RING)]
        rows = [sb(f"rows{u}", [P, SLOTS * (2 * LD + HEADS)]) for u in range(RING)]
        part = sb("part", [P, 2 * LD])
        score, lrel, ex_in, ex = (sb(n, [P, SLOTS + 1, HEADS]) for n in ("score", "lrel", "ex_in", "ex"))
        top, new_max, den_part = (sb(n, [P, HEADS]) for n in ("top", "new_max", "den_part"))

        x_st = [sb(f"x_st{u}", [P, 2 * LD]) for u in range(PAIR)]
        xT = [sb(f"xT{u}", [P, 2, P]) for u in range(PAIR)]
        mid = [sb(f"mid{u}", [P, P]) for u in range(PAIR)]
        mid_e = [sb(f"mid_e{u}", [P, P]) for u in range(PAIR)]
        row_st = [sb(f"row_st{u}", [P, 2 * LD + HEADS]) for u in range(PAIR)]
        row_tmp = [sb(f"row_tmp{u}", [P, D]) for u in range(PAIR)]
        row_node = [sb(f"row_node{u}", [P, 1], I32) for u in range(PAIR)]
        mean, var, rstd, rtmp = (sb(n, [P, 2 * LD]) for n in ("mean", "var", "rstd", "rtmp"))
        ln_a, ln_b, ln_c, ln_d = (sb(n, [P, T]) for n in ("ln_a", "ln_b", "ln_c", "ln_d"))

        banks = ctx.enter_context(nc.psum_tensor("banks", [P, 8, 512], F32))
        tops_ps = banks[:, 0:4, :].rearrange("p b n -> p (b n)")
        T_ps = [banks[:, u, :] for u in range(PAIR)]
        A_ps = [banks[:, 2 + u, :] for u in range(PAIR)]
        B_ps = [banks[:, 4 + u, :] for u in range(PAIR)]
        sum_ps = banks[:, 6, :]

        tops_landed, edges_landed, vec_landed, weights_landed = (
            sem(n) for n in ("tops_landed", "edges_landed", "vec_landed", "weights_landed"))
        iota_done, ident_done, ones_done, pads_ready = (sem(n) for n in ("iota_done", "ident_done", "ones_done", "pads_ready"))
        tops_ready, tops_spread, sw_ready, sw_stored = (sem(n) for n in ("tops_ready", "tops_spread", "sw_ready", "sw_stored"))
        blk_ready, dst_gathered = sem("blk_ready"), sem("dst_gathered")
        rp_ready, rp_stored, rp1_landed = sem("rp_ready"), sem("rp_stored"), sem("rp1_landed")
        key_ready, key_stored, key_landed = sem("key_ready"), sem("key_stored"), sem("key_landed")
        rec_ready, recs_landed = sem("rec_ready"), sem("recs_landed")
        deg_ready, deg_maxed, node_ready, x_gathered = (sem(n) for n in ("deg_ready", "deg_maxed", "node_ready", "x_gathered"))
        meta_sp, meta_pool = sem("meta_sp"), sem("meta_pool")
        pick_ready, pair_gathered = sem("pick_ready"), sem("pair_gathered")
        ell_ready, ell_stored, ell_free_new = sem("ell_ready"), sem("ell_stored"), sem("ell_free_new")
        ell_all = sem("ell_all")
        pads_stored = sem("pads_stored")
        dve_chain, act_chain, pool_chain = sem("dve_chain"), sem("act_chain"), sem("pool_chain")
        ticks = {e: sem(f"ticks_{e}") for e in ("dve", "pool", "act")}
        ell_landed = [sem(f"ell_landed{u}") for u in range(RING)]
        ell_free = [sem(f"ell_free{u}") for u in range(RING)]
        rows_free = [sem(f"rows_free{u}") for u in range(RING)]
        rows_landed = [[sem(f"rows_landed{l}_{u}") for u in range(RING)] for l in range(6)]
        table_ready, table_stored = sem("table_ready"), sem("table_stored")
        row_ready = [sem(f"row_ready{u}") for u in range(PAIR)]
        row_stored = [sem(f"row_stored{u}") for u in range(PAIR)]
        x_staged = [sem(f"x_staged{u}") for u in range(PAIR)]
        xT_made = [sem(f"xT_made{u}") for u in range(PAIR)]
        xT_copied = [sem(f"xT_copied{u}") for u in range(PAIR)]
        mid_made = [sem(f"mid_made{u}") for u in range(PAIR)]
        mid_copied = [sem(f"mid_copied{u}") for u in range(PAIR)]
        A_made = [sem(f"A_made{u}") for u in range(PAIR)]
        A_free = [sem(f"A_free{u}") for u in range(PAIR)]
        B_made = [sem(f"B_made{u}") for u in range(PAIR)]
        B_free = [sem(f"B_free{u}") for u in range(PAIR)]
        dense_in, agg_ready = sem("dense_in"), sem("agg_ready")
        sqrt_in, sqrt_done, exp_in, exp_done = (sem(n) for n in ("sqrt_in", "sqrt_done", "exp_in", "exp_done"))
        sin_in, sin_done = sem("sin_in"), sem("sin_done")
        sum_in, sum_made = sem("sum_in"), sem("sum_made")
        z_made = [sem(f"z_made{u}") for u in range(PAIR)]
        z_done = [sem(f"z_done{u}") for u in range(PAIR)]
        gat_w_ready = sem("gat_w_ready")
        fin_ready, out_stored = sem("fin_ready"), sem("out_stored")
        PREP_STORES = T // PAIR * 16
        LOOP_STORES = T // PAIR * 16

        block = ctx.enter_context(nc.Block())

        def tile_at(t, it, u):
            return t[:, bass.ds(it * PAIR + u, 1), :]

        def plane(ap):
            return ap.rearrange("p a f -> p (a f)")

        @block.sync
        def _(sp):
            sp.dma_start(tops_i, dst_d.rearrange("(a b k) -> a b k", a=1, k=BLOCK)[:, :, 0], allow_slow_non_contiguous=True)\
                .then_inc(tops_landed, 16)
            sp.dma_start(src_i, src_d.rearrange("(p e) -> p e", p=P)).then_inc(edges_landed, 16)
            sp.dma_start(w_f, w_d.rearrange("(p e) -> p e", p=P)).then_inc(edges_landed, 16)
            sp.dma_start(vec[:, :], nv_d.rearrange("(p t) -> p t", p=P)).then_inc(vec_landed, 16)
            take(sp, pads_ready)
            for l in range(3):
                sp.dma_start(gin_tab[l][PAD:PAD + 1, :], pad_row[0:1, 0:D]).then_inc(pads_stored, 16)
                wide = GAT_OUT[l]
                sp.dma_start(gat_tab[l][PAD:PAD + 1, :], pad_row[0:1, 2 * LD - wide:]).then_inc(pads_stored, 16)
            take(sp, sw_ready)
            sp.dma_start(sw_d[0:EP, :].rearrange("(p e) c -> p e c", p=P), sw).then_inc(sw_stored, 16)
            sp.dma_start(sw_d[EP:EP + 2 * BLOCK, :].rearrange("(a e) c -> a (e c)", a=1), zeros[:, :]).then_inc(sw_stored, 16)
            take(sp, rp_ready)
            sp.dma_start(rp_d[0:NP].rearrange("(p t) -> p t", p=P), rp[:, :]).then_inc(rp_stored, 16)
            sp.dma_start(rp_d[NP:NP + 1].rearrange("(a b) -> a b", a=1), e_end[:, :]).then_inc(rp_stored, 16)
            sp.wait_ge(rp_stored, 32)
            sp.dma_start(rp1[:, :], rp_d[1:NP + 1].rearrange("(p t) -> p t", p=P)).then_inc(rp1_landed, 16)
            take(sp, key_ready)
            sp.dma_start(key_d.rearrange("(p t) -> p t", p=P), key[:, :]).then_inc(key_stored, 16)
            sp.wait_ge(key_stored, 16)
            sp.dma_start(key_all, key_d.partition_broadcast(P)).then_inc(key_landed, 16)
            for u in range(PAIR):
                sp.wait_ge(row_stored[u], PREP_STORES)
            sp.dma_start(recs[:, :, :], rec_d.rearrange("(t p) c -> p t c", p=P)).then_inc(recs_landed, 16)
            take(sp, meta_sp)
            with sp.Fori(0, T) as t:
                blocks = sp.value_load(blocks_i[0:1, bass.ds(t, 1)], min_val=1, max_val=BLOCKS + 1)
                start = sp.value_load(start_i[0:1, bass.ds(t, 1)], min_val=0, max_val=CHUNKS - PER_BLOCK)
                with sp.Fori(0, blocks) as s:
                    take(sp, ell_ready)
                    row = nc.s_assert_within(start + s * PER_BLOCK, 0, CHUNKS - PER_BLOCK,
                                             skip_runtime_bounds_check_because="CHUNKS has room for every tile's last block")
                    sp.dma_start(ell_d[bass.ds(row, PER_BLOCK), :, :].rearrange("k p c -> p k c"),
                                 ell_new[:, :, :]).then_inc(ell_stored, 16)
                    take(sp, ell_stored, 16)
                    sp.sem_inc(ell_free_new, 1)
            rounds = sp.value_load(meta[0:1, 0:1], min_val=1, max_val=CHUNKS // RING)
            for layer in range(6):
                with sp.Fori(0, rounds) as it:
                    for u in range(RING):
                        take(sp, ell_free[u])
                        sp.dma_start(ell[u][:, :], ell_d[bass.ds(it * RING + u, 1), :, :].rearrange("k p c -> (k p) c"))\
                          .then_inc(ell_landed[u], 16)

        @block.gpsimd
        def _(pool):
            g = nc.gpsimd
            chain = Chain(pool, pool_chain)

            def gather(dst, table, idx):
                return g.indirect_dma_start(out=dst, out_offset=None, in_=table,
                                            in_offset=bass.IndirectOffsetOnAxis(ap=idx, axis=0))

            def scatter(table, idx, data):
                return g.indirect_dma_start(out=table, out_offset=bass.IndirectOffsetOnAxis(ap=idx, axis=0),
                                            in_=data, in_offset=None)

            g.iota(id_i[:, :], pattern=[[1, T]], base=0, channel_multiplier=T).then_inc(iota_done, 1)
            g.iota(slot_i[:, :], pattern=[[1, BLOCK]], base=0, channel_multiplier=0).then_inc(iota_done, 1)
            chain(g.memset(ident[:, :], 0.0))
            g.affine_select(out=ident[:, :], in_=ident[:, :], compare_op=ALU.not_equal, fill=1.0, base=0,
                            pattern=[[-1, P]], channel_multiplier=1).then_inc(ident_done, 1)
            take(pool, blk_ready)
            for t in range(T):
                gather(dst_i[:, t, :], dst_d.rearrange("(b k) -> b k", k=BLOCK), blk_i[:, t:t + 1]).then_inc(dst_gathered, 16)
            take(pool, rec_ready)
            for t in range(T):
                scatter(rec_d, rank_i[:, t:t + 1], rec[:, t, :]).then_inc(row_stored[t % PAIR], 16)
            take(pool, deg_ready)
            g.partition_all_reduce(deg_max[:, :], recs[:, :, 1], P, R_MAX).then_inc(deg_maxed, 1)
            take(pool, node_ready)
            for t in range(T):
                gather(x_res[:, t, :], x_d, node_in[:, t:t + 1]).then_inc(x_gathered, 16)
            take(pool, meta_pool)
            pool.wait_ge(sw_stored, 32)
            sw_blocks = sw_d.rearrange("(b k) c -> b (k c)", k=BLOCK)
            with pool.Fori(0, T) as t:
                blocks = pool.value_load(blocks_i[0:1, bass.ds(t, 1)], min_val=1, max_val=BLOCKS + 1)
                with pool.Fori(0, blocks) as s:
                    take(pool, pick_ready)
                    for j in range(2):
                        gather(pair[:, j, :], sw_blocks, pick_i[:, j:j + 1]).then_inc(pair_gathered, 16)
            rounds = pool.value_load(meta[0:1, 0:1], min_val=1, max_val=CHUNKS // RING)
            pool.wait_ge(pads_stored, 6 * 16)

            def chunk_gathers(layer, table, width):
                with pool.Fori(0, rounds) as it:
                    for u in range(RING):
                        take(pool, ell_landed[u], 16)
                        take(pool, rows_free[u])
                        for r in range(SLOTS):
                            gather(rows[u][:, r * width:(r + 1) * width], table, ell[u][:, r:r + 1])\
                                .then_inc(rows_landed[layer][u], 16)

            def store_rows(table, width):
                with pool.Fori(0, T // PAIR) as it:
                    for u in range(PAIR):
                        take(pool, row_ready[u])
                        scatter(table, row_node[u][:, 0:1], row_st[u][:, 0:width]).then_inc(row_stored[u], 16)

            def rows_all_stored(loops):
                for u in range(PAIR):
                    pool.wait_ge(row_stored[u], PREP_STORES + LOOP_STORES * loops)

            take(pool, table_ready)
            for t in range(T):
                scatter(gin_tab[0], node_i[:, t:t + 1], h_in[:, t, :]).then_inc(table_stored, 16)
            pool.wait_ge(table_stored, 16 * T)
            for l in range(3):
                chunk_gathers(l, gin_tab[l], D)
                if l < 2:
                    store_rows(gin_tab[l + 1], D)
                    rows_all_stored(l + 1)
            for l in range(3):
                store_rows(gat_tab[l], gat_row[l])
                rows_all_stored(3 + l)
                chunk_gathers(3 + l, gat_tab[l], gat_row[l])
            take(pool, fin_ready)
            for t in range(TILES):
                n = P if t < TILES - 1 else LAST
                scatter(out, node_i[0:n, t:t + 1], x_res[0:n, t, :]).then_inc(out_stored, 16)
            pool.wait_ge(out_stored, 16 * TILES)

        @block.scalar
        def _(act):
            s = nc.scalar
            loads = []

            def load(dst, src):
                act.dma_start(dst, src).then_inc(weights_landed, 16)

            column = lambda v: v.rearrange("(d a) -> d a", a=1)
            load(freqs[:, :], freq_d.partition_broadcast(P))
            for l, (i1, i2) in enumerate((("11", "12"), ("21", "22"), ("31", "32"))):
                load(w1[l][:, :], a[f"L0_gnn_w{i1}"])
                load(w2[l][:, :], a[f"L0_gnn_w{i2}"])
                load(b1[l][:, :], column(a[f"L0_gnn_b{i1}"]))
                load(b2[l][:, :], a[f"L0_gnn_b{i2}"].partition_broadcast(P))
            load(te_w1[:, :], a["L1_gnn_te_w1"])
            load(te_w2[:, :], a["L1_gnn_te_w2"])
            load(te_b1[:, :], column(a["L1_gnn_te_b1"]))
            load(te_b2[:, :], a["L1_gnn_te_b2"].partition_broadcast(P))
            load(init_w[:, :], a["L1_gnn_init_w"])
            load(init_b[:, :], a["L1_gnn_init_b"].partition_broadcast(P))
            for l in range(3):
                load(gat_w[l][:, :, 0:GAT_OUT[l]], a[f"L1_gnn_gat_w{l}"].rearrange("(k p) n -> p k n", p=P))
                load(adj_w[l][:, :, :], a[f"L1_gnn_adj_w{l}"].rearrange("(k p) n -> p k n", p=P))
                load(att[l][:, 0, :], a[f"L1_gnn_att_src{l}"].rearrange("h c -> (h c)").partition_broadcast(P))
                load(att[l][:, 1, :], a[f"L1_gnn_att_dst{l}"].rearrange("h c -> (h c)").partition_broadcast(P))
                load(gat_b[l][:, :], a[f"L1_gnn_gat_b{l}"].partition_broadcast(P))
                load(adj_b[l][:, :], a[f"L1_gnn_adj_b{l}"].partition_broadcast(P))
                load(bn_g[l][:, :], a[f"L1_gnn_bn_g{l}"].partition_broadcast(P))
                load(bn_b[l][:, :], a[f"L1_gnn_bn_b{l}"].partition_broadcast(P))
            load(out_w[:, :], a["L1_gnn_out_w"])
            load(out_b[:, :], a["L1_gnn_out_b"].partition_broadcast(P))
            act.wait_ge(weights_landed, 16 * WEIGHTS)

            def sqrt(n, wide):
                take(act, sqrt_in)
                s.activation(rtmp[:, 0:wide] if n else ln_c[:, :], var[:, 0:wide] if n else ln_b[:, :],
                             ACT.Sqrt).then_inc(sqrt_done, 1)

            def stage(src, it, width):
                for u in range(PAIR):
                    s.activation(x_st[u][:, 0:width], plane(src[:, bass.ds(it * PAIR + u, 1), 0:width]), ACT.Copy)\
                        .then_inc(x_staged[u], 1)

            def copy_T(parts, k):
                for u in range(PAIR):
                    take(act, xT_made[u])
                    s.activation(xT[u][0:parts, 0:k, :].rearrange("p k n -> p (k n)"), T_ps[u][0:parts, 0:k * P], ACT.Copy)\
                        .then_inc(xT_copied[u], 1)

            sqrt(0, 0)
            for l in range(3):
                take(act, agg_ready)
                m = GIN_MID[l]
                with act.Fori(0, T // PAIR) as it:
                    stage(acc, it, D)
                    copy_T(D, 1)
                    for u in range(PAIR):
                        take(act, mid_made[u])
                        s.activation(mid[u][0:m, :], A_ps[u][0:m, 0:P], ACT.Relu, bias=b1[l][:, 0:1]).then_inc(mid_copied[u], 1)
            sqrt(0, 0)
            take(act, sin_in)
            s.activation(acc[:, :, 0:LD], x_a[:, :, 0:LD], ACT.Sin).then_inc(sin_done, 1)
            take(act, dense_in)
            with act.Fori(0, T // PAIR) as it:
                for u in range(PAIR):
                    s.activation(x_st[u][:, 0:LD], plane(acc[:, bass.ds(it * PAIR + u, 1), 0:LD]), ACT.Copy)
                    s.activation(x_st[u][:, LD:LD + D], plane(tile_at(h_in, it, u)), ACT.Copy).then_inc(x_staged[u], 1)
                for u in range(PAIR):
                    take(act, xT_made[u])
                    s.activation(xT[u][:, 0, :], T_ps[u][:, 0:P], ACT.Copy)
                    s.activation(xT[u][0:D, 1, :], T_ps[u][0:D, P:2 * P], ACT.Copy).then_inc(xT_copied[u], 1)
                for u in range(PAIR):
                    take(act, z_made[u])
                    s.activation(mid_e[u][:, :], mid[u][:, :], ACT.Exp, scale=-1.0).then_inc(z_done[u], 1)
            for l in range(3):
                wide, k = GAT_OUT[l], kin[l]
                stored = PREP_STORES + LOOP_STORES * (2 + l)
                take(act, dense_in)
                with act.Fori(0, T // PAIR) as it:
                    stage(x_a, it, GAT_IN[l])
                    copy_T(P, k)
                    for u in range(PAIR):
                        act.wait_ge(row_stored[u], stored + it * 16)
                        act.sem_inc(ticks["act"], 1)
                        s.activation(row_node[u][:, :], recs[:, bass.ds(it * PAIR + u, 1), 2], ACT.Copy)
                        take(act, A_made[u])
                        s.activation(row_st[u][:, 0:wide + HEADS], A_ps[u][:, 0:wide + HEADS], ACT.Copy).then_inc(row_ready[u], 1)
                        s.activation(plane(tile_at(sd, it, u)), A_ps[u][:, wide:wide + 2 * HEADS], ACT.Copy)
                        s.activation(plane(acc[:, bass.ds(it * PAIR + u, 1), 0:wide]), A_ps[u][:, 0:wide], ACT.Copy)\
                            .then_inc(A_free[u], 1)
                rounds = act.value_load(meta[0:1, 0:1], min_val=1, max_val=CHUNKS // RING)
                with act.Fori(0, rounds) as it:
                    for u in range(RING):
                        take(act, exp_in)
                        s.activation(ex[:, :, :], ex_in[:, :, :], ACT.Exp).then_inc(exp_done, 1)
                sqrt(1, wide)
                take(act, exp_in)
                s.activation(res[:, :, 0:wide], x_a[:, :, 0:wide], ACT.Exp, scale=-1.0).then_inc(exp_done, 1)
            take(act, dense_in)
            with act.Fori(0, T // PAIR) as it:
                stage(x_a, it, LD)
                copy_T(P, 1)

        @block.tensor
        def _(pe):
            t = nc.tensor
            take(pe, ones_done)
            take(pe, tops_ready)
            for n in range(0, BLOCKS, 512):
                m = min(512, BLOCKS - n)
                last = t.matmul(tops_ps[:, n:n + m], ones[0:1, :], tops_f[:, n:n + m], start=True, stop=True)
            last.then_inc(tops_spread, 1)
            take(pe, ident_done)
            pe.wait_ge(weights_landed, 16 * WEIGHTS)

            def transposes(k, width):
                for u in range(PAIR):
                    take(pe, x_staged[u])
                    for j in range(k):
                        last = t.transpose(T_ps[u][0:width, j * P:(j + 1) * P], x_st[u][:, j * P:j * P + width], ident[:, :])
                    last.then_inc(xT_made[u], 1)

            for l in range(3):
                m = GIN_MID[l]
                with pe.Fori(0, T // PAIR) as it:
                    transposes(1, D)
                    for u in range(PAIR):
                        take(pe, xT_copied[u])
                        t.matmul(A_ps[u][0:m, 0:P], w1[l][:, :], xT[u][0:D, 0, :], start=True, stop=True).then_inc(mid_made[u], 1)
                    for u in range(PAIR):
                        take(pe, mid_copied[u])
                        take(pe, B_free[u])
                        t.matmul(B_ps[u][:, 0:D], mid[u][0:m, :], w2[l][:, :], start=True, stop=True).then_inc(B_made[u], 1)
            with pe.Fori(0, T // PAIR) as it:
                for u in range(PAIR):
                    take(pe, x_staged[u])
                    t.transpose(T_ps[u][:, 0:P], x_st[u][:, 0:P], ident[:, :])
                    t.transpose(T_ps[u][0:D, P:2 * P], x_st[u][:, P:P + D], ident[:, :]).then_inc(xT_made[u], 1)
                for u in range(PAIR):
                    take(pe, xT_copied[u])
                    t.matmul(A_ps[u][:, 0:P], te_w1[:, :], xT[u][:, 0, :], start=True, stop=True).then_inc(A_made[u], 1)
                for u in range(PAIR):
                    take(pe, mid_copied[u])
                    take(pe, B_free[u])
                    t.matmul(B_ps[u][:, 0:LD], mid[u][:, :], te_w2[:, :], start=True, stop=False)
                    t.matmul(B_ps[u][:, 0:LD], xT[u][0:D, 1, :], init_w[:, :], start=False, stop=True).then_inc(B_made[u], 1)

            def column_sums(src, wide):
                take(pe, sum_in)
                for n in range(TILES):
                    last = t.matmul(sum_ps[:, 0:wide], (ones if n < TILES - 1 else ones_last)[:, :], src[:, n, 0:wide],
                                    start=(n == 0), stop=(n == TILES - 1))
                last.then_inc(sum_made, 1)

            take(pe, gat_w_ready)
            for l in range(3):
                wide, k = GAT_OUT[l], kin[l]
                with pe.Fori(0, T // PAIR) as it:
                    transposes(k, P)
                    for u in range(PAIR):
                        take(pe, xT_copied[u])
                        take(pe, A_free[u])
                        for j in range(k):
                            last = t.matmul(A_ps[u][:, 0:wide + 2 * HEADS], xT[u][:, j, :], gat_w[l][:, j, :],
                                            start=(j == 0), stop=(j == k - 1))
                        last.then_inc(A_made[u], 1)
                        take(pe, B_free[u])
                        for j in range(k):
                            last = t.matmul(B_ps[u][:, 0:wide], xT[u][:, j, :], adj_w[l][:, j, :],
                                            start=(j == 0), stop=(j == k - 1))
                        last.then_inc(B_made[u], 1)
                column_sums(acc, wide)
                column_sums(res, wide)
            with pe.Fori(0, T // PAIR) as it:
                transposes(1, P)
                for u in range(PAIR):
                    take(pe, xT_copied[u])
                    take(pe, B_free[u])
                    t.matmul(B_ps[u][:, 0:D], xT[u][:, 0, :], out_w[:, :], start=True, stop=True).then_inc(B_made[u], 1)

        @block.vector
        def _(dve):
            v = nc.vector
            link = Chain(dve, dve_chain)

            def signal(sm, n=1):
                dve.sem_inc(sm, n)

            for u in range(RING):
                signal(ell_free[u])
                signal(rows_free[u])
            for u in range(PAIR):
                signal(A_free[u])
                signal(B_free[u])
            signal(ell_free_new)
            v.memset(pad_row[:, 0:2 * LD], 0.0)
            link(v.memset(pad_row[:, 2 * LD:], NEG))
            signal(pads_ready)
            v.memset(ones[:, :], 1.0)
            v.memset(ones_last[:, :], 0.0)
            link(v.memset(zeros[:, :], 0.0))
            link(v.memset(ones_last[0:LAST, :], 1.0))
            signal(ones_done)
            v.memset(e_end[:, :], float(E))
            link(v.memset(zero_t[:, :], 0.0))
            take(dve, iota_done, 2)
            v.tensor_copy(id_f[:, :], id_i[:, :])
            link(v.tensor_copy(slot_f[:, :], slot_i[:, :]))
            dve.wait_ge(tops_landed, 16)
            link(v.tensor_copy(tops_f, tops_i))
            signal(tops_ready)
            dve.wait_ge(edges_landed, 32)
            v.tensor_copy(sw[:, :, 0], src_i)
            link(v.tensor_copy(sw[:, :, 1], w_f))
            signal(sw_ready)
            take(dve, tops_spread)
            for t in range(T):
                link(v.tensor_scalar(junk[:, 0:BLOCKS], tops_ps[:, 0:BLOCKS], id_f[:, t:t + 1], None, ALU.is_lt, ALU.add,
                                     accum_out=cnt[:, t:t + 1]))
            link(v.tensor_scalar(blk[:, :], cnt[:, :], -1.0, 0.0, ALU.add, ALU.max))
            link(v.tensor_copy(blk_i[:, :], blk[:, :]))
            signal(blk_ready)
            dve.wait_ge(dst_gathered, 16 * T)
            link(v.tensor_copy(dst_f, dst_i))
            link(v.tensor_tensor(below, dst_f, id_f[:, :].unsqueeze(2).to_broadcast([P, T, BLOCK]), ALU.is_lt))
            link(v.tensor_reduce(cnt[:, :], below, AX.X, ALU.add))
            link(v.scalar_tensor_tensor(rp[:, :], blk[:, :], float(BLOCK), cnt[:, :], ALU.mult, ALU.add))
            signal(rp_ready)
            dve.wait_ge(rp1_landed, 16)
            v.tensor_copy(rec[:, :, 0], rp[:, :])
            v.tensor_copy(rec[:, :, 2], id_f[:, :])
            link(v.tensor_tensor(rec[:, :, 1], rp1[:, :], rp[:, :], ALU.subtract))
            link(v.tensor_scalar(key[:, :], rec[:, :, 1], 4095.0, 4096.0, ALU.min, ALU.mult))
            link(v.tensor_tensor(key[:, :], key[:, :], id_f[:, :], ALU.subtract))
            link(v.tensor_scalar(key[:, :], key[:, :], 4095.0, None, ALU.add))
            signal(key_ready)
            dve.wait_ge(key_landed, 16)
            for t in range(T):
                link(v.tensor_scalar(junk, key_all, key[:, t:t + 1], None, ALU.is_gt, ALU.add, accum_out=rank[:, t:t + 1]))
            dve.wait_ge(vec_landed, 16)
            v.tensor_copy(rec[:, :, 3], vec[:, :])
            link(v.tensor_copy(rank_i[:, :], rank[:, :]))
            signal(rec_ready)
            dve.wait_ge(recs_landed, 16)
            signal(deg_ready)
            v.tensor_copy(node_i[:, :], recs[:, :, 2])
            link(v.tensor_scalar(node_in[:, :], recs[:, :, 2], float(N - 1), None, ALU.min))
            signal(node_ready)
            link(v.tensor_copy(first_i[:, :], recs[:, :, 0]))
            link(v.tensor_scalar(tmp_i[:, :], first_i[:, :], 6, None, ALU.arith_shift_right))
            link(v.tensor_copy(first_blk[:, :], tmp_i[:, :]))
            for b in range(6):
                link(v.tensor_scalar(tmp_i[:, :], first_i[:, :], b, 1, ALU.arith_shift_right, ALU.bitwise_and))
                link(v.tensor_copy(bit[:, b, :], tmp_i[:, :]))
            link(v.tensor_scalar(nbit[:, :, :], bit[:, :, :], -1.0, 1.0, ALU.mult, ALU.add))
            take(dve, deg_maxed)

            def ceil_div(dst, shift):
                link(v.tensor_scalar(chunks_f[:, :], deg_max[:, :], float((1 << shift) - 1), None, ALU.add))
                link(v.tensor_copy(tmp_i[:, :], chunks_f[:, :]))
                link(v.tensor_scalar(dst, tmp_i[:, :], shift, None, ALU.arith_shift_right))

            def starts(dst, counts):
                link(v.tensor_copy(chunks_f[:, :], counts))
                link(v.tensor_tensor_scan(start_f[:, :], zero_t[:, :], chunks_f[:, :], 0.0, ALU.add, ALU.add))
                v.tensor_scalar(cnt[:, 0:1], start_f[:, T - 1:T], float(RING - 1), None, ALU.add)
                link(v.tensor_tensor(first_blk_at[:, :], start_f[:, :], chunks_f[:, :], ALU.subtract))
                link(v.tensor_copy(dst, first_blk_at[:, :]))

            ceil_div(blocks_i[:, :], 6)
            link(v.tensor_copy(chunks_f[:, :], blocks_i[:, :]))
            link(v.tensor_scalar(blocks_i[:, :], chunks_f[:, :], 1.0, None, ALU.max))
            starts(block_start_i[:, :], blocks_i[:, :])
            ceil_div(chunks_i[:, :], 3)
            starts(start_i[:, :], chunks_i[:, :])
            link(v.tensor_copy(tmp_i[:, 0:1], cnt[:, 0:1]))
            link(v.tensor_scalar(meta[:, :], tmp_i[:, 0:1], 2, None, ALU.arith_shift_right))
            signal(meta_sp)
            signal(meta_pool)
            link(v.memset(tile_no[:, :], 0.0))
            link.reset()
            with dve.Fori(0, T) as t:
                v.tensor_copy(at_blk[:, :], first_blk[:, bass.ds(t, 1)])
                link(v.tensor_copy(left[:, :], recs[:, bass.ds(t, 1), 1]))
                blocks = dve.value_load(blocks_i[0:1, bass.ds(t, 1)], min_val=1, max_val=BLOCKS + 1)
                block_start = dve.value_load(block_start_i[0:1, bass.ds(t, 1)], min_val=0, max_val=BLOCKS + T)
                link.reset()
                with dve.Fori(0, blocks) as s:
                    v.tensor_scalar(pick_i[:, 0:1], at_blk[:, :], float(BLOCKS), None, ALU.min)
                    link(v.tensor_scalar(pick_i[:, 1:2], at_blk[:, :], 1.0, float(BLOCKS), ALU.add, ALU.min))
                    signal(pick_ready)
                    v.tensor_scalar(valid[:, :], slot_f[:, :], left[:, 0:1], None, ALU.is_lt)
                    link(v.tensor_scalar(at_blk[:, :], at_blk[:, :], 1.0, None, ALU.add))
                    dve.wait_ge(pair_gathered, (block_start + s) * 32 + 32)
                    signal(ticks["dve"])
                    cur, keep = pair[:, :, :].rearrange("p j n -> p (j n)"), 2 * BLOCK
                    for b in range(5, -1, -1):
                        keep = BLOCK + (1 << b) - 1
                        by = 2 << b
                        link(v.tensor_scalar(shift_a[:, 0:2 * keep], cur[:, 0:2 * keep], nbit[:, b, bass.ds(t, 1)], None, ALU.mult))
                        link(v.scalar_tensor_tensor(shift_b[:, 0:2 * keep], cur[:, by:by + 2 * keep], bit[:, b, bass.ds(t, 1)],
                                                    shift_a[:, 0:2 * keep], ALU.mult, ALU.add))
                        cur = shift_b
                    sw_now = shift_b[:, 0:2 * BLOCK].rearrange("p (e c) -> p e c", c=2)
                    take(dve, ell_free_new)
                    link(v.scalar_tensor_tensor(srcv[:, :], sw_now[:, :, 0], float(-PAD), valid[:, :], ALU.add, ALU.mult))
                    v.tensor_scalar(ell_new[:, :, 0:SLOTS], srcv[:, :].rearrange("p (k r) -> p k r", r=SLOTS), float(PAD), None, ALU.add)
                    v.tensor_tensor(ell_new[:, :, SLOTS:2 * SLOTS].bitcast(F32), sw_now[:, :, 1].rearrange("p (k r) -> p k r", r=SLOTS),
                                    valid[:, :].rearrange("p (k r) -> p k r", r=SLOTS), ALU.mult)
                    v.tensor_copy(ell_new[:, :, TILE_AT], tile_no[:, :].to_broadcast([P, PER_BLOCK]))
                    link(v.tensor_scalar(left[:, :], left[:, :], float(-BLOCK), None, ALU.add))
                    signal(ell_ready)
                    link.reset()
                link(v.tensor_scalar(tile_no[:, :], tile_no[:, :], 1.0, None, ALU.add))
                link.reset()


            def layernorm(dst):
                def spread(s):
                    return s[:, :].unsqueeze(2).to_broadcast([P, T, D])
                link(v.tensor_reduce(ln_a[:, :], x_res[:, :, :], AX.X, ALU.add))
                link(v.tensor_scalar(ln_a[:, :], ln_a[:, :], 1.0 / D, None, ALU.mult))
                link(v.tensor_tensor(acc[:, :, 0:D], x_res[:, :, :], spread(ln_a), ALU.subtract))
                link(v.tensor_tensor(acc[:, :, D:2 * D], acc[:, :, 0:D], acc[:, :, 0:D], ALU.mult))
                link(v.tensor_reduce(ln_a[:, :], acc[:, :, D:2 * D], AX.X, ALU.add))
                link(v.tensor_scalar(ln_b[:, :], ln_a[:, :], 1.0 / D, LN_EPS, ALU.mult, ALU.add))
                signal(sqrt_in)
                take(dve, sqrt_done)
                link(v.reciprocal(ln_c[:, :], ln_c[:, :]))
                newton(ln_c[:, :], ln_b[:, :], ln_d[:, :])
                link(v.tensor_tensor(acc[:, :, 0:D], acc[:, :, 0:D], spread(ln_c), ALU.mult))
                link(v.tensor_scalar(dst[:, :, :], acc[:, :, 0:D], 0.0, None, ALU.max))

            def newton(y, sq, tmp):
                link(v.tensor_tensor(tmp, y, y, ALU.mult))
                link(v.tensor_tensor(tmp, tmp, sq, ALU.mult))
                link(v.tensor_scalar(tmp, tmp, -0.5, 1.5, ALU.mult, ALU.add))
                link(v.tensor_tensor(y, y, tmp, ALU.mult))

            dve.wait_ge(x_gathered, 16 * T)
            layernorm(h_in)
            signal(table_ready)
            link(v.tensor_copy(acc[:, :, 0:D], h_in[:, :, :]))
            dve.wait_ge(weights_landed, 16 * WEIGHTS)
            rounds = dve.value_load(meta[0:1, 0:1], min_val=1, max_val=CHUNKS // RING)
            link.reset()

            def chunk_tile(u):
                return dve.value_load(ell[u][0:1, TILE_AT:TILE_AT + 1], min_val=0, max_val=T - 1)

            for l in range(3):
                with dve.Fori(0, rounds) as it:
                    for u in range(RING):
                        dve.wait_ge(rows_landed[l][u], (it + 1) * (16 * SLOTS))
                        signal(ticks["dve"])
                        t = chunk_tile(u)
                        msg = rows[u][:, 0:SLOTS * D].rearrange("p (r f) -> p r f", f=D)
                        weight = ell[u][:, SLOTS:2 * SLOTS].bitcast(F32).unsqueeze(2).to_broadcast([P, SLOTS, D])
                        link(v.tensor_tensor(msg, msg, weight, ALU.mult))
                        signal(ell_free[u])
                        link(v.tensor_reduce(part[:, 0:D], msg.rearrange("p r f -> p f r"), AX.X, ALU.add))
                        signal(rows_free[u])
                        at = plane(acc[:, bass.ds(t, 1), 0:D])
                        link(v.tensor_tensor(at, at, part[:, 0:D], ALU.add))
                    link.reset()
                signal(agg_ready)
                with dve.Fori(0, T // PAIR) as it:
                    for u in range(PAIR):
                        if l < 2:
                            dve.wait_ge(row_stored[u], it * 16 + (PREP_STORES + LOOP_STORES * l))
                            signal(ticks["dve"])
                        take(dve, B_made[u])
                        v.tensor_copy(row_node[u][:, :], recs[:, bass.ds(it * PAIR + u, 1), 2])
                        ins = v.tensor_tensor(row_tmp[u][:, :], B_ps[u][:, 0:D], b2[l][:, :], ALU.add)
                        link(ins)
                        signal(B_free[u])
                        if l < 2:
                            link(v.tensor_scalar(row_st[u][:, 0:D], row_tmp[u][:, :], 0.0, None, ALU.max))
                            signal(row_ready[u])
                            link(v.tensor_scalar(plane(acc[:, bass.ds(it * PAIR + u, 1), 0:D]), row_tmp[u][:, :], 0.0, None, ALU.max))
                        else:
                            at = plane(tile_at(x_res, it, u))
                            link(v.tensor_tensor(at, at, row_tmp[u][:, :], ALU.add))
                    link.reset()

            layernorm(h_in)
            arg, turn = res[:, :, 0:HALF], res[:, :, HALF:LD]
            link(v.tensor_tensor(arg, recs[:, :, 3].unsqueeze(2).to_broadcast([P, T, HALF]),
                                 freqs[:, :].unsqueeze(1).to_broadcast([P, T, HALF]), ALU.mult))
            for quarter in range(2):
                link(v.tensor_scalar(turn, arg, 1.0 / TWO_PI, 0.25 * quarter, ALU.mult, ALU.add))
                link(v.tensor_scalar(turn, turn, ROUND, None, ALU.add))
                link(v.tensor_scalar(turn, turn, -ROUND, None, ALU.add))
                to = x_a[:, :, quarter * HALF:(quarter + 1) * HALF]
                link(v.scalar_tensor_tensor(to, turn, -PI_HI, arg, ALU.mult, ALU.add))
                link(v.scalar_tensor_tensor(to, turn, -PI_MID, to, ALU.mult, ALU.add))
                link(v.scalar_tensor_tensor(to, turn, -PI_LO, to, ALU.mult, ALU.add))
                link(v.tensor_scalar(to, to, np.pi / 2 * quarter, 3.1415925, ALU.add, ALU.min))
                link(v.tensor_scalar(to, to, -3.1415925, None, ALU.max))
            signal(sin_in)
            link(v.tensor_tensor(init_b[:, :], init_b[:, :], te_b2[:, :], ALU.add))
            for l in range(3):
                wide, c = GAT_OUT[l], GAT_OUT[l] // HEADS
                for j in range(kin[l]):
                    for e in range(2):
                        link(v.tensor_tensor(res[:, 0, 0:wide], gat_w[l][:, j, 0:wide], att[l][:, e, :], ALU.mult))
                        link(v.tensor_reduce(gat_w[l][:, j, wide + e * HEADS:wide + (e + 1) * HEADS],
                                             res[:, 0, 0:wide].rearrange("p (h c) -> p h c", c=c), AX.X, ALU.add))
                link(v.tensor_tensor(gat_b[l][:, :], gat_b[l][:, :], adj_b[l][:, :], ALU.add))
            signal(gat_w_ready)
            take(dve, sin_done)
            signal(dense_in)
            link.reset()
            with dve.Fori(0, T // PAIR) as it:
                for u in range(PAIR):
                    take(dve, A_made[u])
                    link(v.tensor_scalar(mid[u][:, :], A_ps[u][:, 0:P], te_b1[:, 0:1], None, ALU.add))
                    signal(z_made[u])
                for u in range(PAIR):
                    take(dve, z_done[u])
                    link(v.tensor_scalar(mid_e[u][:, :], mid_e[u][:, :], 1.0, None, ALU.add))
                    link(v.reciprocal(mid_e[u][:, :], mid_e[u][:, :]))
                    link(v.tensor_tensor(mid[u][:, :], mid[u][:, :], mid_e[u][:, :], ALU.mult))
                    signal(mid_copied[u])
                for u in range(PAIR):
                    take(dve, B_made[u])
                    link(v.tensor_tensor(plane(x_a[:, bass.ds(it * PAIR + u, 1), 0:LD]), B_ps[u][:, 0:LD], init_b[:, :], ALU.add))
                    signal(B_free[u])
                link.reset()
            for l in range(3):
                wide, c, width = GAT_OUT[l], GAT_OUT[l] // HEADS, gat_row[l]
                signal(dense_in)
                with dve.Fori(0, T // PAIR) as it:
                    for u in range(PAIR):
                        take(dve, B_made[u])
                        link(v.tensor_tensor(plane(res[:, bass.ds(it * PAIR + u, 1), 0:wide]), B_ps[u][:, 0:wide], gat_b[l][:, :], ALU.add))
                        signal(B_free[u])
                    link.reset()
                take(dve, A_free[0])
                take(dve, A_free[1])
                signal(A_free[0])
                signal(A_free[1])
                link(v.tensor_tensor(m_all[:, :, :], sd[:, :, 0:HEADS], sd[:, :, HEADS:], ALU.add))
                link(v.scalar_tensor_tensor(m_all[:, :, :], m_all[:, :, :], LRELU_SLOPE, m_all[:, :, :], ALU.mult, ALU.max))
                link(v.memset(den[:, :, :], 1.0))
                link.reset()
                with dve.Fori(0, rounds) as it:
                    for u in range(RING):
                        dve.wait_ge(rows_landed[3 + l][u], (it + 1) * (16 * SLOTS))
                        signal(ticks["dve"])
                        t = chunk_tile(u)
                        signal(ell_free[u])
                        row = rows[u][:, 0:SLOTS * width].rearrange("p (r f) -> p r f", f=width)
                        now = bass.ds(t, 1)
                        sub = [P, SLOTS, HEADS]
                        link(v.tensor_tensor(score[:, 0:SLOTS, :], row[:, :, wide:], sd[:, now, HEADS:].to_broadcast(sub), ALU.add))
                        link(v.scalar_tensor_tensor(lrel[:, 0:SLOTS, :], score[:, 0:SLOTS, :], LRELU_SLOPE, score[:, 0:SLOTS, :], ALU.mult, ALU.max))
                        link(v.tensor_reduce(top[:, :], lrel[:, 0:SLOTS, :].rearrange("p r h -> p h r"), AX.X, ALU.max))
                        at = plane(m_all[:, now, :])
                        link(v.tensor_tensor(new_max[:, :], at, top[:, :], ALU.max))
                        v.tensor_tensor(ex_in[:, 0:SLOTS, :], lrel[:, 0:SLOTS, :], new_max[:, :].unsqueeze(1).to_broadcast(sub), ALU.subtract)
                        link(v.tensor_tensor(ex_in[:, SLOTS, :], at, new_max[:, :], ALU.subtract))
                        signal(exp_in)
                        link(v.tensor_copy(at, new_max[:, :]))
                        take(dve, exp_done)
                        link(v.tensor_reduce(den_part[:, :], ex[:, 0:SLOTS, :].rearrange("p r h -> p h r"), AX.X, ALU.add))
                        at = plane(den[:, now, :])
                        link(v.tensor_tensor(at, at, ex[:, SLOTS, :], ALU.mult))
                        link(v.tensor_tensor(at, at, den_part[:, :], ALU.add))
                        msg = row[:, :, 0:wide].rearrange("p r (h c) -> p r h c", c=c)
                        link(v.tensor_tensor(msg, msg, ex[:, 0:SLOTS, :].unsqueeze(3).to_broadcast([P, SLOTS, HEADS, c]), ALU.mult))
                        link(v.tensor_reduce(part[:, 0:wide], row[:, :, 0:wide].rearrange("p r f -> p f r"), AX.X, ALU.add))
                        signal(rows_free[u])
                        at = plane(acc[:, now, 0:wide])
                        at_h = at.rearrange("p (h c) -> p h c", c=c)
                        link(v.tensor_tensor(at_h, at_h, ex[:, SLOTS, :].unsqueeze(2).to_broadcast([P, HEADS, c]), ALU.mult))
                        link(v.tensor_tensor(at, at, part[:, 0:wide], ALU.add))
                    link.reset()
                full = [P, T, wide]
                y, z, x = acc[:, :, 0:wide], res[:, :, 0:wide], x_a[:, :, 0:wide]
                link(v.reciprocal(den[:, :, :], den[:, :, :]))
                for t in range(T):
                    v.tensor_tensor(acc[:, t, 0:wide].rearrange("p (h c) -> p h c", c=c), acc[:, t, 0:wide].rearrange("p (h c) -> p h c", c=c),
                                    den[:, t, :].unsqueeze(2).to_broadcast([P, HEADS, c]), ALU.mult)
                link(v.memset(part[:, 0:1], 0.0))
                link(v.tensor_tensor(y, y, z, ALU.add))
                signal(sum_in)
                take(dve, sum_made)
                link(v.tensor_scalar(mean[:, 0:wide], sum_ps[:, 0:wide], 1.0 / N, None, ALU.mult))
                link(v.tensor_tensor(y, y, mean[:, 0:wide].unsqueeze(1).to_broadcast(full), ALU.subtract))
                link(v.tensor_tensor(z, y, y, ALU.mult))
                signal(sum_in)
                take(dve, sum_made)
                link(v.tensor_scalar(var[:, 0:wide], sum_ps[:, 0:wide], 1.0 / N, BN_EPS, ALU.mult, ALU.add))
                signal(sqrt_in)
                take(dve, sqrt_done)
                link(v.reciprocal(rstd[:, 0:wide], rtmp[:, 0:wide]))
                newton(rstd[:, 0:wide], var[:, 0:wide], rtmp[:, 0:wide])
                link(v.tensor_tensor(rstd[:, 0:wide], rstd[:, 0:wide], bn_g[l][:, :], ALU.mult))
                link(v.tensor_tensor(y, y, rstd[:, 0:wide].unsqueeze(1).to_broadcast(full), ALU.mult))
                link(v.tensor_tensor(x, y, bn_b[l][:, :].unsqueeze(1).to_broadcast(full), ALU.add))
                signal(exp_in)
                take(dve, exp_done)
                link(v.tensor_scalar(z, z, 1.0, None, ALU.add))
                link(v.reciprocal(z, z))
                link(v.tensor_tensor(x, x, z, ALU.mult))
                link.reset()
            signal(dense_in)
            with dve.Fori(0, T // PAIR) as it:
                for u in range(PAIR):
                    take(dve, B_made[u])
                    link(v.tensor_tensor(row_tmp[u][:, :], B_ps[u][:, 0:D], out_b[:, :], ALU.add))
                    signal(B_free[u])
                    at = plane(tile_at(x_res, it, u))
                    link(v.tensor_tensor(at, at, row_tmp[u][:, :], ALU.add))
                link.reset()
            signal(fin_ready)


WEIGHTS = 1 + 3 * 4 + 6 + 3 * 8 + 2


def kernel(**inputs):
    import concourse.bacc as bacc
    from concourse.bass_utils import run_bass_kernel_spmd

    nc = bacc.Bacc("TRN2", target_bir_lowering=False, num_devices=1)
    arrays = {k: np.asarray(x) for k, x in inputs.items()}

    def padded(x, n, fill):
        y = np.full((n,), fill, x.dtype)
        y[:x.shape[0]] = x
        return y

    arrays["src"] = padded(arrays["src"], EP, 0)
    arrays["dst"] = padded(arrays["dst"], EP, 2 * NP)
    arrays["edge_weight"] = padded(arrays["edge_weight"], EP, 0)
    arrays["node_vec"] = padded(arrays["node_vec"], NP, 0)
    steps = np.arange(HALF, dtype=np.float32) / np.float32(HALF)
    arrays["freqs"] = np.float32(1.0 / 10000.0) ** steps
    aps = {k: nc.dram_tensor(f"in_{k}", x.shape, mybir.dt.from_np(x.dtype), kind="ExternalInput").ap() for k, x in arrays.items()}
    out = nc.dram_tensor("out", (N, D), F32, kind="ExternalOutput").ap()
    program(nc, aps, out, ())
    result = run_bass_kernel_spmd(nc, [{f"in_{k}": x for k, x in arrays.items()}], core_ids=[0])
    return result.results[0]["out"]
```

```python
from contextlib import ExitStack

import numpy as np

import concourse.bass as bass
from concourse import mybir

F32, I32, BF16 = mybir.dt.float32, mybir.dt.int32, mybir.dt.bfloat16
ALU, ACT, AX = mybir.AluOpType, mybir.ActivationFunctionType, mybir.AxisListType
R_MAX = bass.bass_isa.ReduceOp.max

P = 128
N = 3125
E = 103125
D = 64
LD = 128
HEADS = 8
TILES = -(-N // P)
T = TILES + 1
NP = T * P
LAST = N - (TILES - 1) * P
PAD = NP
BLOCK = 64
EP = -(-E // (P * 2)) * P * 2
EC = EP // P
BLOCKS = EP // BLOCK
SLOTS = 8
PER_BLOCK = BLOCK // SLOTS
RING = 4
TILE_AT = SLOTS
CHUNK = TILE_AT + 1
CHUNKS = E // SLOTS + T + PER_BLOCK * T + RING
LN_EPS = BN_EPS = 1e-5
LRELU_SLOPE = 0.2
NEG = -1.0e30
HALF = LD // 2
PAIR = 2
STRIP = 512
STRIPS = [(n, min(STRIP, NP - n)) for n in range(0, NP, STRIP)]
DOUBLES = T // 2
GIN_MID = (64, 128, 64)
GAT_IN = (LD, 2 * LD, 2 * LD)
GAT_OUT = (2 * LD, 2 * LD, LD)
TWO_PI = 2.0 * np.pi
PI_HI = 6.28125
PI_MID = float(np.float32(np.round((TWO_PI - PI_HI) * 2.0**20) / 2.0**20))
PI_LO = float(np.float32(TWO_PI - PI_HI - PI_MID))
ROUND = 12582912.0


class Chain:

    def __init__(self, eng, sem):
        self.eng, self.sem, self.n = eng, sem, 0

    def __call__(self, ins):
        self.n += 1
        ins.then_inc(self.sem, 1)
        self.eng.wait_ge(self.sem, self.n)

    def reset(self):
        if self.n:
            self.eng.sem_inc(self.sem, -self.n)
        self.n = 0


def take(eng, sem, n=1):
    eng.wait_ge(sem, n)
    eng.sem_inc(sem, -n)


def program(nc, a, out, debug):
    x_d, src_d, dst_d, w_d, nv_d, freq_d = (a[k] for k in ("x", "src", "dst", "edge_weight", "node_vec", "freqs"))

    def dram(name, shape, dt=F32):
        return nc.dram_tensor(name, shape, dt, kind="ExternalOutput" if name in debug else "Internal").ap()

    sw_d = dram("sw_d", (EP + 2 * BLOCK, 2))
    rp_d = dram("rp_d", (NP + 1,))
    key_d = dram("key_d", (NP,))
    rec_d = dram("rec_d", (NP, 4))
    ell_d = dram("ell_d", (CHUNKS, P, CHUNK), I32)
    adj_t = dram("adj_t", (NP + BLOCK, NP))
    x1_d = dram("x1_d", (NP, D))
    gat_row = [GAT_OUT[l] + HEADS for l in range(3)]
    gat_tab = [dram(f"gat_tab{l}", (NP + 1, gat_row[l])) for l in range(3)]

    with ExitStack() as ctx:
        def sb(name, shape, dt=F32):
            return ctx.enter_context(nc.sbuf_tensor(name, shape, dt))

        def sem(name):
            return ctx.enter_context(nc.semaphore(name))

        ident = sb("ident", [P, P])
        ones = sb("ones", [P, P])
        ones_last = sb("ones_last", [P, P])
        pad_row = sb("pad_row", [1, 2 * LD + HEADS])
        freqs = sb("freqs", [P, 1])
        quarter, half_pi = sb("quarter", [P, 1]), sb("half_pi", [P, 1])
        w1 = [sb(f"w1_{l}", [D, GIN_MID[l]]) for l in range(3)]
        w2 = [sb(f"w2_{l}", [GIN_MID[l], D]) for l in range(3)]
        b1 = [sb(f"b1_{l}", [GIN_MID[l], 1]) for l in range(3)]
        b2 = [sb(f"b2_{l}", [P, D]) for l in range(3)]
        te_w1, te_w2 = sb("te_w1", [LD, LD]), sb("te_w2", [LD, LD])
        te_b1 = sb("te_b1", [LD, 1])
        init_w = sb("init_w", [D, LD])
        init_b, te_b2 = sb("init_b", [LD, 1]), sb("te_b2", [LD, 1])
        kin = [GAT_IN[l] // P for l in range(3)]
        gat_w = [sb(f"gat_w{l}", [P, kin[l], GAT_OUT[l] + 2 * HEADS]) for l in range(3)]
        adj_w = [sb(f"adj_w{l}", [P, kin[l], GAT_OUT[l]]) for l in range(3)]
        att = [sb(f"att{l}", [P, 2, GAT_OUT[l]]) for l in range(3)]
        gat_b = [sb(f"gat_b{l}", [P, GAT_OUT[l]]) for l in range(3)]
        adj_b = [sb(f"adj_b{l}", [P, GAT_OUT[l]]) for l in range(3)]
        bn_g = [sb(f"bn_g{l}", [P, GAT_OUT[l]]) for l in range(3)]
        bn_b = [sb(f"bn_b{l}", [P, GAT_OUT[l]]) for l in range(3)]
        out_w = sb("out_w", [LD, D])
        out_b = sb("out_b", [P, D])

        x_a = sb("x_a", [P, T, 2 * LD])
        res = sb("res", [P, T, 2 * LD])
        acc = sb("acc", [P, T, 2 * LD])
        x_res = sb("x_res", [P, T, D])
        h_in = sb("h_in", [P, T, D])
        sd = sb("sd", [P, T, 2 * HEADS])
        m_all = sb("m_all", [P, T, HEADS])
        den = sb("den", [P, T, HEADS])
        flat = lambda t: t[:, :, :].rearrange("p t f -> p (t f)")
        xf, rf, af = flat(x_a), flat(res), flat(acc)

        key_all, junk = xf[:, 0:NP], xf[:, NP:2 * NP]
        src_i, w_f = rf[:, 0:EC].bitcast(I32), rf[:, EC:2 * EC]
        sw = rf[:, 2 * EC:4 * EC].rearrange("p (e c) -> p e c", c=2)
        dst_i = rf[:, 4 * EC:4 * EC + T * BLOCK].bitcast(I32).rearrange("p (t k) -> p t k", k=BLOCK)
        dst_f = af[:, 0:T * BLOCK].rearrange("p (t k) -> p t k", k=BLOCK)
        below = af[:, T * BLOCK:2 * T * BLOCK].rearrange("p (t k) -> p t k", k=BLOCK)
        tops_i = af[0:1, 2 * T * BLOCK:2 * T * BLOCK + BLOCKS].bitcast(I32)
        tops_f = xf[0:1, 0:BLOCKS]
        zeros = sb("zeros", [1, 4 * BLOCK])
        id_i, id_f = sb("id_i", [P, T], I32), sb("id_f", [P, T])
        slot_i, slot_f = sb("slot_i", [P, BLOCK], I32), sb("slot_f", [P, BLOCK])
        cnt, blk, rp, rp1 = (sb(n, [P, T]) for n in ("cnt", "blk", "rp", "rp1"))
        blk_i, rank_i = sb("blk_i", [P, T], I32), sb("rank_i", [P, T], I32)
        key, rank = sb("key", [P, T]), sb("rank", [P, T])
        e_end = sb("e_end", [1, 1])
        rec = sb("rec", [P, T, 4])
        vec = sb("vec", [P, T])
        recs = sb("recs", [P, T, 4])
        node_i = sb("node_i", [P, T], I32)
        tmp_i, first_i = sb("tmp_i", [P, T], I32), sb("first_i", [P, T], I32)
        first_blk = sb("first_blk", [P, T + 1])
        blocks_f = sb("blocks_f", [P, T])
        bit, nbit = sb("bit", [P, 6, T]), sb("nbit", [P, 6, T])
        deg_max = sb("deg_max", [P, T])
        chunks_i, blocks_i = sb("chunks_i", [P, T], I32), sb("blocks_i", [P, T], I32)
        chunks_f, start_f, zero_t = (sb(n, [P, T]) for n in ("chunks_f", "start_f", "zero_t"))
        first_blk_at, block_start_i = sb("first_blk_at", [P, T]), sb("block_start_i", [P, T], I32)
        start_i, meta = sb("start_i", [P, T], I32), sb("meta", [P, 2], I32)
        at_blk, next_blk, left, blocks_left, is_last, tile_no = (
            sb(n, [P, 1]) for n in ("at_blk", "next_blk", "left", "blocks_left", "is_last", "tile_no"))
        pick_i = sb("pick_i", [P, 2], I32)
        pair = sb("pair", [P, 2, 2 * BLOCK])
        shift_a, shift_b = sb("shift_a", [P, 4 * BLOCK]), sb("shift_b", [P, 4 * BLOCK])
        valid, srcv, dump = sb("valid", [P, BLOCK]), sb("srcv", [P, BLOCK]), sb("dump", [P, BLOCK])
        adj_row, adj_w_new, w_valid, repeats = (sb(n, [P, BLOCK]) for n in ("adj_row", "adj_w_new", "w_valid", "repeats"))
        post_i, post_w = sb("post_i", [P, BLOCK], I32), sb("post_w", [P, BLOCK])
        before = sb("before", [P, BLOCK, BLOCK], BF16)
        same = sb("same", [P, BLOCK, BLOCK], BF16)
        ell_new = sb("ell_new", [P, PER_BLOCK, CHUNK], I32)

        ell = [sb(f"ell{u}", [P, CHUNK], I32) for u in range(RING)]
        rows_all = sb("rows_all", [P, RING * SLOTS * (2 * LD + HEADS)])
        rows = [rows_all[:, u * SLOTS * (2 * LD + HEADS):(u + 1) * SLOTS * (2 * LD + HEADS)] for u in range(RING)]
        zero_rows = rows_all[:, 0:NP]
        same_w = rows_all[:, 0:BLOCK * BLOCK].rearrange("p (r q) -> p r q", q=BLOCK)
        adj_buf = [t.rearrange("p (b n) -> p b n", n=NP) for t in (xf, rf)]
        h_st = [sb(f"h_st{u}", [P, 2, D]) for u in range(2)]
        agg_sb = rows_all[0:D, 0:NP]
        gin_mid = [rows_all[:, NP + u * STRIP:NP + (u + 1) * STRIP] for u in range(2)]
        arg, turn = af[:, 0:NP], af[:, NP:2 * NP]
        emb_in, emb_mid, emb = turn, arg, turn
        x0_t = xf[:, 0:NP]
        h_t = rf[0:D, 0:NP]
        part = sb("part", [P, 2 * LD])
        score, lrel, ex_in, ex = (sb(n, [P, SLOTS + 1, HEADS]) for n in ("score", "lrel", "ex_in", "ex"))
        top, new_max, den_part = (sb(n, [P, HEADS]) for n in ("top", "new_max", "den_part"))

        x_st = [sb(f"x_st{u}", [P, 2 * LD]) for u in range(PAIR)]
        xT = [sb(f"xT{u}", [P, 2, P]) for u in range(PAIR)]
        mid = [sb(f"mid{u}", [P, P]) for u in range(PAIR)]
        row_st = [sb(f"row_st{u}", [P, 2 * LD + HEADS]) for u in range(PAIR)]
        row_tmp = [sb(f"row_tmp{u}", [P, D]) for u in range(PAIR)]
        row_node = [sb(f"row_node{u}", [P, 1], I32) for u in range(PAIR)]
        mean, var, rstd, rtmp = (sb(n, [P, 2 * LD]) for n in ("mean", "var", "rstd", "rtmp"))
        ln_a, ln_b, ln_c, ln_d = (sb(n, [P, T]) for n in ("ln_a", "ln_b", "ln_c", "ln_d"))

        banks = ctx.enter_context(nc.psum_tensor("banks", [P, 8, 512], F32))
        tops_ps = banks[:, 0:4, :].rearrange("p b n -> p (b n)")
        T_ps = [banks[:, u, :] for u in range(PAIR)]
        A_ps = [banks[:, 2 + u, :] for u in range(PAIR)]
        B_ps = [banks[:, 4 + u, :] for u in range(PAIR)]
        sum_ps = banks[:, 6, :]
        agg_ps = banks[0:D, 0:7, :].rearrange("p b n -> p (b n)")
        gin_mid_ps = [banks[:, u, :] for u in range(2)]
        gin_out_ps = [banks[:, 2 + u, 0:STRIP // P * D] for u in range(2)]
        spread_ps = banks[:, 0:7, :].rearrange("p b n -> p (b n)")

        tops_landed, edges_landed, vec_landed, weights_landed = (
            sem(n) for n in ("tops_landed", "edges_landed", "vec_landed", "weights_landed"))
        iota_done, ident_done, ones_done, pads_ready = (sem(n) for n in ("iota_done", "ident_done", "ones_done", "pads_ready"))
        tops_ready, tops_spread, sw_ready, sw_stored = (sem(n) for n in ("tops_ready", "tops_spread", "sw_ready", "sw_stored"))
        blk_ready, dst_gathered = sem("blk_ready"), sem("dst_gathered")
        rp_ready, rp_stored, rp1_landed = sem("rp_ready"), sem("rp_stored"), sem("rp1_landed")
        key_ready, key_stored, key_landed = sem("key_ready"), sem("key_stored"), sem("key_landed")
        rec_ready, recs_landed = sem("rec_ready"), sem("recs_landed")
        deg_ready, deg_maxed, x_gathered = (sem(n) for n in ("deg_ready", "deg_maxed", "x_gathered"))
        meta_sp, meta_pool = sem("meta_sp"), sem("meta_pool")
        pick_ready, pair_gathered = sem("pick_ready"), sem("pair_gathered")
        ell_ready, ell_stored, ell_free_new = sem("ell_ready"), sem("ell_stored"), sem("ell_free_new")
        ell_all = sem("ell_all")
        pads_stored = sem("pads_stored")
        dve_chain, act_chain, pool_chain = sem("dve_chain"), sem("act_chain"), sem("pool_chain")
        ticks = {e: sem(f"ticks_{e}") for e in ("dve", "pool", "act")}
        ell_landed = [sem(f"ell_landed{u}") for u in range(RING)]
        ell_free = [sem(f"ell_free{u}") for u in range(RING)]
        rows_free = [sem(f"rows_free{u}") for u in range(RING)]
        rows_landed = [[sem(f"rows_landed{l}_{u}") for u in range(RING)] for l in range(3)]
        row_ready = [sem(f"row_ready{u}") for u in range(PAIR)]
        row_stored = [sem(f"row_stored{u}") for u in range(PAIR)]
        x_staged = [sem(f"x_staged{u}") for u in range(PAIR)]
        xT_made = [sem(f"xT_made{u}") for u in range(PAIR)]
        xT_copied = [sem(f"xT_copied{u}") for u in range(PAIR)]
        mid_made = [sem(f"mid_made{u}") for u in range(PAIR)]
        mid_copied = [sem(f"mid_copied{u}") for u in range(PAIR)]
        A_made = [sem(f"A_made{u}") for u in range(PAIR)]
        A_free = [sem(f"A_free{u}") for u in range(PAIR)]
        B_made = [sem(f"B_made{u}") for u in range(PAIR)]
        B_free = [sem(f"B_free{u}") for u in range(PAIR)]
        dense_in, own_copied = sem("dense_in"), sem("own_copied")
        zeros_ready, zero_rows_ready, adj_zeroed, x_landed = (sem(n) for n in ("zeros_ready", "zero_rows_ready", "adj_zeroed", "x_landed"))
        post_ready, post_free, scattered, adj_built = sem("post_ready"), sem("post_free"), sem("scattered"), sem("adj_built")
        diag_ready, vec_spread, vec_copied = sem("diag_ready"), sem("vec_spread"), sem("vec_copied")
        adj_landed, adj_free = ([sem(f"{n}{u}") for u in range(2)] for n in ("adj_landed", "adj_free"))
        h_staged, h_free = ([sem(f"{n}{u}") for u in range(2)] for n in ("h_staged", "h_free"))
        agg_made, agg_copied = sem("agg_made"), [sem(f"agg_copied{u}") for u in range(2)]
        h_ready, gin_done = sem("h_ready"), sem("gin_done")
        emb_z, emb_silu, emb_made, emb_copied = ([sem(f"{n}{u}") for u in range(2)] for n in ("emb_z", "emb_silu", "emb_made", "emb_copied"))
        x1_ready, x1_stored = sem("x1_ready"), sem("x1_stored")
        ht_made, ht_copied, x0_made, x0_added = ([sem(f"{n}{u}") for u in range(2)] for n in ("ht_made", "ht_copied", "x0_made", "x0_added"))
        sqrt_in, sqrt_done, exp_in, exp_done = (sem(n) for n in ("sqrt_in", "sqrt_done", "exp_in", "exp_done"))
        sin_in, sin_done = sem("sin_in"), sem("sin_done")
        sum_in, sum_made = sem("sum_in"), sem("sum_made")
        gat_w_ready = sem("gat_w_ready")
        fin_ready, out_stored = sem("fin_ready"), sem("out_stored")
        PREP_STORES = [len(range(u or PAIR, T, PAIR)) * 16 for u in range(PAIR)]
        SCATTERED = 16
        GROUP = 16 * SLOTS
        LOOP_STORES = T // PAIR * 16

        block = ctx.enter_context(nc.Block())

        def tile_at(t, it, u):
            return t[:, bass.ds(it * PAIR + u, 1), :]

        def plane(ap):
            return ap.rearrange("p a f -> p (a f)")

        @block.sync
        def _(sp):
            sp.dma_start(tops_i, dst_d.rearrange("(a b k) -> a b k", a=1, k=BLOCK)[:, :, 0], allow_slow_non_contiguous=True)\
                .then_inc(tops_landed, 16)
            sp.dma_start(src_i, src_d.rearrange("(p e) -> p e", p=P)).then_inc(edges_landed, 16)
            sp.dma_start(w_f, w_d.rearrange("(p e) -> p e", p=P)).then_inc(edges_landed, 16)
            sp.dma_start(vec[:, :], nv_d.rearrange("(p t) -> p t", p=P)).then_inc(vec_landed, 16)
            sp.dma_start(x_res[:, 0:TILES - 1, :], x_d[0:(TILES - 1) * P, :].rearrange("(t p) f -> p t f", p=P)).then_inc(x_landed, 16)
            take(sp, zeros_ready)
            sp.dma_start(x_res[0:LAST, TILES - 1, :], x_d[(TILES - 1) * P:N, :]).then_inc(x_landed, 16)
            take(sp, pads_ready)
            for l in range(3):
                wide = GAT_OUT[l]
                sp.dma_start(gat_tab[l][PAD:PAD + 1, :], pad_row[0:1, 2 * LD - wide:]).then_inc(pads_stored, 16)
            take(sp, sw_ready)
            sp.dma_start(sw_d[0:EP, :].rearrange("(p e) c -> p e c", p=P), sw).then_inc(sw_stored, 16)
            sp.dma_start(sw_d[EP:EP + 2 * BLOCK, :].rearrange("(a e) c -> a (e c)", a=1), zeros[:, :]).then_inc(sw_stored, 16)
            take(sp, rp_ready)
            sp.dma_start(rp_d[0:NP].rearrange("(p t) -> p t", p=P), rp[:, :]).then_inc(rp_stored, 16)
            sp.dma_start(rp_d[NP:NP + 1].rearrange("(a b) -> a b", a=1), e_end[:, :]).then_inc(rp_stored, 16)
            sp.wait_ge(rp_stored, 32)
            sp.dma_start(rp1[:, :], rp_d[1:NP + 1].rearrange("(p t) -> p t", p=P)).then_inc(rp1_landed, 16)
            take(sp, key_ready)
            sp.dma_start(key_d.rearrange("(p t) -> p t", p=P), key[:, :]).then_inc(key_stored, 16)
            sp.wait_ge(key_stored, 16)
            sp.dma_start(key_all, key_d.partition_broadcast(P)).then_inc(key_landed, 16)
            sp.wait_ge(scattered, 16)
            for u in range(PAIR):
                sp.wait_ge(row_stored[u], PREP_STORES[u])
            sp.dma_start(recs[:, :, :], rec_d.rearrange("(t p) c -> p t c", p=P)).then_inc(recs_landed, 16)
            take(sp, meta_sp)
            with sp.Fori(0, T) as t:
                blocks = sp.value_load(blocks_i[0:1, bass.ds(t, 1)], min_val=1, max_val=BLOCKS + 1)
                start = sp.value_load(start_i[0:1, bass.ds(t, 1)], min_val=0, max_val=CHUNKS - PER_BLOCK)
                with sp.Fori(0, blocks) as s:
                    take(sp, ell_ready)
                    row = nc.s_assert_within(start + s * PER_BLOCK, 0, CHUNKS - PER_BLOCK,
                                             skip_runtime_bounds_check_because="CHUNKS has room for every tile's last block")
                    sp.dma_start(ell_d[bass.ds(row, PER_BLOCK), :, :].rearrange("k p c -> p k c"),
                                 ell_new[:, :, :]).then_inc(ell_stored, 16)
                    take(sp, ell_stored, 16)
                    sp.sem_inc(ell_free_new, 1)
            take(sp, adj_built)

            def load_adj(u, at):
                take(sp, adj_free[u])
                sp.dma_start(adj_buf[u], adj_t[bass.ds(at * (2 * P), 2 * P), :].rearrange("(b p) n -> p b n", p=P)).then_inc(adj_landed[u], 16)

            for l in range(3):
                load_adj(l % 2, 0)
                with sp.Fori(0, DOUBLES // 2) as it:
                    load_adj(1 - l % 2, it * 2 + 1)
                    load_adj(l % 2, it * 2 + 2)
            take(sp, x1_ready)
            sp.dma_start(x1_d.rearrange("(t p) f -> p t f", p=P), x_res[:, :, :]).then_inc(x1_stored, 16)
            rounds = sp.value_load(meta[0:1, 0:1], min_val=1, max_val=CHUNKS // RING)
            for layer in range(3):
                with sp.Fori(0, rounds) as it:
                    for u in range(RING):
                        take(sp, ell_free[u])
                        sp.dma_start(ell[u][:, :], ell_d[bass.ds(it * RING + u, 1), :, :].rearrange("k p c -> (k p) c"))\
                          .then_inc(ell_landed[u], 16)

        @block.gpsimd
        def _(pool):
            g = nc.gpsimd
            chain = Chain(pool, pool_chain)

            def gather(dst, table, idx):
                return g.indirect_dma_start(out=dst, out_offset=None, in_=table,
                                            in_offset=bass.IndirectOffsetOnAxis(ap=idx, axis=0))

            def scatter(table, idx, data):
                return g.indirect_dma_start(out=table, out_offset=bass.IndirectOffsetOnAxis(ap=idx, axis=0),
                                            in_=data, in_offset=None)

            g.iota(id_i[:, :], pattern=[[1, T]], base=0, channel_multiplier=T).then_inc(iota_done, 1)
            g.iota(slot_i[:, :], pattern=[[1, BLOCK]], base=0, channel_multiplier=0).then_inc(iota_done, 1)
            chain(g.memset(ident[:, :], 0.0))
            g.affine_select(out=ident[:, :], in_=ident[:, :], compare_op=ALU.not_equal, fill=1.0, base=0,
                            pattern=[[-1, P]], channel_multiplier=1).then_inc(ident_done, 1)
            take(pool, blk_ready)
            for t in range(T):
                gather(dst_i[:, t, :], dst_d.rearrange("(b k) -> b k", k=BLOCK), blk_i[:, t:t + 1]).then_inc(dst_gathered, 16)
            take(pool, rec_ready)
            for t in range(T):
                scatter(rec_d, rank_i[:, t:t + 1], rec[:, t, :]).then_inc(row_stored[t % PAIR] if t else scattered, 16)
            take(pool, deg_ready)
            g.partition_all_reduce(deg_max[:, :], recs[:, :, 1], P, R_MAX).then_inc(deg_maxed, 1)
            take(pool, meta_pool)
            pool.wait_ge(sw_stored, 32)
            sw_blocks = sw_d.rearrange("(b k) c -> b (k c)", k=BLOCK)
            adj_cells = adj_t.rearrange("s (n a) -> (s n) a", a=1)

            def pick_blocks():
                take(pool, pick_ready)
                for j in range(2):
                    gather(pair[:, j, :], sw_blocks, pick_i[:, j:j + 1]).then_inc(pair_gathered, 16)

            pick_blocks()
            pool.wait_ge(adj_zeroed, 16 * ZERO_FILLS)
            with pool.Fori(0, T) as t:
                blocks = pool.value_load(blocks_i[0:1, bass.ds(t, 1)], min_val=1, max_val=BLOCKS + 1)
                start = pool.value_load(start_i[0:1, bass.ds(t, 1)], min_val=0, max_val=CHUNKS - PER_BLOCK)
                chunks = pool.value_load(chunks_i[0:1, bass.ds(t, 1)], min_val=0, max_val=CHUNKS)
                with pool.Fori(0, blocks) as s:
                    pick_blocks()
                    pool.wait_ge(scattered, (start + s * PER_BLOCK) * GROUP + SCATTERED)
                    pool.sem_inc(ticks["pool"], 1)
                    pool.sem_inc(post_free, 1)
                    take(pool, post_ready)
                    for j in range(PER_BLOCK):
                        with pool.If(chunks - s * PER_BLOCK > j):
                            for r in range(j * SLOTS, (j + 1) * SLOTS):
                                scatter(adj_cells, post_i[:, r:r + 1], post_w[:, r:r + 1]).then_inc(scattered, 16)
            chunks = pool.value_load(meta[0:1, 1:2], min_val=0, max_val=CHUNKS)
            pool.wait_ge(scattered, chunks * GROUP + SCATTERED)
            pool.sem_inc(adj_built, 1)
            rounds = pool.value_load(meta[0:1, 0:1], min_val=1, max_val=CHUNKS // RING)
            pool.wait_ge(pads_stored, 3 * 16)

            def chunk_gathers(layer, table, width):
                with pool.Fori(0, rounds) as it:
                    for u in range(RING):
                        take(pool, ell_landed[u], 16)
                        take(pool, rows_free[u])
                        for r in range(SLOTS):
                            gather(rows[u][:, r * width:(r + 1) * width], table, ell[u][:, r:r + 1])\
                                .then_inc(rows_landed[layer][u], 16)

            def store_rows(table, width):
                with pool.Fori(0, T // PAIR) as it:
                    for u in range(PAIR):
                        take(pool, row_ready[u])
                        scatter(table, row_node[u][:, 0:1], row_st[u][:, 0:width]).then_inc(row_stored[u], 16)

            def rows_all_stored(loops):
                for u in range(PAIR):
                    pool.wait_ge(row_stored[u], PREP_STORES[u] + LOOP_STORES * loops)

            pool.wait_ge(x1_stored, 16)
            for t in range(T):
                gather(x_res[:, t, :], x1_d, node_i[:, t:t + 1]).then_inc(x_gathered, 16)
            for l in range(3):
                store_rows(gat_tab[l], gat_row[l])
                rows_all_stored(1 + l)
                chunk_gathers(l, gat_tab[l], gat_row[l])
            take(pool, fin_ready)
            for t in range(TILES):
                n = P if t < TILES - 1 else LAST
                scatter(out, node_i[0:n, t:t + 1], x_res[0:n, t, :]).then_inc(out_stored, 16)
            pool.wait_ge(out_stored, 16 * TILES)

        @block.scalar
        def _(act):
            s = nc.scalar
            loads = []

            def load(dst, src):
                act.dma_start(dst, src).then_inc(weights_landed, 16)

            column = lambda v: v.rearrange("(d a) -> d a", a=1)
            load(freqs[:, :], column(freq_d))
            for l, (i1, i2) in enumerate((("11", "12"), ("21", "22"), ("31", "32"))):
                load(w1[l][:, :], a[f"L0_gnn_w{i1}"])
                load(w2[l][:, :], a[f"L0_gnn_w{i2}"])
                load(b1[l][:, :], column(a[f"L0_gnn_b{i1}"]))
                load(b2[l][:, :], a[f"L0_gnn_b{i2}"].partition_broadcast(P))
            load(te_w1[:, :], a["L1_gnn_te_w1"])
            load(te_w2[:, :], a["L1_gnn_te_w2"])
            load(te_b1[:, :], column(a["L1_gnn_te_b1"]))
            load(te_b2[:, :], column(a["L1_gnn_te_b2"]))
            load(init_w[:, :], a["L1_gnn_init_w"])
            load(init_b[:, :], column(a["L1_gnn_init_b"]))
            for l in range(3):
                load(gat_w[l][:, :, 0:GAT_OUT[l]], a[f"L1_gnn_gat_w{l}"].rearrange("(k p) n -> p k n", p=P))
                load(adj_w[l][:, :, :], a[f"L1_gnn_adj_w{l}"].rearrange("(k p) n -> p k n", p=P))
                load(att[l][:, 0, :], a[f"L1_gnn_att_src{l}"].rearrange("h c -> (h c)").partition_broadcast(P))
                load(att[l][:, 1, :], a[f"L1_gnn_att_dst{l}"].rearrange("h c -> (h c)").partition_broadcast(P))
                load(gat_b[l][:, :], a[f"L1_gnn_gat_b{l}"].partition_broadcast(P))
                load(adj_b[l][:, :], a[f"L1_gnn_adj_b{l}"].partition_broadcast(P))
                load(bn_g[l][:, :], a[f"L1_gnn_bn_g{l}"].partition_broadcast(P))
                load(bn_b[l][:, :], a[f"L1_gnn_bn_b{l}"].partition_broadcast(P))
            load(out_w[:, :], a["L1_gnn_out_w"])
            load(out_b[:, :], a["L1_gnn_out_b"].partition_broadcast(P))
            act.wait_ge(zero_rows_ready, 1)
            for n in range(T):
                act.dma_start(adj_t[n * P:(n + 1) * P, :], zero_rows).then_inc(adj_zeroed, 16)
            act.wait_ge(weights_landed, 16 * WEIGHTS)

            def sqrt(n, wide):
                take(act, sqrt_in)
                s.activation(rtmp[:, 0:wide] if n else ln_c[:, :], var[:, 0:wide] if n else ln_b[:, :],
                             ACT.Sqrt).then_inc(sqrt_done, 1)

            def stage(src, it, width):
                for u in range(PAIR):
                    s.activation(x_st[u][:, 0:width], plane(src[:, bass.ds(it * PAIR + u, 1), 0:width]), ACT.Copy)\
                        .then_inc(x_staged[u], 1)

            def copy_T(parts, k):
                for u in range(PAIR):
                    take(act, xT_made[u])
                    s.activation(xT[u][0:parts, 0:k, :].rearrange("p k n -> p (k n)"), T_ps[u][0:parts, 0:k * P], ACT.Copy)\
                        .then_inc(xT_copied[u], 1)

            take(act, vec_spread)
            s.activation(arg, spread_ps[:, 0:NP], ACT.Copy).then_inc(vec_copied, 1)
            sqrt(0, 0)
            for l in range(3):
                m = GIN_MID[l]
                take(act, h_ready)

                def stage_h(u, at):
                    take(act, h_free[u])
                    s.activation(h_st[u][:, :, :], h_in[:, bass.ds(at * 2, 2), :], ACT.Copy).then_inc(h_staged[u], 1)

                stage_h(l % 2, 0)
                with act.Fori(0, DOUBLES // 2) as it:
                    stage_h(1 - l % 2, it * 2 + 1)
                    stage_h(l % 2, it * 2 + 2)
                if l == 0:
                    take(act, sin_in)
                    s.activation(emb_in, arg, ACT.Sin).then_inc(sin_done, 1)
                for u in range(2):
                    take(act, h_free[u])
                    act.sem_inc(h_free[u], 1)
                act.sem_inc(adj_free[l % 2], 1)
                act.sem_inc(agg_made, 1)
                for n, width in STRIPS[0::2]:
                    s.activation(agg_sb[:, n:n + width], agg_ps[:, n:n + width], ACT.Copy).then_inc(agg_copied[0], 1)
                for i, (n, width) in enumerate(STRIPS):
                    take(act, mid_made[i % 2])
                    s.activation(gin_mid[i % 2][0:m, 0:width], gin_mid_ps[i % 2][0:m, 0:width], ACT.Relu, bias=b1[l][:, 0:1])                        .then_inc(mid_copied[i % 2], 1)
                if l == 0:
                    for i, (n, width) in enumerate(STRIPS):
                        take(act, emb_z[i % 2])
                        s.activation(emb_mid[:, n:n + width], banks[:, i % 2, 0:width], ACT.Silu, bias=te_b1[:, 0:1]).then_inc(emb_silu[i % 2], 1)
                    for i, (n, width) in enumerate(STRIPS):
                        take(act, emb_made[i % 2])
                        s.activation(emb[:, n:n + width], banks[:, 2 + i % 2, 0:width], ACT.Identity, bias=te_b2[:, 0:1]).then_inc(emb_copied[i % 2], 1)
            sqrt(0, 0)
            for i, (n, width) in enumerate(STRIPS):
                take(act, ht_made[i % 2])
                s.activation(h_t[:, n:n + width], banks[0:D, i % 2, 0:width], ACT.Copy).then_inc(ht_copied[i % 2], 1)
            for l in range(3):
                wide, k = GAT_OUT[l], kin[l]
                stored = LOOP_STORES * l
                take(act, dense_in)
                with act.Fori(0, T // PAIR) as it:
                    if l == 0:
                        for u in range(PAIR):
                            s.activation(xT[u][:, 0, :], x0_t[:, bass.ds((it * PAIR + u) * P, P)], ACT.Copy).then_inc(xT_copied[u], 1)
                    else:
                        stage(x_a, it, GAT_IN[l])
                        copy_T(P, k)
                    for u in range(PAIR):
                        act.wait_ge(row_stored[u], stored + PREP_STORES[u] + it * 16)
                        act.sem_inc(ticks["act"], 1)
                        s.activation(row_node[u][:, :], recs[:, bass.ds(it * PAIR + u, 1), 2], ACT.Copy)
                        take(act, A_made[u])
                        s.activation(row_st[u][:, 0:wide + HEADS], A_ps[u][:, 0:wide + HEADS], ACT.Copy).then_inc(row_ready[u], 1)
                        s.activation(plane(tile_at(sd, it, u)), A_ps[u][:, wide:wide + 2 * HEADS], ACT.Copy)
                        s.activation(plane(acc[:, bass.ds(it * PAIR + u, 1), 0:wide]), A_ps[u][:, 0:wide], ACT.Copy)\
                            .then_inc(A_free[u], 1)
                for u in range(PAIR):
                    take(act, A_free[u])
                    act.sem_inc(A_free[u], 1)
                act.sem_inc(own_copied, 1)
                rounds = act.value_load(meta[0:1, 0:1], min_val=1, max_val=CHUNKS // RING)
                with act.Fori(0, rounds) as it:
                    for u in range(RING):
                        take(act, exp_in)
                        s.activation(ex[:, :, :], ex_in[:, :, :], ACT.Exp).then_inc(exp_done, 1)
                sqrt(1, wide)
                take(act, exp_in)
                s.activation(res[:, :, 0:wide], x_a[:, :, 0:wide], ACT.Exp, scale=-1.0).then_inc(exp_done, 1)
            take(act, dense_in)
            with act.Fori(0, T // PAIR) as it:
                stage(x_a, it, LD)
                copy_T(P, 1)

        @block.tensor
        def _(pe):
            t = nc.tensor
            take(pe, ones_done)
            take(pe, tops_ready)
            for n in range(0, BLOCKS, 512):
                m = min(512, BLOCKS - n)
                last = t.matmul(tops_ps[:, n:n + m], ones[0:1, :], tops_f[:, n:n + m], start=True, stop=True)
            last.then_inc(tops_spread, 1)
            pe.wait_ge(ident_done, 1)
            pe.wait_ge(weights_landed, 16 * WEIGHTS)

            def transposes(k, width):
                for u in range(PAIR):
                    take(pe, x_staged[u])
                    for j in range(k):
                        last = t.transpose(T_ps[u][0:width, j * P:(j + 1) * P], x_st[u][:, j * P:j * P + width], ident[:, :])
                    last.then_inc(xT_made[u], 1)

            take(pe, diag_ready)
            for tile in range(T):
                last = t.matmul(spread_ps[:, tile * P:(tile + 1) * P], ones[:, :], turn[:, tile * P:(tile + 1) * P], start=True, stop=True)
            last.then_inc(vec_spread, 1)
            pe.wait_ge(vec_copied, 1)
            for l in range(3):
                m = GIN_MID[l]

                def own(u, at, b):
                    return t.matmul(agg_ps[:, bass.ds((at * 2 + b) * P, P)], h_st[u][:, b, :], ident[:, :], start=False, stop=False)

                def neighbours(u, b, first=False, last=False):
                    for n, width in STRIPS:
                        ins = t.matmul(agg_ps[:, n:n + width], h_st[u][:, b, :], adj_buf[u][:, b, n:n + width], start=first, stop=last)
                    return ins

                def aggregate(u, at, first=False):
                    take(pe, h_staged[u])
                    take(pe, adj_landed[u], 16)
                    neighbours(u, 0, first=first)
                    neighbours(u, 1).then_inc(adj_free[u], 1)
                    own(u, at, 0)
                    own(u, at, 1).then_inc(h_free[u], 1)

                aggregate(l % 2, 0, first=True)
                with pe.Fori(0, DOUBLES // 2 - 1) as it:
                    aggregate(1 - l % 2, it * 2 + 1)
                    aggregate(l % 2, it * 2 + 2)
                aggregate(1 - l % 2, DOUBLES - 2)
                u = l % 2
                take(pe, h_staged[u])
                take(pe, adj_landed[u], 16)
                own(u, DOUBLES - 1, 0)
                own(u, DOUBLES - 1, 1)
                neighbours(u, 0)
                neighbours(u, 1, last=True).then_inc(h_free[u], 1)
                for u in range(2):
                    take(pe, agg_copied[u], len(STRIPS[u::2]))

                def gin_out(i, width):
                    take(pe, mid_copied[i % 2])
                    take(pe, B_free[i % 2])
                    for k in range(width // P):
                        ins = t.matmul(gin_out_ps[i % 2][:, k * D:(k + 1) * D], gin_mid[i % 2][0:m, k * P:(k + 1) * P], w2[l][:, :],
                                       start=True, stop=True)
                    ins.then_inc(B_made[i % 2], 1)

                for i, (n, width) in enumerate(STRIPS):
                    t.matmul(gin_mid_ps[i % 2][0:m, 0:width], w1[l][:, :], agg_sb[:, n:n + width], start=True, stop=True)                        .then_inc(mid_made[i % 2], 1)
                    if i:
                        gin_out(i - 1, STRIP)
                gin_out(i, width)
                for u in range(2):
                    take(pe, B_free[u])
                    pe.sem_inc(B_free[u], 1)
                if l == 0:
                    take(pe, sin_done)
                    for i, (n, width) in enumerate(STRIPS):
                        if i >= 2:
                            pe.wait_ge(emb_silu[i % 2], i // 2)
                        t.matmul(banks[:, i % 2, 0:width], te_w1[:, :], emb_in[:, n:n + width], start=True, stop=True).then_inc(emb_z[i % 2], 1)
                    for i, (n, width) in enumerate(STRIPS):
                        pe.wait_ge(emb_silu[i % 2], i // 2 + 1)
                        if i >= 2:
                            pe.wait_ge(emb_copied[i % 2], i // 2)
                        t.matmul(banks[:, 2 + i % 2, 0:width], te_w2[:, :], emb_mid[:, n:n + width], start=True, stop=True).then_inc(emb_made[i % 2], 1)
                    for u in range(2):
                        pe.wait_ge(emb_copied[u], len(STRIPS[u::2]))
            take(pe, h_ready)
            for i, (n, width) in enumerate(STRIPS):
                if i >= 2:
                    pe.wait_ge(ht_copied[i % 2], i // 2)
                for k in range(0, width, P):
                    last = t.transpose(banks[0:D, i % 2, k:k + P], h_in[:, (n + k) // P, :], ident[:, :])
                last.then_inc(ht_made[i % 2], 1)
            for i, (n, width) in enumerate(STRIPS):
                pe.wait_ge(ht_copied[i % 2], i // 2 + 1)
                if i >= 2:
                    pe.wait_ge(x0_added[i % 2], i // 2)
                t.matmul(banks[:, 2 + i % 2, 0:width], init_w[:, :], h_t[:, n:n + width], start=True, stop=True).then_inc(x0_made[i % 2], 1)

            def column_sums(src, wide):
                take(pe, sum_in)
                for n in range(TILES):
                    last = t.matmul(sum_ps[:, 0:wide], (ones if n < TILES - 1 else ones_last)[:, :], src[:, n, 0:wide],
                                    start=(n == 0), stop=(n == TILES - 1))
                last.then_inc(sum_made, 1)

            take(pe, gat_w_ready)
            for l in range(3):
                wide, k = GAT_OUT[l], kin[l]
                with pe.Fori(0, T // PAIR) as it:
                    if l:
                        transposes(k, P)
                    for u in range(PAIR):
                        take(pe, xT_copied[u])
                        take(pe, B_free[u])
                        for j in range(k):
                            last = t.matmul(B_ps[u][:, 0:wide], xT[u][:, j, :], adj_w[l][:, j, :],
                                            start=(j == 0), stop=(j == k - 1))
                        last.then_inc(B_made[u], 1)
                        take(pe, A_free[u])
                        for j in range(k):
                            last = t.matmul(A_ps[u][:, 0:wide + 2 * HEADS], xT[u][:, j, :], gat_w[l][:, j, :],
                                            start=(j == 0), stop=(j == k - 1))
                        last.then_inc(A_made[u], 1)
                column_sums(acc, wide)
                column_sums(res, wide)
            with pe.Fori(0, T // PAIR) as it:
                transposes(1, P)
                for u in range(PAIR):
                    take(pe, xT_copied[u])
                    take(pe, B_free[u])
                    t.matmul(B_ps[u][:, 0:D], xT[u][:, 0, :], out_w[:, :], start=True, stop=True).then_inc(B_made[u], 1)

        @block.vector
        def _(dve):
            v = nc.vector
            link = Chain(dve, dve_chain)

            def signal(sm, n=1):
                dve.sem_inc(sm, n)

            for u in range(RING):
                signal(ell_free[u])
                signal(rows_free[u])
            for u in range(PAIR):
                signal(A_free[u])
                signal(B_free[u])
            for u in range(2):
                signal(adj_free[u])
                signal(h_free[u])
            signal(ell_free_new)
            v.memset(pad_row[:, 0:2 * LD], 0.0)
            link(v.memset(pad_row[:, 2 * LD:], NEG))
            signal(pads_ready)
            link(v.memset(zero_rows, 0.0))
            signal(zero_rows_ready)
            link(v.memset(x_res[:, TILES - 1:, :], 0.0))
            signal(zeros_ready)
            v.memset(quarter[:, :], 0.0)
            v.memset(half_pi[:, :], 0.0)
            link(v.memset(ones[:, :], 1.0))
            v.memset(quarter[HALF:, :], 0.25)
            v.memset(half_pi[HALF:, :], np.pi / 2)
            v.memset(ones_last[:, :], 0.0)
            link(v.memset(zeros[:, :], 0.0))
            link(v.memset(ones_last[0:LAST, :], 1.0))
            signal(ones_done)
            v.memset(e_end[:, :], float(E))
            link(v.memset(zero_t[:, :], 0.0))
            take(dve, iota_done, 2)
            v.tensor_copy(id_f[:, :], id_i[:, :])
            link(v.tensor_copy(slot_f[:, :], slot_i[:, :]))
            dve.wait_ge(tops_landed, 16)
            link(v.tensor_copy(tops_f, tops_i))
            signal(tops_ready)
            dve.wait_ge(edges_landed, 32)
            v.tensor_copy(sw[:, :, 0], src_i)
            link(v.tensor_copy(sw[:, :, 1], w_f))
            signal(sw_ready)
            take(dve, tops_spread)
            for t in range(T):
                link(v.tensor_scalar(junk[:, 0:BLOCKS], tops_ps[:, 0:BLOCKS], id_f[:, t:t + 1], None, ALU.is_lt, ALU.add,
                                     accum_out=cnt[:, t:t + 1]))
            link(v.tensor_scalar(blk[:, :], cnt[:, :], -1.0, 0.0, ALU.add, ALU.max))
            link(v.tensor_copy(blk_i[:, :], blk[:, :]))
            signal(blk_ready)
            dve.wait_ge(dst_gathered, 16 * T)
            link(v.tensor_copy(dst_f, dst_i))
            link(v.tensor_tensor(below, dst_f, id_f[:, :].unsqueeze(2).to_broadcast([P, T, BLOCK]), ALU.is_lt))
            link(v.tensor_reduce(cnt[:, :], below, AX.X, ALU.add))
            link(v.scalar_tensor_tensor(rp[:, :], blk[:, :], float(BLOCK), cnt[:, :], ALU.mult, ALU.add))
            signal(rp_ready)
            dve.wait_ge(rp1_landed, 16)
            v.tensor_copy(rec[:, :, 0], rp[:, :])
            v.tensor_copy(rec[:, :, 2], id_f[:, :])
            link(v.tensor_tensor(rec[:, :, 1], rp1[:, :], rp[:, :], ALU.subtract))
            link(v.tensor_scalar(key[:, :], rec[:, :, 1], 4095.0, 4096.0, ALU.min, ALU.mult))
            link(v.tensor_tensor(key[:, :], key[:, :], id_f[:, :], ALU.subtract))
            link(v.tensor_scalar(key[:, :], key[:, :], 4095.0, None, ALU.add))
            signal(key_ready)
            dve.wait_ge(key_landed, 16)
            for t in range(T):
                link(v.tensor_scalar(junk, key_all, key[:, t:t + 1], None, ALU.is_gt, ALU.add, accum_out=rank[:, t:t + 1]))
            dve.wait_ge(vec_landed, 16)
            v.tensor_copy(rec[:, :, 3], vec[:, :])
            link(v.tensor_copy(rank_i[:, :], rank[:, :]))
            signal(rec_ready)
            dve.wait_ge(recs_landed, 16)
            signal(deg_ready)
            link(v.tensor_copy(node_i[:, :], recs[:, :, 2]))
            link(v.tensor_copy(first_i[:, :], recs[:, :, 0]))
            link(v.tensor_scalar(tmp_i[:, :], first_i[:, :], 6, None, ALU.arith_shift_right))
            v.memset(first_blk[:, T:], 0.0)
            link(v.tensor_copy(first_blk[:, 0:T], tmp_i[:, :]))
            for b in range(6):
                link(v.tensor_scalar(tmp_i[:, :], first_i[:, :], b, 1, ALU.arith_shift_right, ALU.bitwise_and))
                link(v.tensor_copy(bit[:, b, :], tmp_i[:, :]))
            link(v.tensor_scalar(nbit[:, :, :], bit[:, :, :], -1.0, 1.0, ALU.mult, ALU.add))
            take(dve, deg_maxed)

            def ceil_div(dst, shift):
                link(v.tensor_scalar(chunks_f[:, :], deg_max[:, :], float((1 << shift) - 1), None, ALU.add))
                link(v.tensor_copy(tmp_i[:, :], chunks_f[:, :]))
                link(v.tensor_scalar(dst, tmp_i[:, :], shift, None, ALU.arith_shift_right))

            def starts(dst, counts):
                link(v.tensor_copy(chunks_f[:, :], counts))
                link(v.tensor_tensor_scan(start_f[:, :], zero_t[:, :], chunks_f[:, :], 0.0, ALU.add, ALU.add))
                v.tensor_scalar(cnt[:, 0:1], start_f[:, T - 1:T], float(RING - 1), None, ALU.add)
                link(v.tensor_tensor(first_blk_at[:, :], start_f[:, :], chunks_f[:, :], ALU.subtract))
                link(v.tensor_copy(dst, first_blk_at[:, :]))

            ceil_div(blocks_i[:, :], 6)
            link(v.tensor_copy(chunks_f[:, :], blocks_i[:, :]))
            link(v.tensor_scalar(blocks_f[:, :], chunks_f[:, :], 1.0, None, ALU.max))
            link(v.tensor_copy(blocks_i[:, :], blocks_f[:, :]))
            starts(block_start_i[:, :], blocks_i[:, :])
            ceil_div(chunks_i[:, :], SLOTS.bit_length() - 1)
            starts(start_i[:, :], chunks_i[:, :])
            link(v.tensor_copy(tmp_i[:, 0:1], cnt[:, 0:1]))
            v.tensor_copy(meta[:, 1:2], start_f[:, T - 1:T])
            link(v.tensor_scalar(meta[:, 0:1], tmp_i[:, 0:1], RING.bit_length() - 1, None, ALU.arith_shift_right))
            signal(meta_sp)
            signal(meta_pool)
            link(v.memset(tile_no[:, :], 0.0))
            link(v.tensor_scalar(dump[:, :], slot_f[:, :], float(NP), None, ALU.add))
            link(v.tensor_tensor(before[:, :, :], slot_f[:, :].unsqueeze(1).to_broadcast([P, BLOCK, BLOCK]),
                                 slot_f[:, :].unsqueeze(2).to_broadcast([P, BLOCK, BLOCK]), ALU.is_lt))

            def pick():
                v.tensor_scalar(pick_i[:, 0:1], at_blk[:, :], float(BLOCKS), None, ALU.min)
                link(v.tensor_scalar(pick_i[:, 1:2], at_blk[:, :], 1.0, float(BLOCKS), ALU.add, ALU.min))
                signal(pick_ready)

            link(v.tensor_copy(at_blk[:, :], first_blk[:, 0:1]))
            pick()
            dve.wait_ge(ident_done, 1)
            link(v.tensor_tensor(turn.rearrange("p (t n) -> p t n", n=P), ident[:, :].unsqueeze(1).to_broadcast([P, T, P]),
                                 recs[:, :, 3].unsqueeze(2).to_broadcast([P, T, P]), ALU.mult))
            signal(diag_ready)
            dve.wait_ge(adj_zeroed, 16 * ZERO_FILLS)
            link.reset()
            with dve.Fori(0, T) as t:
                v.tensor_copy(blocks_left[:, :], blocks_f[:, bass.ds(t, 1)])
                link(v.tensor_copy(left[:, :], recs[:, bass.ds(t, 1), 1]))
                blocks = dve.value_load(blocks_i[0:1, bass.ds(t, 1)], min_val=1, max_val=BLOCKS + 1)
                block_start = dve.value_load(block_start_i[0:1, bass.ds(t, 1)], min_val=0, max_val=BLOCKS + T)
                link.reset()
                with dve.Fori(0, blocks) as s:
                    link(v.tensor_scalar(blocks_left[:, :], blocks_left[:, :], -1.0, None, ALU.add))
                    v.tensor_scalar(is_last[:, :], blocks_left[:, :], 0.0, None, ALU.is_le)
                    v.tensor_scalar(next_blk[:, :], at_blk[:, :], 1.0, None, ALU.add)
                    link(v.tensor_scalar(valid[:, :], slot_f[:, :], left[:, 0:1], None, ALU.is_lt))
                    link(v.tensor_tensor(at_blk[:, :], first_blk[:, bass.ds(t + 1, 1)], next_blk[:, :], ALU.subtract))
                    link(v.scalar_tensor_tensor(at_blk[:, :], at_blk[:, :], is_last[:, 0:1], next_blk[:, :], ALU.mult, ALU.add))
                    dve.wait_ge(pair_gathered, (block_start + s) * 32 + 32)
                    signal(ticks["dve"])
                    cur = pair[:, :, :].rearrange("p j n -> p (j n)")
                    for b in range(5, -1, -1):
                        keep = BLOCK + (1 << b) - 1
                        by = 2 << b
                        link(v.tensor_scalar(shift_a[:, 0:2 * keep], cur[:, 0:2 * keep], nbit[:, b, bass.ds(t, 1)], None, ALU.mult))
                        link(v.scalar_tensor_tensor(shift_b[:, 0:2 * keep], cur[:, by:by + 2 * keep], bit[:, b, bass.ds(t, 1)],
                                                    shift_a[:, 0:2 * keep], ALU.mult, ALU.add))
                        if b == 5:
                            pick()
                        cur = shift_b
                    sw_now = shift_b[:, 0:2 * BLOCK].rearrange("p (e c) -> p e c", c=2)
                    take(dve, ell_free_new)
                    v.tensor_tensor(w_valid[:, :], sw_now[:, :, 1], valid[:, :], ALU.mult)
                    link(v.scalar_tensor_tensor(srcv[:, :], sw_now[:, :, 0], float(-PAD), valid[:, :], ALU.add, ALU.mult))
                    v.tensor_scalar(ell_new[:, :, 0:SLOTS], srcv[:, :].rearrange("p (k r) -> p k r", r=SLOTS), float(PAD), None, ALU.add)
                    v.tensor_copy(ell_new[:, :, TILE_AT], tile_no[:, :].to_broadcast([P, PER_BLOCK]))
                    link(v.tensor_tensor(adj_row[:, :], sw_now[:, :, 0], dump[:, :], ALU.subtract))
                    signal(ell_ready)
                    link(v.tensor_tensor(adj_row[:, :], adj_row[:, :], valid[:, :], ALU.mult))
                    link(v.tensor_tensor(adj_row[:, :], adj_row[:, :], dump[:, :], ALU.add))
                    square = [P, BLOCK, BLOCK]
                    link(v.tensor_tensor(same[:, :, :], adj_row[:, :].unsqueeze(1).to_broadcast(square),
                                         adj_row[:, :].unsqueeze(2).to_broadcast(square), ALU.is_equal))
                    link(v.tensor_tensor(same_w, same[:, :, :], w_valid[:, :].unsqueeze(1).to_broadcast(square), ALU.mult))
                    link(v.tensor_reduce(adj_w_new[:, :], same_w, AX.X, ALU.add))
                    link(v.tensor_tensor(same[:, :, :], same[:, :, :], before[:, :, :], ALU.mult))
                    link(v.tensor_reduce(repeats[:, :], same[:, :, :], AX.X, ALU.max))
                    link(v.tensor_tensor(srcv[:, :], dump[:, :], adj_row[:, :], ALU.subtract))
                    link(v.tensor_tensor(srcv[:, :], srcv[:, :], repeats[:, :], ALU.mult))
                    link(v.tensor_tensor(adj_row[:, :], srcv[:, :], adj_row[:, :], ALU.add))
                    link(v.tensor_scalar(adj_row[:, :], adj_row[:, :], float(NP), recs[:, bass.ds(t, 1), 2], ALU.mult, ALU.add))
                    take(dve, post_free)
                    v.tensor_copy(post_i[:, :], adj_row[:, :])
                    v.tensor_copy(post_w[:, :], adj_w_new[:, :])
                    link(v.tensor_scalar(left[:, :], left[:, :], float(-BLOCK), None, ALU.add))
                    signal(post_ready)
                    link.reset()
                link(v.tensor_scalar(tile_no[:, :], tile_no[:, :], 1.0, None, ALU.add))
                link.reset()

            def layernorm(dst, room):
                def spread(s):
                    return s[:, :].unsqueeze(2).to_broadcast([P, T, D])
                link(v.tensor_reduce(ln_a[:, :], x_res[:, :, :], AX.X, ALU.add))
                link(v.tensor_scalar(ln_a[:, :], ln_a[:, :], 1.0 / D, None, ALU.mult))
                centred, square = (room[:, n * T * D:(n + 1) * T * D].rearrange("p (t f) -> p t f", f=D) for n in range(2))
                link(v.tensor_tensor(centred, x_res[:, :, :], spread(ln_a), ALU.subtract))
                link(v.tensor_tensor(square, centred, centred, ALU.mult))
                link(v.tensor_reduce(ln_a[:, :], square, AX.X, ALU.add))
                link(v.tensor_scalar(ln_b[:, :], ln_a[:, :], 1.0 / D, LN_EPS, ALU.mult, ALU.add))
                signal(sqrt_in)
                take(dve, sqrt_done)
                link(v.reciprocal(ln_c[:, :], ln_c[:, :]))
                newton(ln_c[:, :], ln_b[:, :], ln_d[:, :])
                link(v.tensor_tensor(centred, centred, spread(ln_c), ALU.mult))
                link(v.tensor_scalar(dst[:, :, :], centred, 0.0, None, ALU.max))

            def newton(y, sq, tmp):
                link(v.tensor_tensor(tmp, y, y, ALU.mult))
                link(v.tensor_tensor(tmp, tmp, sq, ALU.mult))
                link(v.tensor_scalar(tmp, tmp, -0.5, 1.5, ALU.mult, ALU.add))
                link(v.tensor_tensor(y, y, tmp, ALU.mult))

            dve.wait_ge(x_landed, 32)
            dve.wait_ge(vec_copied, 1)
            layernorm(h_in, turn)
            signal(h_ready)
            dve.wait_ge(weights_landed, 16 * WEIGHTS)
            link(v.tensor_scalar(arg, arg, freqs[:, 0:1], None, ALU.mult))
            link(v.tensor_scalar(turn, arg, 1.0 / TWO_PI, quarter[:, 0:1], ALU.mult, ALU.add))
            link(v.tensor_scalar(turn, turn, ROUND, None, ALU.add))
            link(v.tensor_scalar(turn, turn, -ROUND, None, ALU.add))
            link(v.scalar_tensor_tensor(arg, turn, -PI_HI, arg, ALU.mult, ALU.add))
            link(v.scalar_tensor_tensor(arg, turn, -PI_MID, arg, ALU.mult, ALU.add))
            link(v.scalar_tensor_tensor(arg, turn, -PI_LO, arg, ALU.mult, ALU.add))
            link(v.tensor_scalar(arg, arg, half_pi[:, 0:1], 3.1415925, ALU.add, ALU.min))
            link(v.tensor_scalar(arg, arg, -3.1415925, None, ALU.max))
            link(v.tensor_tensor(te_b2[:, :], te_b2[:, :], init_b[:, :], ALU.add))
            signal(sin_in)
            room = part[:, :]
            for l in range(3):
                wide, c = GAT_OUT[l], GAT_OUT[l] // HEADS
                for j in range(kin[l]):
                    for e in range(2):
                        link(v.tensor_tensor(room[:, 0:wide], gat_w[l][:, j, 0:wide], att[l][:, e, :], ALU.mult))
                        link(v.tensor_reduce(gat_w[l][:, j, wide + e * HEADS:wide + (e + 1) * HEADS],
                                             room[:, 0:wide].rearrange("p (h c) -> p h c", c=c), AX.X, ALU.add))
                link(v.tensor_tensor(gat_b[l][:, :], gat_b[l][:, :], adj_b[l][:, :], ALU.add))
            signal(gat_w_ready)
            rounds = dve.value_load(meta[0:1, 0:1], min_val=1, max_val=CHUNKS // RING)
            link.reset()

            def chunk_tile(u):
                return dve.value_load(ell[u][0:1, TILE_AT:TILE_AT + 1], min_val=0, max_val=T - 1)

            for l in range(3):
                take(dve, agg_made)
                for n, width in STRIPS[1::2]:
                    link(v.tensor_copy(agg_sb[:, n:n + width], agg_ps[:, n:n + width]))
                    signal(agg_copied[1])
                for i, (n, width) in enumerate(STRIPS):
                    tiles, k = slice(n // P, (n + width) // P), width // P
                    take(dve, B_made[i % 2])
                    made = gin_out_ps[i % 2][:, 0:k * D].rearrange("p (k f) -> p k f", f=D)
                    bias = b2[l][:, :].unsqueeze(1).to_broadcast([P, k, D])
                    if l < 2:
                        link(v.tensor_tensor(h_in[:, tiles, :], made, bias, ALU.add))
                        signal(B_free[i % 2])
                        link(v.tensor_scalar(h_in[:, tiles, :], h_in[:, tiles, :], 0.0, None, ALU.max))
                    else:
                        link(v.tensor_tensor(h_in[:, tiles, :], made, bias, ALU.add))
                        signal(B_free[i % 2])
                        link(v.tensor_tensor(x_res[:, tiles, :], x_res[:, tiles, :], h_in[:, tiles, :], ALU.add))
                link.reset()
                signal(h_ready if l < 2 else x1_ready)
            dve.wait_ge(x_gathered, 16 * T)
            layernorm(h_in, arg)
            signal(h_ready)
            for u in range(2):
                dve.wait_ge(emb_copied[u], len(STRIPS[u::2]))
            for i, (n, width) in enumerate(STRIPS):
                dve.wait_ge(x0_made[i % 2], i // 2 + 1)
                link(v.tensor_tensor(x0_t[:, n:n + width], banks[:, 2 + i % 2, 0:width], emb[:, n:n + width], ALU.add))
                signal(x0_added[i % 2])
            link.reset()
            for l in range(3):
                wide, c, width = GAT_OUT[l], GAT_OUT[l] // HEADS, gat_row[l]
                signal(dense_in)
                with dve.Fori(0, T // PAIR) as it:
                    for u in range(PAIR):
                        take(dve, B_made[u])
                        link(v.tensor_tensor(plane(res[:, bass.ds(it * PAIR + u, 1), 0:wide]), B_ps[u][:, 0:wide], gat_b[l][:, :], ALU.add))
                        signal(B_free[u])
                    link.reset()
                take(dve, own_copied)
                link(v.tensor_tensor(m_all[:, :, :], sd[:, :, 0:HEADS], sd[:, :, HEADS:], ALU.add))
                link(v.scalar_tensor_tensor(m_all[:, :, :], m_all[:, :, :], LRELU_SLOPE, m_all[:, :, :], ALU.mult, ALU.max))
                link(v.memset(den[:, :, :], 1.0))
                link.reset()
                with dve.Fori(0, rounds) as it:
                    for u in range(RING):
                        dve.wait_ge(rows_landed[l][u], (it + 1) * (16 * SLOTS))
                        signal(ticks["dve"])
                        t = chunk_tile(u)
                        signal(ell_free[u])
                        row = rows[u][:, 0:SLOTS * width].rearrange("p (r f) -> p r f", f=width)
                        now = bass.ds(t, 1)
                        sub = [P, SLOTS, HEADS]
                        link(v.tensor_tensor(score[:, 0:SLOTS, :], row[:, :, wide:], sd[:, now, HEADS:].to_broadcast(sub), ALU.add))
                        link(v.scalar_tensor_tensor(lrel[:, 0:SLOTS, :], score[:, 0:SLOTS, :], LRELU_SLOPE, score[:, 0:SLOTS, :], ALU.mult, ALU.max))
                        link(v.tensor_reduce(top[:, :], lrel[:, 0:SLOTS, :].rearrange("p r h -> p h r"), AX.X, ALU.max))
                        at = plane(m_all[:, now, :])
                        link(v.tensor_tensor(new_max[:, :], at, top[:, :], ALU.max))
                        v.tensor_tensor(ex_in[:, 0:SLOTS, :], lrel[:, 0:SLOTS, :], new_max[:, :].unsqueeze(1).to_broadcast(sub), ALU.subtract)
                        link(v.tensor_tensor(ex_in[:, SLOTS, :], at, new_max[:, :], ALU.subtract))
                        signal(exp_in)
                        link(v.tensor_copy(at, new_max[:, :]))
                        take(dve, exp_done)
                        link(v.tensor_reduce(den_part[:, :], ex[:, 0:SLOTS, :].rearrange("p r h -> p h r"), AX.X, ALU.add))
                        at = plane(den[:, now, :])
                        link(v.tensor_tensor(at, at, ex[:, SLOTS, :], ALU.mult))
                        link(v.tensor_tensor(at, at, den_part[:, :], ALU.add))
                        msg = row[:, :, 0:wide].rearrange("p r (h c) -> p r h c", c=c)
                        link(v.tensor_tensor(msg, msg, ex[:, 0:SLOTS, :].unsqueeze(3).to_broadcast([P, SLOTS, HEADS, c]), ALU.mult))
                        link(v.tensor_reduce(part[:, 0:wide], row[:, :, 0:wide].rearrange("p r f -> p f r"), AX.X, ALU.add))
                        signal(rows_free[u])
                        at = plane(acc[:, now, 0:wide])
                        at_h = at.rearrange("p (h c) -> p h c", c=c)
                        link(v.tensor_tensor(at_h, at_h, ex[:, SLOTS, :].unsqueeze(2).to_broadcast([P, HEADS, c]), ALU.mult))
                        link(v.tensor_tensor(at, at, part[:, 0:wide], ALU.add))
                    link.reset()
                full = [P, T, wide]
                y, z, x = acc[:, :, 0:wide], res[:, :, 0:wide], x_a[:, :, 0:wide]
                link(v.reciprocal(den[:, :, :], den[:, :, :]))
                for t in range(T):
                    v.tensor_tensor(acc[:, t, 0:wide].rearrange("p (h c) -> p h c", c=c), acc[:, t, 0:wide].rearrange("p (h c) -> p h c", c=c),
                                    den[:, t, :].unsqueeze(2).to_broadcast([P, HEADS, c]), ALU.mult)
                link(v.memset(part[:, 0:1], 0.0))
                link(v.tensor_tensor(y, y, z, ALU.add))
                signal(sum_in)
                take(dve, sum_made)
                link(v.tensor_scalar(mean[:, 0:wide], sum_ps[:, 0:wide], 1.0 / N, None, ALU.mult))
                link(v.tensor_tensor(y, y, mean[:, 0:wide].unsqueeze(1).to_broadcast(full), ALU.subtract))
                link(v.tensor_tensor(z, y, y, ALU.mult))
                signal(sum_in)
                take(dve, sum_made)
                link(v.tensor_scalar(var[:, 0:wide], sum_ps[:, 0:wide], 1.0 / N, BN_EPS, ALU.mult, ALU.add))
                signal(sqrt_in)
                take(dve, sqrt_done)
                link(v.reciprocal(rstd[:, 0:wide], rtmp[:, 0:wide]))
                newton(rstd[:, 0:wide], var[:, 0:wide], rtmp[:, 0:wide])
                link(v.tensor_tensor(rstd[:, 0:wide], rstd[:, 0:wide], bn_g[l][:, :], ALU.mult))
                link(v.tensor_tensor(y, y, rstd[:, 0:wide].unsqueeze(1).to_broadcast(full), ALU.mult))
                link(v.tensor_tensor(x, y, bn_b[l][:, :].unsqueeze(1).to_broadcast(full), ALU.add))
                signal(exp_in)
                take(dve, exp_done)
                link(v.tensor_scalar(z, z, 1.0, None, ALU.add))
                link(v.reciprocal(z, z))
                link(v.tensor_tensor(x, x, z, ALU.mult))
                link.reset()
            signal(dense_in)
            with dve.Fori(0, T // PAIR) as it:
                for u in range(PAIR):
                    take(dve, B_made[u])
                    link(v.tensor_tensor(row_tmp[u][:, :], B_ps[u][:, 0:D], out_b[:, :], ALU.add))
                    signal(B_free[u])
                    at = plane(tile_at(x_res, it, u))
                    link(v.tensor_tensor(at, at, row_tmp[u][:, :], ALU.add))
                link.reset()
            signal(fin_ready)


WEIGHTS = 1 + 3 * 4 + 6 + 3 * 8 + 2
ZERO_FILLS = T


def kernel(**inputs):
    import concourse.bacc as bacc
    from concourse.bass_utils import run_bass_kernel_spmd

    nc = bacc.Bacc("TRN2", target_bir_lowering=False, num_devices=1)
    arrays = {k: np.asarray(x) for k, x in inputs.items()}

    def padded(x, n, fill):
        y = np.full((n,), fill, x.dtype)
        y[:x.shape[0]] = x
        return y

    arrays["src"] = padded(arrays["src"], EP, 0)
    arrays["dst"] = padded(arrays["dst"], EP, 2 * NP)
    arrays["edge_weight"] = padded(arrays["edge_weight"], EP, 0)
    arrays["node_vec"] = padded(arrays["node_vec"], NP, 0)
    steps = np.arange(HALF, dtype=np.float32) / np.float32(HALF)
    arrays["freqs"] = np.tile(np.float32(1.0 / 10000.0) ** steps, 2)
    aps = {k: nc.dram_tensor(f"in_{k}", x.shape, mybir.dt.from_np(x.dtype), kind="ExternalInput").ap() for k, x in arrays.items()}
    out = nc.dram_tensor("out", (N, D), F32, kind="ExternalOutput").ap()
    program(nc, aps, out, ())
    result = run_bass_kernel_spmd(nc, [{f"in_{k}": x for k, x in arrays.items()}], core_ids=[0])
    return result.results[0]["out"]
```

```python
from contextlib import ExitStack

import numpy as np

import concourse.bass as bass
from concourse import mybir

F32, I32, BF16 = mybir.dt.float32, mybir.dt.int32, mybir.dt.bfloat16
ALU, ACT, AX = mybir.AluOpType, mybir.ActivationFunctionType, mybir.AxisListType
R_MAX = bass.bass_isa.ReduceOp.max

P = 128
N = 3125
E = 103125
D = 64
LD = 128
HEADS = 8
TILES = -(-N // P)
T = TILES + 1
NP = T * P
LAST = N - (TILES - 1) * P
PAD = NP
BLOCK = 64
EP = -(-E // (P * 2)) * P * 2
EC = EP // P
BLOCKS = EP // BLOCK
SLOTS = 4
PER_BLOCK = BLOCK // SLOTS
DVE_TILES = T // 2
SORT_TILES = EP // P
RING = 6
TILE_AT = SLOTS
CHUNK = TILE_AT + 1
CHUNKS = E // SLOTS + T + PER_BLOCK * T + RING
LN_EPS = BN_EPS = 1e-5
LRELU_SLOPE = 0.2
NEG = -1.0e30
HALF = LD // 2
PAIR = 2
STEPS = T // PAIR
SILU_STEPS = ((0, 2), (2, 6), (6, STEPS))
SUMS = 3
LAG = 3
STRIP = 512
STRIPS = [(n, min(STRIP, NP - n)) for n in range(0, NP, STRIP)]
NA = TILES * P
NODE_STRIPS = [(n, min(STRIP, NA - n)) for n in range(0, NA, STRIP)]
DOUBLES = TILES // 2
GIN_MID = (64, 128, 64)
GAT_IN = (LD, 2 * LD, 2 * LD)
GAT_OUT = (2 * LD, 2 * LD, LD)
TWO_PI = 2.0 * np.pi
PI_HI = 6.28125
PI_MID = float(np.float32(np.round((TWO_PI - PI_HI) * 2.0**20) / 2.0**20))
PI_LO = float(np.float32(TWO_PI - PI_HI - PI_MID))
ROUND = 12582912.0


class Chain:

    def __init__(self, eng, sem):
        self.eng, self.sem, self.n = eng, sem, 0

    def __call__(self, ins):
        self.n += 1
        ins.then_inc(self.sem, 1)
        self.eng.wait_ge(self.sem, self.n)

    def mark(self, ins):
        self.n += 1
        ins.then_inc(self.sem, 1)
        return self.n

    def wait(self, n):
        self.eng.wait_ge(self.sem, n)

    def reset(self):
        if self.n:
            self.eng.sem_inc(self.sem, -self.n)
        self.n = 0


def take(eng, sem, n=1):
    eng.wait_ge(sem, n)
    eng.sem_inc(sem, -n)


def program(nc, a, out, debug):
    x_d, src_d, dst_d, w_d, nv_d, freq_d = (a[k] for k in ("x", "src", "dst", "edge_weight", "node_vec", "freqs"))

    def dram(name, shape, dt=F32):
        return nc.dram_tensor(name, shape, dt, kind="ExternalOutput" if name in debug else "Internal").ap()

    sw_d = dram("sw_d", (EP + 2 * BLOCK, 2))
    sdst_d = dram("sdst_d", (EP,), I32)
    cnt_d = dram("cnt_d", (NP + 1 + P, 1))
    rp_d = dram("rp_d", (NP + 1,))
    key_d = dram("key_d", (NP,))
    rec_d = dram("rec_d", (NP, 4))
    ell_d = dram("ell_d", (CHUNKS, P, CHUNK), I32)
    adj_t = dram("adj_t", (NA + BLOCK, NA))
    x1_d = dram("x1_d", (NP, D))
    gat_row = [GAT_OUT[l] + HEADS for l in range(3)]
    gat_tab = [dram(f"gat_tab{l}", (NP + 1, gat_row[l])) for l in range(3)]

    with ExitStack() as ctx:
        def sb(name, shape, dt=F32):
            return ctx.enter_context(nc.sbuf_tensor(name, shape, dt))

        def sem(name):
            return ctx.enter_context(nc.semaphore(name))

        ident = sb("ident", [P, P])
        ones = sb("ones", [P, P])
        pad_row = [sb(f"pad_row{l}", [1, gat_row[l]]) for l in range(3)]
        freqs = sb("freqs", [P, 1])
        quarter, half_pi = sb("quarter", [P, 1]), sb("half_pi", [P, 1])
        w1 = [sb(f"w1_{l}", [D, GIN_MID[l]]) for l in range(3)]
        w2 = [sb(f"w2_{l}", [GIN_MID[l], D]) for l in range(3)]
        b1 = [sb(f"b1_{l}", [GIN_MID[l], 1]) for l in range(3)]
        b2 = [sb(f"b2_{l}", [P, D]) for l in range(3)]
        te_w1, te_w2 = sb("te_w1", [LD, LD]), sb("te_w2", [LD, LD])
        te_b1 = sb("te_b1", [LD, 1])
        init_w = sb("init_w", [D, LD])
        init_b, te_b2 = sb("init_b", [LD, 1]), sb("te_b2", [LD, 1])
        kin = [GAT_IN[l] // P for l in range(3)]
        kout = [GAT_OUT[l] // P for l in range(3)]
        head = [GAT_OUT[l] // HEADS for l in range(3)]
        gat_w = [sb(f"gat_w{l}", [P, kin[l], gat_row[l] + HEADS]) for l in range(3)]
        adj_w = [sb(f"adj_w{l}", [P, kin[l], GAT_OUT[l]]) for l in range(3)]
        att = [sb(f"att{l}", [P, 2, GAT_OUT[l]]) for l in range(3)]
        gat_b, adj_b, bn_g, bn_b = ([sb(f"{n}{l}", [P, kout[l]]) for l in range(3)] for n in ("gat_b", "adj_b", "bn_g", "bn_b"))
        out_w = sb("out_w", [LD, D])
        out_b = sb("out_b", [P, D])

        x_t = sb("x_t", [P, 2, NP])
        y_t = sb("y_t", [P, 2, NP])
        acc = sb("acc", [P, T * max(gat_row)])
        x_res = sb("x_res", [P, T, D])
        h_in = sb("h_in", [P, T, D])
        sd = sb("sd", [P, T, HEADS])
        m_all = sb("m_all", [P, T, HEADS])
        den = sb("den", [P, T, HEADS])
        flat = lambda t: t[:, :, :].rearrange("p t f -> p (t f)")
        xf, rf, af = flat(x_t), flat(y_t), acc[:, :]

        key_all, junk = xf[:, 0:NP], xf[:, NP:2 * NP]
        src_i, w_f = rf[:, 0:EC].bitcast(I32), rf[:, EC:2 * EC]
        sw = rf[:, 2 * EC:4 * EC].rearrange("p (e c) -> p e c", c=2)
        dst_i = rf[:, 4 * EC:4 * EC + T * BLOCK].bitcast(I32).rearrange("p (t k) -> p t k", k=BLOCK)
        dst_f = af[:, 0:T * BLOCK].rearrange("p (t k) -> p t k", k=BLOCK)
        below = af[:, T * BLOCK:2 * T * BLOCK].rearrange("p (t k) -> p t k", k=BLOCK)
        tops_i = af[0:1, 2 * T * BLOCK:2 * T * BLOCK + BLOCKS].bitcast(I32)
        tops_f = xf[0:1, 0:BLOCKS]
        zeros = sb("zeros", [1, 4 * BLOCK])
        id_i, id_f = sb("id_i", [P, T], I32), sb("id_f", [P, T])
        slot_i, slot_f = sb("slot_i", [P, BLOCK], I32), sb("slot_f", [P, BLOCK])
        cnt, blk, rp, rp1 = (sb(n, [P, T]) for n in ("cnt", "blk", "rp", "rp1"))
        blk_i, rank_i = sb("blk_i", [P, T], I32), sb("rank_i", [P, T], I32)
        key, rank = sb("key", [P, T]), sb("rank", [P, T])
        dst_all, falls = xf[:, NP:NP + EC].bitcast(I32), xf[:, NP + EC:NP + 2 * EC]
        dst_next, unsorted = sb("dst_next", [P, 1], I32), sb("unsorted", [P, 1])
        sort_n, sort_i = sb("sort_n", [P, 1]), sb("sort_i", [P, 1], I32)
        later = sb("later", [P, P])
        edge_dst, edge_src = sb("edge_dst", [P, 1], I32), sb("edge_src", [P, 1], I32)
        edge_sw, edge_key = sb("edge_sw", [P, 2]), sb("edge_key", [P, 1])
        key_wide, key_same = sb("key_wide", [P, P]), sb("key_same", [P, P])
        place, twins, later_twins, spare, spare_f = (sb(n, [P, 1]) for n in ("place", "twins", "later_twins", "spare", "spare_f"))
        place_i, count_i, spare_i = (sb(n, [P, 1], I32) for n in ("place_i", "count_i", "spare_i"))
        count_to, next_place = sb("count_to", [P, 1], I32), sb("next_place", [P, 1])
        node_count, node_scan, node_start, node_sum = (sb(n, sh) for n, sh in (
            ("node_count", [P, T]), ("node_scan", [P, T]), ("node_start", [P, T]), ("node_sum", [P, 1])))
        tops_all, junk_a = af[:, 2 * T * BLOCK + BLOCKS:2 * T * BLOCK + 2 * BLOCKS], rf[:, 0:NP]
        tops_junk = rf[:, 4 * EC + T * BLOCK:4 * EC + T * BLOCK + BLOCKS]
        id_half, key_neg = sb("id_half", [P, T]), sb("key_neg", [P, T])
        cnt_a, rank_a = sb("cnt_a", [P, T]), sb("rank_a", [P, T])
        e_end = sb("e_end", [1, 1])
        rec = sb("rec", [P, T, 4])
        vec = sb("vec", [P, T])
        recs = sb("recs", [P, T, 4])
        node_i = sb("node_i", [P, T], I32)
        tmp_i, first_i = sb("tmp_i", [P, T], I32), sb("first_i", [P, T], I32)
        first_blk = sb("first_blk", [P, T + 1])
        blocks_f = sb("blocks_f", [P, T])
        bit, nbit = sb("bit", [P, 6, T]), sb("nbit", [P, 6, T])
        deg_max = sb("deg_max", [P, T])
        chunks_i, blocks_i = sb("chunks_i", [P, T], I32), sb("blocks_i", [P, T], I32)
        chunks_f, start_f, zero_t = (sb(n, [P, T]) for n in ("chunks_f", "start_f", "zero_t"))
        first_blk_at, block_start_i = sb("first_blk_at", [P, T]), sb("block_start_i", [P, T], I32)
        start_i, meta = sb("start_i", [P, T], I32), sb("meta", [P, 2], I32)
        at_blk, next_blk, left, blocks_left, is_last, tile_no = (
            sb(n, [P, 1]) for n in ("at_blk", "next_blk", "left", "blocks_left", "is_last", "tile_no"))
        pick_i = sb("pick_i", [P, 2], I32)
        pair = sb("pair", [P, 2, 2 * BLOCK])
        shift_a, shift_b = sb("shift_a", [P, 4 * BLOCK]), sb("shift_b", [P, 4 * BLOCK])
        valid, srcv, dump = sb("valid", [P, BLOCK]), sb("srcv", [P, BLOCK]), sb("dump", [P, BLOCK])
        adj_row, adj_w_new, w_valid, repeats = (sb(n, [P, BLOCK]) for n in ("adj_row", "adj_w_new", "w_valid", "repeats"))
        post_i, post_w = sb("post_i", [P, BLOCK], I32), sb("post_w", [P, BLOCK])
        before = sb("before", [P, BLOCK, BLOCK], BF16)
        same = sb("same", [P, BLOCK, BLOCK], BF16)
        ell_new = sb("ell_new", [P, PER_BLOCK, CHUNK], I32)

        ell = [sb(f"ell{u}", [P, CHUNK], I32) for u in range(RING)]
        rows_all = sb("rows_all", [P, max(RING * SLOTS * max(gat_row), 2 * BLOCK * BLOCK)])
        rows = [rows_all[:, u * SLOTS * max(gat_row):(u + 1) * SLOTS * max(gat_row)] for u in range(RING)]
        zero_rows = rows_all[:, 0:NP + 1 + P]
        same_w = rows_all[:, 0:BLOCK * BLOCK].rearrange("p (r q) -> p r q", q=BLOCK)
        adj_buf = [t[:, 0:2 * NA].rearrange("p (b n) -> p b n", n=NA) for t in (xf, rf)]
        h_st = [sb(f"h_st{u}", [P, 2, D]) for u in range(2)]
        agg_sb = rows_all[0:D, 0:NA]
        gin_mid = [rows_all[:, NP + u * STRIP:NP + (u + 1) * STRIP] for u in range(2)]
        arg, turn = af[:, 0:NP], af[:, NP:2 * NP]
        emb_in, emb_mid, emb = turn, arg, turn
        x0_t = x_t[:, 0, :]
        h_t = rf[0:D, 0:NP]
        tile_kept = sb("tile_kept", [1, RING], I32)
        no_sums = sb("no_sums", [P, max(gat_row)])
        score = sb("score", [P, SLOTS, HEADS])
        lrel, ex_in = sb("lrel", [P, SLOTS + 1, HEADS]), sb("ex_in", [P, SLOTS + 1, HEADS])
        shrink = [sb(f"shrink{u}", [P, HEADS]) for u in range(RING)]

        x_st = [sb(f"x_st{u}", [P, 2 * PAIR * P]) for u in range(2)]
        row_st = [sb(f"row_st{u}", [P, PAIR, max(gat_row) + HEADS]) for u in range(2)]
        row_node = [sb(f"row_node{u}", [P, PAIR], I32) for u in range(2)]
        bn_parts = sb("bn_parts", [P, 2, STEPS])
        bn_sum, bn_sq, mean, var, rstd, rtmp, scale, shift = (
            sb(n, [P, 2]) for n in ("bn_sum", "bn_sq", "mean", "var", "rstd", "rtmp", "scale", "shift"))
        ln_a, ln_b, ln_c, ln_d = (sb(n, [P, T]) for n in ("ln_a", "ln_b", "ln_c", "ln_d"))

        banks = ctx.enter_context(nc.psum_tensor("banks", [P, 8, 512], F32))
        tops_ps = banks[:, 0:4, :].rearrange("p b n -> p (b n)")
        A_ps = [[banks[:, 4 * u + b, :] for b in range(PAIR)] for u in range(2)]
        T_ps = [banks[:, 2 + u, :] for u in range(2)]
        sum_ps = [banks[:, 4 + u, :] for u in range(SUMS)]
        agg_ps = banks[0:D, 0:7, :].rearrange("p b n -> p (b n)")
        gin_mid_ps = [banks[:, u, :] for u in range(2)]
        gin_out_ps = [banks[:, 2 + u, 0:STRIP // P * D] for u in range(2)]
        twin_ps = banks[:, 7, 0:P]
        spread_ps = banks[:, 0:7, :].rearrange("p b n -> p (b n)")

        dst_landed, tops_landed, edges_landed, vec_landed, weights_landed = (
            sem(n) for n in ("dst_landed", "tops_landed", "edges_landed", "vec_landed", "weights_landed"))
        iota_done, ident_done, ones_done, pads_ready = (sem(n) for n in ("iota_done", "ident_done", "ones_done", "pads_ready"))
        tops_ready, tops_spread, sw_ready, sw_stored = (sem(n) for n in ("tops_ready", "tops_spread", "sw_ready", "sw_stored"))
        dst_copied, count_zeroed, order_in, order_made = (sem(n) for n in ("dst_copied", "count_zeroed", "order_in", "order_made"))
        order_known = {e: sem(f"order_known_{e}") for e in ("sp", "pool", "pe")}
        sort_free, edge_landed, key_ready_to_spread, key_spread = (
            sem(n) for n in ("sort_free", "edge_landed", "key_ready_to_spread", "key_spread"))
        count_wanted, count_got, counted, places_ready, placed = (
            sem(n) for n in ("count_wanted", "count_got", "counted", "places_ready", "placed"))
        counts_landed, starts_ready, starts_stored = (sem(n) for n in ("counts_landed", "starts_ready", "starts_stored"))
        tops_copied, tops_counted, keys_counted = sem("tops_copied"), sem("tops_counted"), sem("keys_counted")
        blk_ready, dst_gathered = sem("blk_ready"), sem("dst_gathered")
        rp_ready, rp_stored, rp1_landed = sem("rp_ready"), sem("rp_stored"), sem("rp1_landed")
        key_ready, key_stored, key_landed = sem("key_ready"), sem("key_stored"), sem("key_landed")
        rec_ready, recs_landed = sem("rec_ready"), sem("recs_landed")
        deg_ready, deg_maxed, x_gathered = (sem(n) for n in ("deg_ready", "deg_maxed", "x_gathered"))
        meta_sp, meta_pool = sem("meta_sp"), sem("meta_pool")
        pick_ready, pair_gathered = sem("pick_ready"), sem("pair_gathered")
        ell_ready, ell_stored, ell_free_new = sem("ell_ready"), sem("ell_stored"), sem("ell_free_new")
        pads_stored = sem("pads_stored")
        dve_chain, act_done, pool_chain = sem("dve_chain"), sem("act_done"), sem("pool_chain")
        ticks = {e: sem(f"ticks_{e}") for e in ("dve", "pool", "act")}
        ell_landed = [sem(f"ell_landed{u}") for u in range(RING)]
        ell_free = sem("ell_free")
        rows_free = sem("rows_free")
        rows_landed = [sem(f"rows_landed{u}") for u in range(RING)]
        msg_ready, tile_known = sem("msg_ready"), sem("tile_known")
        summed, sum_made = sem("summed"), sem("sum_made")
        res_made, res_copied = ([sem(f"{n}{u}") for u in range(2)] for n in ("res_made", "res_copied"))
        row_made = sem("row_made")
        means_kept, bn_in, bn_done, silu_in, silu_done = (sem(n) for n in ("means_kept", "bn_in", "bn_done", "silu_in", "silu_done"))
        row_ready = sem("row_ready")
        row_stored = [[sem(f"row_stored{u}_{b}") for b in range(PAIR)] for u in range(2)]
        x_staged = sem("x_staged")
        xT_made = sem("xT_made")
        mid_made = [sem(f"mid_made{u}") for u in range(PAIR)]
        mid_copied = [sem(f"mid_copied{u}") for u in range(PAIR)]
        A_made = sem("A_made")
        B_made = [sem(f"B_made{u}") for u in range(PAIR)]
        B_free = [sem(f"B_free{u}") for u in range(PAIR)]
        zeros_ready, zero_rows_ready, adj_zeroed, x_landed = (sem(n) for n in ("zeros_ready", "zero_rows_ready", "adj_zeroed", "x_landed"))
        post_ready, post_free, scattered, adj_built = sem("post_ready"), sem("post_free"), sem("scattered"), sem("adj_built")
        diag_ready, vec_spread, vec_copied = sem("diag_ready"), sem("vec_spread"), sem("vec_copied")
        adj_landed, adj_free = ([sem(f"{n}{u}") for u in range(2)] for n in ("adj_landed", "adj_free"))
        h_staged, h_free = ([sem(f"{n}{u}") for u in range(2)] for n in ("h_staged", "h_free"))
        agg_made, agg_copied = sem("agg_made"), [sem(f"agg_copied{u}") for u in range(2)]
        h_ready = sem("h_ready")
        x1_ready, x1_stored = sem("x1_ready"), sem("x1_stored")
        ht_made, ht_copied, x0_made, x0_added = (sem(n) for n in ("ht_made", "ht_copied", "x0_made", "x0_added"))
        sqrt_in, sqrt_done, exp_in, exp_done = (sem(n) for n in ("sqrt_in", "sqrt_done", "exp_in", "exp_done"))
        sin_in, sin_done = sem("sin_in"), sem("sin_done")
        gat_w_ready = sem("gat_w_ready")
        fin_ready, out_stored = sem("fin_ready"), sem("out_stored")
        PREP_STORES = [[len(range((PAIR * u + b) or 2 * PAIR, T, 2 * PAIR)) * 16 for b in range(PAIR)] for u in range(2)]
        LOOP_STORES = [len(range(u, STEPS, 2)) * 16 for u in range(2)]
        SCATTERED = 16
        GROUP = 16 * SLOTS

        block = ctx.enter_context(nc.Block())

        def in_steps(eng, body):
            with eng.Fori(0, STEPS // 2) as it:
                for u in range(2):
                    body(it * 2 + u, u, it)
            body(STEPS - 1, 0, STEPS // 2)

        def plane(ap):
            return ap.rearrange("p a f -> p (a f)")

        @block.sync
        def _(sp):
            by_part = dst_d.rearrange("(p e) -> p e", p=P)
            sp.dma_start(dst_all, by_part).then_inc(dst_landed, 16)
            sp.dma_start(dst_next[0:P - 1, :], by_part[1:P, 0:1], allow_slow_non_contiguous=True).then_inc(dst_landed, 16)
            def load_tops(dst):
                sp.dma_start(tops_i, dst.rearrange("(a b k) -> a b k", a=1, k=BLOCK)[:, :, 0], allow_slow_non_contiguous=True)\
                    .then_inc(tops_landed, 16)

            load_tops(dst_d)
            sp.dma_start(src_i, src_d.rearrange("(p e) -> p e", p=P)).then_inc(edges_landed, 16)
            sp.dma_start(w_f, w_d.rearrange("(p e) -> p e", p=P)).then_inc(edges_landed, 16)
            sp.dma_start(sdst_d, dst_d).then_inc(dst_copied, 16)
            sp.dma_start(vec[:, :], nv_d.rearrange("(p t) -> p t", p=P)).then_inc(vec_landed, 16)
            take(sp, sw_ready)
            sp.dma_start(sw_d[0:EP, :].rearrange("(p e) c -> p e c", p=P), sw).then_inc(sw_stored, 16)
            sp.dma_start(sw_d[EP:EP + 2 * BLOCK, :].rearrange("(a e) c -> a (e c)", a=1), zeros[:, :]).then_inc(sw_stored, 16)
            sp.dma_start(cnt_d.rearrange("(a n) c -> a (n c)", a=1), zero_rows[0:1, :]).then_inc(count_zeroed, 16)
            take(sp, order_known["sp"])
            sort_tiles = sp.value_load(sort_i[0:1, 0:1], min_val=0, max_val=SORT_TILES)

            def sort_loads():
                with sp.Fori(0, sort_tiles) as it:
                    take(sp, sort_free)
                    at = bass.ds(it * P, P)
                    one = lambda v: v[at].rearrange("(p a) -> p a", a=1)
                    sp.dma_start(edge_dst[:, :], one(dst_d)).then_inc(edge_landed, 16)
                    sp.dma_start(edge_src[:, :], one(src_d)).then_inc(edge_landed, 16)
                    sp.dma_start(edge_sw[:, 1:2], one(w_d)).then_inc(edge_landed, 16)

            with sp.If(sort_tiles > 0):
                sp.wait_ge(dst_copied, 16)
                sp.wait_ge(sw_stored, 32)
                sp.wait_ge(count_zeroed, 16)
                sort_loads()
                take(sp, sort_free)
                counts = cnt_d[0:NP, :].rearrange("(p t) c -> p (t c)", p=P)
                sp.dma_start(node_count[:, :], counts).then_inc(counts_landed, 16)
                take(sp, starts_ready)
                sp.dma_start(counts, node_start[:, :]).then_inc(starts_stored, 16)
                sp.dma_start(cnt_d[NP:NP + 1, :], e_end[:, :]).then_inc(starts_stored, 16)
                take(sp, starts_stored, 32)
                sp.sem_inc(sort_free, 1)
                sort_loads()
                take(sp, sort_free)
                load_tops(sdst_d)
            sp.dma_start(x_res[:, 0:TILES - 1, :], x_d[0:(TILES - 1) * P, :].rearrange("(t p) f -> p t f", p=P)).then_inc(x_landed, 16)
            take(sp, zeros_ready)
            sp.dma_start(x_res[0:LAST, TILES - 1, :], x_d[(TILES - 1) * P:N, :]).then_inc(x_landed, 16)
            take(sp, pads_ready)
            for l in range(3):
                sp.dma_start(gat_tab[l][PAD:PAD + 1, :], pad_row[l][:, :]).then_inc(pads_stored, 16)
            take(sp, rp_ready)
            sp.dma_start(rp_d[0:NP].rearrange("(p t) -> p t", p=P), rp[:, :]).then_inc(rp_stored, 16)
            sp.dma_start(rp_d[NP:NP + 1].rearrange("(a b) -> a b", a=1), e_end[:, :]).then_inc(rp_stored, 16)
            sp.wait_ge(rp_stored, 32)
            sp.dma_start(rp1[:, :], rp_d[1:NP + 1].rearrange("(p t) -> p t", p=P)).then_inc(rp1_landed, 16)
            take(sp, key_ready)
            sp.dma_start(key_d.rearrange("(p t) -> p t", p=P), key[:, :]).then_inc(key_stored, 16)
            sp.wait_ge(key_stored, 16)
            sp.dma_start(key_all, key_d.partition_broadcast(P)).then_inc(key_landed, 16)
            sp.wait_ge(scattered, 16)
            for u in range(2):
                for b in range(PAIR):
                    sp.wait_ge(row_stored[u][b], PREP_STORES[u][b])
            sp.dma_start(recs[:, :, :], rec_d.rearrange("(t p) c -> p t c", p=P)).then_inc(recs_landed, 16)
            take(sp, meta_sp)
            with sp.Fori(0, T) as t:
                blocks = sp.value_load(blocks_i[0:1, bass.ds(t, 1)], min_val=1, max_val=BLOCKS + 1)
                start = sp.value_load(start_i[0:1, bass.ds(t, 1)], min_val=0, max_val=CHUNKS - PER_BLOCK)
                with sp.Fori(0, blocks) as s:
                    take(sp, ell_ready)
                    row = nc.s_assert_within(start + s * PER_BLOCK, 0, CHUNKS - PER_BLOCK,
                                             skip_runtime_bounds_check_because="CHUNKS has room for every tile's last block")
                    sp.dma_start(ell_d[bass.ds(row, PER_BLOCK), :, :].rearrange("k p c -> p k c"),
                                 ell_new[:, :, :]).then_inc(ell_stored, 16)
                    take(sp, ell_stored, 16)
                    sp.sem_inc(ell_free_new, 1)
            take(sp, adj_built)

            def load_adj(u, at):
                take(sp, adj_free[u])
                sp.dma_start(adj_buf[u], adj_t[bass.ds(at * (2 * P), 2 * P), :].rearrange("(b p) n -> p b n", p=P)).then_inc(adj_landed[u], 16)

            for l in range(3):
                load_adj(l % 2, 0)
                with sp.Fori(0, DOUBLES // 2 - 1) as it:
                    load_adj(1 - l % 2, it * 2 + 1)
                    load_adj(l % 2, it * 2 + 2)
                load_adj(1 - l % 2, DOUBLES - 1)
                take(sp, adj_free[l % 2])
                sp.dma_start(adj_buf[l % 2][:, 0, :], adj_t[NA - P:NA, :]).then_inc(adj_landed[l % 2], 16)
            take(sp, x1_ready)
            sp.dma_start(x1_d.rearrange("(t p) f -> p t f", p=P), x_res[:, :, :]).then_inc(x1_stored, 16)
            rounds = sp.value_load(meta[0:1, 0:1], min_val=1, max_val=CHUNKS // RING)
            for layer in range(3):
                with sp.Fori(0, rounds) as it:
                    for u in range(RING):
                        take(sp, ell_free)
                        sp.dma_start(ell[u][:, :], ell_d[bass.ds(it * RING + u, 1), :, :].rearrange("k p c -> (k p) c"))\
                          .then_inc(ell_landed[u], 16)

        @block.gpsimd
        def _(pool):
            g = nc.gpsimd
            chain = Chain(pool, pool_chain)

            def gather(dst, table, idx):
                return g.indirect_dma_start(out=dst, out_offset=None, in_=table,
                                            in_offset=bass.IndirectOffsetOnAxis(ap=idx, axis=0))

            def scatter(table, idx, data):
                return g.indirect_dma_start(out=table, out_offset=bass.IndirectOffsetOnAxis(ap=idx, axis=0),
                                            in_=data, in_offset=None)

            def add(table, idx, data):
                return g.indirect_dma_start(out=table, out_offset=bass.IndirectOffsetOnAxis(ap=idx, axis=0),
                                            in_=data, in_offset=None, compute_op=ALU.add)

            g.iota(id_i[:, :], pattern=[[1, T]], base=0, channel_multiplier=T).then_inc(iota_done, 1)
            g.iota(slot_i[:, :], pattern=[[1, BLOCK]], base=0, channel_multiplier=0).then_inc(iota_done, 1)
            chain(g.memset(ident[:, :], 0.0))
            g.affine_select(out=ident[:, :], in_=ident[:, :], compare_op=ALU.not_equal, fill=1.0, base=0,
                            pattern=[[-1, P]], channel_multiplier=1).then_inc(ident_done, 1)
            chain(g.memset(later[:, :], 1.0))
            chain(g.affine_select(out=later[:, :], in_=later[:, :], compare_op=ALU.is_gt, fill=0.0, base=0,
                                  pattern=[[1, P]], channel_multiplier=-1))
            g.iota(spare_i[:, :], pattern=[[1, 1]], base=NP + 1, channel_multiplier=1).then_inc(iota_done, 1)
            take(pool, order_in)
            g.partition_all_reduce(unsorted[:, :], unsorted[:, :], P, R_MAX).then_inc(order_made, 1)
            take(pool, order_known["pool"])
            sort_tiles = pool.value_load(sort_i[0:1, 0:1], min_val=0, max_val=SORT_TILES)

            def sort_scatters(turns_before, placing):
                with pool.Fori(0, sort_tiles) as it:
                    take(pool, count_wanted)
                    gather(place[:, :], cnt_d, count_i[:, 0:1]).then_inc(count_got, 16)
                    take(pool, places_ready)
                    scatter(cnt_d, count_to[:, 0:1], next_place[:, :]).then_inc(counted, 16)
                    if placing:
                        scatter(sw_d, place_i[:, 0:1], edge_sw[:, :]).then_inc(placed, 16)
                        scatter(sdst_d.rearrange("(e a) -> e a", a=1), place_i[:, 0:1], edge_dst[:, :]).then_inc(placed, 16)
                        pool.wait_ge(placed, (it + 1) * 32)
                    pool.wait_ge(counted, (it + turns_before + 1) * 16)
                    pool.sem_inc(ticks["pool"], 1)
                    pool.sem_inc(sort_free, 1)

            with pool.If(sort_tiles > 0):
                sort_scatters(0, False)
                sort_scatters(sort_tiles, True)
            pool.wait_ge(dst_copied, 16)
            take(pool, blk_ready)
            for t in range(T):
                gather(dst_i[:, t, :], sdst_d.rearrange("(b k) -> b k", k=BLOCK), blk_i[:, t:t + 1]).then_inc(dst_gathered, 16)
            take(pool, rec_ready)
            for t in range(T):
                scatter(rec_d, rank_i[:, t:t + 1], rec[:, t, :]).then_inc(row_stored[t // PAIR % 2][t % PAIR] if t else scattered, 16)
            take(pool, deg_ready)
            g.partition_all_reduce(deg_max[:, :], recs[:, :, 1], P, R_MAX).then_inc(deg_maxed, 1)
            take(pool, meta_pool)
            pool.wait_ge(sw_stored, 32)
            sw_blocks = sw_d.rearrange("(b k) c -> b (k c)", k=BLOCK)
            adj_cells = adj_t.rearrange("s (n a) -> (s n) a", a=1)

            def pick_blocks():
                take(pool, pick_ready)
                for j in range(2):
                    gather(pair[:, j, :], sw_blocks, pick_i[:, j:j + 1]).then_inc(pair_gathered, 16)

            def send_block(send, chunks_left):
                for j in range(PER_BLOCK):
                    with pool.If(chunks_left > j):
                        for r in range(j * SLOTS, (j + 1) * SLOTS):
                            send(adj_cells, post_i[:, r:r + 1], post_w[:, r:r + 1]).then_inc(scattered, 16)

            pick_blocks()
            pool.wait_ge(adj_zeroed, 16 * ZERO_FILLS)
            with pool.Fori(0, T) as t:
                blocks = pool.value_load(blocks_i[0:1, bass.ds(t, 1)], min_val=1, max_val=BLOCKS + 1)
                start = pool.value_load(start_i[0:1, bass.ds(t, 1)], min_val=0, max_val=CHUNKS - PER_BLOCK)
                chunks = pool.value_load(chunks_i[0:1, bass.ds(t, 1)], min_val=0, max_val=CHUNKS)
                with pool.Fori(0, blocks) as s:
                    pick_blocks()
                    pool.wait_ge(scattered, (start + s * PER_BLOCK) * GROUP + SCATTERED)
                    pool.sem_inc(ticks["pool"], 1)
                    pool.sem_inc(post_free, 1)
                    take(pool, post_ready)
                    with pool.If(s < 1):
                        send_block(scatter, chunks - s * PER_BLOCK)
                    with pool.If(s > 0):
                        send_block(add, chunks - s * PER_BLOCK)
            chunks = pool.value_load(meta[0:1, 1:2], min_val=0, max_val=CHUNKS)
            pool.wait_ge(scattered, chunks * GROUP + SCATTERED)
            pool.sem_inc(adj_built, 1)
            rounds = pool.value_load(meta[0:1, 0:1], min_val=1, max_val=CHUNKS // RING)
            pool.wait_ge(pads_stored, 3 * 16)

            def chunk_gathers(layer, table, width):
                with pool.Fori(0, rounds) as it:
                    for u in range(RING):
                        take(pool, ell_landed[u], 16)
                        pool.sem_inc(tile_known, 1)
                        take(pool, rows_free)
                        for r in range(SLOTS):
                            gather(rows[u][:, r * width:(r + 1) * width], table, ell[u][:, r:r + 1])\
                                .then_inc(rows_landed[u], 16)

            def store_rows(table, width):
                def store(step, u, turn):
                    for b in range(PAIR):
                        take(pool, row_ready)
                        scatter(table, row_node[u][:, b:b + 1], row_st[u][:, b, 0:width]).then_inc(row_stored[u][b], 16)

                in_steps(pool, store)

            def rows_all_stored(loops):
                for u in range(2):
                    for b in range(PAIR):
                        pool.wait_ge(row_stored[u][b], PREP_STORES[u][b] + LOOP_STORES[u] * loops)

            pool.wait_ge(x1_stored, 16)
            for t in range(T):
                gather(x_res[:, t, :], x1_d, node_i[:, t:t + 1]).then_inc(x_gathered, 16)
            for l in range(3):
                store_rows(gat_tab[l], gat_row[l])
                rows_all_stored(1 + l)
                chunk_gathers(l, gat_tab[l], gat_row[l])
            for t in range(TILES):
                take(pool, fin_ready)
                n = P if t < TILES - 1 else LAST
                scatter(out, node_i[0:n, t:t + 1], x_res[0:n, t, :]).then_inc(out_stored, 16)
            pool.wait_ge(out_stored, 16 * TILES)

        @block.scalar
        def _(act):
            s = nc.scalar
            act_chain = Chain(act, act_done)
            act.wait_ge(zero_rows_ready, 1)
            def zero_adj(fills):
                for n in fills:
                    high = min((n + 1) * P, NA + BLOCK)
                    act.dma_start(adj_t[n * P:high, :], zero_rows[0:high - n * P, 0:NA]).then_inc(adj_zeroed, 16)

            act.wait_ge(edges_landed, 32)
            zero_adj(range(ZERO_FIRST))
            take(act, tops_spread)
            s.activation(tops_all, tops_ps[:, 0:BLOCKS], ACT.Copy).then_inc(tops_copied, 1)
            act.wait_ge(tops_copied, 1)
            for tile in range(DVE_TILES, T):
                act_chain(s.activation(tops_junk, tops_all, ACT.Sign, scale=-1.0, bias=id_half[:, tile:tile + 1], accum_out=cnt_a[:, tile:tile + 1]))
            act.sem_inc(tops_counted, 1)
            act.wait_ge(key_landed, 16)
            act.wait_ge(sw_stored, 32)
            zero_adj(range(ZERO_FIRST, ZERO_FILLS))
            for tile in range(DVE_TILES, T):
                act_chain(s.activation(junk_a, key_all, ACT.Sign, bias=key_neg[:, tile:tile + 1], accum_out=rank_a[:, tile:tile + 1]))
            act.sem_inc(keys_counted, 1)

            def load(dst, src):
                act.dma_start(dst, src).then_inc(weights_landed, 16)

            column = lambda v: v.rearrange("(d a) -> d a", a=1)
            load(freqs[:, :], column(freq_d))
            for l, (i1, i2) in enumerate((("11", "12"), ("21", "22"), ("31", "32"))):
                load(w1[l][:, :], a[f"L0_gnn_w{i1}"])
                load(w2[l][:, :], a[f"L0_gnn_w{i2}"])
                load(b1[l][:, :], column(a[f"L0_gnn_b{i1}"]))
                load(b2[l][:, :], a[f"L0_gnn_b{i2}"].partition_broadcast(P))
            load(te_w1[:, :], a["L1_gnn_te_w1"])
            load(te_w2[:, :], a["L1_gnn_te_w2"])
            load(te_b1[:, :], column(a["L1_gnn_te_b1"]))
            load(te_b2[:, :], column(a["L1_gnn_te_b2"]))
            load(init_w[:, :], a["L1_gnn_init_w"])
            load(init_b[:, :], column(a["L1_gnn_init_b"]))
            for l in range(3):
                for j in range(kin[l]):
                    load(gat_w[l][:, j, 0:gat_row[l]].rearrange("p (h q) -> p h q", h=HEADS)[:, :, 0:head[l]],
                         a[f"L1_gnn_gat_w{l}"][j * P:(j + 1) * P, :].rearrange("p (h c) -> p h c", h=HEADS))
                load(adj_w[l][:, :, :], a[f"L1_gnn_adj_w{l}"].rearrange("(k p) n -> p k n", p=P))
                load(att[l][:, 0, :], a[f"L1_gnn_att_src{l}"].rearrange("h c -> (h c)").partition_broadcast(P))
                load(att[l][:, 1, :], a[f"L1_gnn_att_dst{l}"].rearrange("h c -> (h c)").partition_broadcast(P))
                for t, name in ((gat_b, "gat_b"), (adj_b, "adj_b"), (bn_g, "bn_g"), (bn_b, "bn_b")):
                    for j in range(kout[l]):
                        load(t[l][:, j:j + 1], column(a[f"L1_gnn_{name}{l}"][j * P:(j + 1) * P]))
            load(out_w[:, :], a["L1_gnn_out_w"])
            load(out_b[:, :], a["L1_gnn_out_b"].partition_broadcast(P))
            act.wait_ge(weights_landed, 16 * WEIGHTS)

            def sqrt(n, wide):
                take(act, sqrt_in)
                s.activation(rtmp[:, 0:wide] if n else ln_c[:, :], var[:, 0:wide] if n else ln_b[:, :],
                             ACT.Sqrt).then_inc(sqrt_done, 1)

            take(act, vec_spread)
            s.activation(arg, spread_ps[:, 0:NP], ACT.Copy).then_inc(vec_copied, 1)
            sqrt(0, 0)
            for l in range(3):
                m = GIN_MID[l]
                take(act, h_ready)

                def stage_h(u, at):
                    take(act, h_free[u])
                    s.activation(h_st[u][:, :, :], h_in[:, bass.ds(at * 2, 2), :], ACT.Copy).then_inc(h_staged[u], 1)

                stage_h(l % 2, 0)
                with act.Fori(0, DOUBLES // 2 - 1) as it:
                    stage_h(1 - l % 2, it * 2 + 1)
                    stage_h(l % 2, it * 2 + 2)
                stage_h(1 - l % 2, DOUBLES - 1)
                take(act, h_free[l % 2])
                s.activation(h_st[l % 2][:, 0, :], h_in[:, TILES - 1, :], ACT.Copy).then_inc(h_staged[l % 2], 1)
                if l == 0:
                    take(act, sin_in)
                    s.activation(emb_in, arg, ACT.Sin).then_inc(sin_done, 1)
                for u in range(2):
                    take(act, h_free[u])
                    act.sem_inc(h_free[u], 1)
                act.sem_inc(adj_free[l % 2], 1)
                act.sem_inc(agg_made, 1)
                for n, width in NODE_STRIPS[0::2]:
                    s.activation(agg_sb[:, n:n + width], agg_ps[:, n:n + width], ACT.Copy).then_inc(agg_copied[0], 1)
                for i, (n, width) in enumerate(NODE_STRIPS):
                    take(act, mid_made[i % 2])
                    s.activation(gin_mid[i % 2][0:m, 0:width], gin_mid_ps[i % 2][0:m, 0:width], ACT.Relu, bias=b1[l][:, 0:1])                        .then_inc(mid_copied[i % 2], 1)
                if l == 2:
                    def keep_emb(i):
                        n, width = STRIPS[i]
                        take(act, B_made[i % 2])
                        s.activation(emb[:, n:n + width], banks[:, 2 + i % 2, 0:width], ACT.Identity, bias=te_b2[:, 0:1]).then_inc(B_free[i % 2], 1)

                    for i, (n, width) in enumerate(STRIPS):
                        take(act, mid_made[i % 2])
                        s.activation(emb_mid[:, n:n + width], banks[:, i % 2, 0:width], ACT.Silu, bias=te_b1[:, 0:1]).then_inc(mid_copied[i % 2], 1)
                        if i:
                            keep_emb(i - 1)
                    keep_emb(i)
            sqrt(0, 0)
            for i, (n, width) in enumerate(STRIPS):
                take(act, ht_made)
                s.activation(h_t[:, n:n + width], banks[0:D, i % 2, 0:width], ACT.Copy).then_inc(ht_copied, 1)
            strip = 0
            for l in range(3):
                width, c = gat_row[l], head[l]

                def keep_rows(step, u, turn):
                    take(act, A_made)
                    for b in range(PAIR):
                        act.wait_ge(row_stored[u][b], turn * 16 + (LOOP_STORES[u] * l + PREP_STORES[u][b]))
                        act.sem_inc(ticks["act"], 1)
                        s.activation(row_st[u][:, b, 0:width + HEADS], A_ps[u][b][:, 0:width + HEADS], ACT.Copy).then_inc(row_made, 1)
                        s.activation(row_node[u][:, b:b + 1], recs[:, bass.ds(step * PAIR + b, 1), 2], ACT.Copy).then_inc(row_ready, 1)

                in_steps(act, keep_rows)
                for f in range(kout[l]):
                    for n, w in STRIPS:
                        u = strip % 2
                        take(act, res_made[u])
                        s.activation(y_t[:, f, n:n + w], T_ps[u][:, 0:w], ACT.Identity, bias=gat_b[l][:, f:f + 1]).then_inc(res_copied[u], 1)
                        strip += 1
                rounds = act.value_load(meta[0:1, 0:1], min_val=1, max_val=CHUNKS // RING)
                with act.Fori(0, rounds) as it:
                    for u in range(RING):
                        take(act, exp_in)
                        s.activation(shrink[u][:, :], ex_in[:, SLOTS, :], ACT.Exp)
                        s.activation(rows[u][:, 0:SLOTS * width].rearrange("p (r h q) -> p r h q", h=HEADS, q=c + 1)[:, :, :, c],
                                     ex_in[:, 0:SLOTS, :], ACT.Exp).then_inc(exp_done, 1)
                def keep_means(step, u, turn):
                    take(act, xT_made)
                    for f in range(kout[l]):
                        made, col = T_ps[u][:, f * PAIR * P:(f + 1) * PAIR * P], bass.ds(step, 1)
                        if isinstance(step, int):
                            real = N - step * PAIR * P
                            s.activation(y_t[:, f, N:NP], made[:, real:], ACT.Copy)
                            last = s.activation(y_t[:, f, N - real:N], made[:, 0:real], ACT.Copy, accum_out=bn_parts[:, f, col])
                        else:
                            last = s.activation(y_t[:, f, bass.ds(step * (PAIR * P), PAIR * P)], made, ACT.Copy, accum_out=bn_parts[:, f, col])
                    last.then_inc(means_kept, 1)

                in_steps(act, keep_means)
                junk_t = [af[:, f * N:(f + 1) * N] for f in range(kout[l])]
                take(act, bn_in)
                for f in range(kout[l]):
                    last = s.activation(junk_t[f], y_t[:, f, 0:N], ACT.Square, bias=mean[:, f:f + 1], accum_out=bn_sq[:, f:f + 1])
                last.then_inc(bn_done, 1)
                sqrt(1, kout[l])
                take(act, silu_in)
                for low, high in SILU_STEPS:
                    n = slice(low * PAIR * P, high * PAIR * P)
                    for f in range(kout[l]):
                        last = s.activation(x_t[:, f, n], y_t[:, f, n], ACT.Silu, bias=shift[:, f:f + 1], scale=scale[:, f:f + 1])
                    last.then_inc(silu_done, high - low)

        @block.tensor
        def _(pe):
            t = nc.tensor
            take(pe, ones_done)
            pe.wait_ge(ident_done, 1)
            take(pe, order_known["pe"])
            sort_tiles = pe.value_load(sort_i[0:1, 0:1], min_val=0, max_val=SORT_TILES)

            def sort_spreads():
                with pe.Fori(0, sort_tiles):
                    take(pe, key_ready_to_spread)
                    t.transpose(twin_ps, key_wide[:, :], ident[:, :]).then_inc(key_spread, 1)

            with pe.If(sort_tiles > 0):
                sort_spreads()
                take(pe, key_ready_to_spread)
                t.matmul(twin_ps[:, 0:1], later[:, :], node_sum[:, :], start=True, stop=True).then_inc(key_spread, 1)
                sort_spreads()
            take(pe, tops_ready)
            for n in range(0, BLOCKS, 512):
                m = min(512, BLOCKS - n)
                last = t.matmul(tops_ps[:, n:n + m], ones[0:1, :], tops_f[:, n:n + m], start=True, stop=True)
            last.then_inc(tops_spread, 1)
            pe.wait_ge(weights_landed, 16 * WEIGHTS)

            take(pe, diag_ready)
            for tile in range(T):
                last = t.matmul(spread_ps[:, tile * P:(tile + 1) * P], ones[:, :], turn[:, tile * P:(tile + 1) * P], start=True, stop=True)
            last.then_inc(vec_spread, 1)
            pe.wait_ge(vec_copied, 1)
            for l in range(3):
                m = GIN_MID[l]

                def own(u, at, b):
                    return t.matmul(agg_ps[:, bass.ds((at * 2 + b) * P, P)], h_st[u][:, b, :], ident[:, :], start=False, stop=False)

                def neighbours(u, b, first=False, last=False):
                    for n, width in NODE_STRIPS:
                        ins = t.matmul(agg_ps[:, n:n + width], h_st[u][:, b, :], adj_buf[u][:, b, n:n + width], start=first, stop=last)
                    return ins

                def aggregate(u, at, first=False):
                    take(pe, h_staged[u])
                    take(pe, adj_landed[u], 16)
                    neighbours(u, 0, first=first)
                    neighbours(u, 1).then_inc(adj_free[u], 1)
                    own(u, at, 0)
                    own(u, at, 1).then_inc(h_free[u], 1)

                aggregate(l % 2, 0, first=True)
                with pe.Fori(0, DOUBLES // 2 - 1) as it:
                    aggregate(1 - l % 2, it * 2 + 1)
                    aggregate(l % 2, it * 2 + 2)
                aggregate(1 - l % 2, DOUBLES - 1)
                u = l % 2
                take(pe, h_staged[u])
                take(pe, adj_landed[u], 16)
                own(u, DOUBLES, 0)
                neighbours(u, 0, last=True).then_inc(h_free[u], 1)
                for u in range(2):
                    take(pe, agg_copied[u], len(NODE_STRIPS[u::2]))

                def gin_out(i, width):
                    take(pe, mid_copied[i % 2])
                    take(pe, B_free[i % 2])
                    for k in range(width // P):
                        ins = t.matmul(gin_out_ps[i % 2][:, k * D:(k + 1) * D], gin_mid[i % 2][0:m, k * P:(k + 1) * P], w2[l][:, :],
                                       start=True, stop=True)
                    ins.then_inc(B_made[i % 2], 1)

                for i, (n, width) in enumerate(NODE_STRIPS):
                    t.matmul(gin_mid_ps[i % 2][0:m, 0:width], w1[l][:, :], agg_sb[:, n:n + width], start=True, stop=True)                        .then_inc(mid_made[i % 2], 1)
                    if i:
                        gin_out(i - 1, STRIP)
                gin_out(i, width)
                for u in range(2):
                    take(pe, B_free[u])
                    pe.sem_inc(B_free[u], 1)
                if l == 2:
                    take(pe, sin_done)

                    def emb_out(i):
                        n, width = STRIPS[i]
                        take(pe, mid_copied[i % 2])
                        take(pe, B_free[i % 2])
                        t.matmul(banks[:, 2 + i % 2, 0:width], te_w2[:, :], emb_mid[:, n:n + width], start=True, stop=True).then_inc(B_made[i % 2], 1)

                    for i, (n, width) in enumerate(STRIPS):
                        t.matmul(banks[:, i % 2, 0:width], te_w1[:, :], emb_in[:, n:n + width], start=True, stop=True).then_inc(mid_made[i % 2], 1)
                        if i:
                            emb_out(i - 1)
                    emb_out(i)
                    for u in range(2):
                        take(pe, B_free[u])
                        pe.sem_inc(B_free[u], 1)
            take(pe, h_ready)
            for i, (n, width) in enumerate(STRIPS):
                if i >= 2:
                    pe.wait_ge(ht_copied, i - 1)
                for k in range(0, width, P):
                    last = t.transpose(banks[0:D, i % 2, k:k + P], h_in[:, (n + k) // P, :], ident[:, :])
                last.then_inc(ht_made, 1)
            for i, (n, width) in enumerate(STRIPS):
                pe.wait_ge(ht_copied, i + 1)
                if i >= 2:
                    pe.wait_ge(x0_added, i - 1)
                t.matmul(banks[:, 2 + i % 2, 0:width], init_w[:, :], h_t[:, n:n + width], start=True, stop=True).then_inc(x0_made, 1)

            take(pe, gat_w_ready)
            strip = 0
            for l in range(3):
                width = gat_row[l]
                def rows_of(step, u, turn):
                    take(pe, x_staged)
                    for b in range(PAIR):
                        for j in range(kin[l]):
                            last = t.matmul(A_ps[u][b][:, 0:width + HEADS], x_st[u][:, (j * PAIR + b) * P:(j * PAIR + b + 1) * P], gat_w[l][:, j, :],
                                            start=(j == 0), stop=(j == kin[l] - 1))
                    last.then_inc(A_made, 1)

                in_steps(pe, rows_of)
                for f in range(kout[l]):
                    for n, w in STRIPS:
                        u = strip % 2
                        if strip >= 2:
                            take(pe, res_copied[u])
                        for j in range(kin[l]):
                            last = t.matmul(T_ps[u][:, 0:w], adj_w[l][:, j, f * P:(f + 1) * P], x_t[:, j, n:n + w],
                                            start=(j == 0), stop=(j == kin[l] - 1))
                        last.then_inc(res_made[u], 1)
                        strip += 1
                for u in range(RING - LAG, RING):
                    t.matmul(sum_ps[u % SUMS][:, 0:width], ident[:, :], no_sums[:, 0:width], start=True, stop=True).then_inc(sum_made, 1)
                rounds = pe.value_load(meta[0:1, 0:1], min_val=1, max_val=CHUNKS // RING)
                with pe.Fori(0, rounds) as it:
                    for u in range(RING):
                        take(pe, msg_ready)
                        for r in range(SLOTS):
                            last = t.matmul(sum_ps[u % SUMS][:, 0:width], ident[:, :], rows[u][:, r * width:(r + 1) * width],
                                            start=(r == 0), stop=(r == SLOTS - 1))
                        last.then_inc(summed, 1)
                        take(pe, summed)
                        pe.sem_inc(sum_made, 1)
                        pe.sem_inc(rows_free, 1)
                def turn_means(step, u, turn):
                    take(pe, x_staged)
                    for b in range(PAIR):
                        for f in range(kout[l]):
                            to = T_ps[u][:, (f * PAIR + b) * P:(f * PAIR + b + 1) * P]
                            t.matmul(to, x_st[u][:, (b * kout[l] + f) * P:(b * kout[l] + f + 1) * P], ident[:, :], start=True, stop=False)
                            last = t.matmul(to, ident[:, :], y_t[:, f, bass.ds((step * PAIR + b) * P, P)], start=False, stop=True)
                    last.then_inc(xT_made, 1)

                in_steps(pe, turn_means)
            def out_rows(step, u, turn):
                take(pe, x_staged)
                for b in range(PAIR):
                    last = t.matmul(A_ps[u][0][:, b * D:(b + 1) * D], x_st[u][:, b * P:(b + 1) * P], out_w[:, :], start=True, stop=True)
                last.then_inc(A_made, 1)

            in_steps(pe, out_rows)

        @block.vector
        def _(dve):
            v = nc.vector
            link = Chain(dve, dve_chain)

            def signal(sm, n=1):
                dve.sem_inc(sm, n)

            for u in range(RING):
                signal(ell_free)
                signal(rows_free)
            for u in range(PAIR):
                signal(B_free[u])
            for u in range(2):
                signal(adj_free[u])
                signal(h_free[u])
            signal(ell_free_new)
            link(v.memset(zero_rows, 0.0))
            signal(zero_rows_ready)
            v.memset(zeros[:, :], 0.0)
            v.memset(zero_t[:, :], 0.0)
            v.memset(e_end[:, :], float(E))
            link(v.memset(ones[:, :], 1.0))
            signal(ones_done)
            dve.wait_ge(dst_landed, 32)
            v.tensor_tensor(falls[:, 0:EC - 1], dst_all[:, 0:EC - 1], dst_all[:, 1:EC], ALU.is_gt)
            link(v.tensor_tensor(falls[0:P - 1, EC - 1:EC], dst_all[0:P - 1, EC - 1:EC], dst_next[0:P - 1, :], ALU.is_gt))
            link(v.tensor_reduce(unsorted[:, :], falls[:, 0:EC - 1], AX.X, ALU.max))
            link(v.tensor_tensor(unsorted[0:P - 1, :], unsorted[0:P - 1, :], falls[0:P - 1, EC - 1:EC], ALU.max))
            signal(order_in)
            take(dve, iota_done, 3)
            v.tensor_copy(id_f[:, :], id_i[:, :])
            v.tensor_copy(spare_f[:, :], spare_i[:, :])
            v.tensor_copy(slot_f[:, :], slot_i[:, :])
            dve.wait_ge(tops_landed, 16)
            link(v.tensor_copy(tops_f, tops_i))
            link(v.tensor_scalar(id_half[:, :], id_f[:, :], -0.5, None, ALU.add))
            dve.wait_ge(edges_landed, 32)
            v.tensor_copy(sw[:, :, 0], src_i)
            link(v.tensor_copy(sw[:, :, 1], w_f))
            signal(sw_ready)
            take(dve, order_made)
            link(v.tensor_scalar(sort_n[:, :], unsorted[:, :], float(SORT_TILES), None, ALU.mult))
            link(v.tensor_copy(sort_i[:, :], sort_n[:, :]))
            signal(sort_free)
            for e in order_known.values():
                signal(e)
            sort_tiles = dve.value_load(sort_i[0:1, 0:1], min_val=0, max_val=SORT_TILES)
            link.reset()

            def sort_places(turns_before):
                with dve.Fori(0, sort_tiles) as it:
                    take(dve, edge_landed, 48)
                    v.tensor_copy(edge_sw[:, 0:1], edge_src[:, :])
                    link(v.tensor_copy(edge_key[:, :], edge_dst[:, :]))
                    link(v.tensor_scalar(edge_key[:, :], edge_key[:, :], float(NP), None, ALU.min))
                    v.tensor_copy(key_wide[:, :], edge_key[:, 0:1].to_broadcast([P, P]))
                    link(v.tensor_copy(count_i[:, :], edge_key[:, :]))
                    signal(count_wanted)
                    signal(key_ready_to_spread)
                    take(dve, key_spread)
                    link(v.tensor_scalar(key_same[:, :], twin_ps, edge_key[:, 0:1], None, ALU.is_equal))
                    link(v.tensor_reduce(twins[:, :], key_same[:, :], AX.X, ALU.add))
                    link(v.tensor_tensor(key_same[:, :], key_same[:, :], later[:, :], ALU.mult))
                    link(v.tensor_reduce(later_twins[:, :], key_same[:, :], AX.X, ALU.add))
                    v.tensor_scalar(spare[:, :], later_twins[:, :], 0.0, None, ALU.is_gt)
                    link(v.tensor_tensor(next_place[:, :], spare_f[:, :], edge_key[:, :], ALU.subtract))
                    link(v.scalar_tensor_tensor(spare[:, :], next_place[:, :], spare[:, 0:1], edge_key[:, :], ALU.mult, ALU.add))
                    link(v.tensor_copy(count_to[:, :], spare[:, :]))
                    dve.wait_ge(count_got, (it + turns_before + 1) * 16)
                    signal(ticks["dve"])
                    link(v.tensor_tensor(next_place[:, :], place[:, :], twins[:, :], ALU.add))
                    link(v.tensor_tensor(place[:, :], next_place[:, :], later_twins[:, :], ALU.subtract))
                    link(v.tensor_scalar(place[:, :], place[:, :], -1.0, None, ALU.add))
                    link(v.tensor_copy(place_i[:, :], place[:, :]))
                    signal(places_ready)
                    link.reset()

            with dve.If(sort_tiles > 0):
                sort_places(0)
                take(dve, counts_landed, 16)
                link(v.tensor_tensor_scan(node_scan[:, :], zero_t[:, :], node_count[:, :], 0.0, ALU.add, ALU.add))
                link(v.tensor_copy(node_sum[:, :], node_scan[:, T - 1:T]))
                signal(key_ready_to_spread)
                link(v.tensor_tensor(node_scan[:, :], node_scan[:, :], node_count[:, :], ALU.subtract))
                take(dve, key_spread)
                link(v.tensor_scalar(node_start[:, :], node_scan[:, :], twin_ps[:, 0:1], None, ALU.add))
                signal(starts_ready)
                link.reset()
                sort_places(sort_tiles)
                dve.wait_ge(tops_landed, 32)
                link(v.tensor_copy(tops_f, tops_i))
                link.reset()
            signal(tops_ready)
            v.memset(no_sums[:, :], 0.0)
            link(v.memset(x_res[:, TILES - 1:, :], 0.0))
            signal(zeros_ready)
            for l in range(3):
                link(v.memset(pad_row[l][:, :], 0.0))
                link(v.memset(pad_row[l][:, :].rearrange("p (h q) -> p h q", h=HEADS)[:, :, head[l]], NEG))
            signal(pads_ready)
            v.memset(quarter[:, :], 0.0)
            link(v.memset(half_pi[:, :], 0.0))
            v.memset(quarter[HALF:, :], 0.25)
            v.memset(half_pi[HALF:, :], np.pi / 2)
            v.tensor_scalar(dump[:, :], slot_f[:, :], float(NA), None, ALU.add)
            link(v.tensor_tensor(before[:, :, :], slot_f[:, :].unsqueeze(1).to_broadcast([P, BLOCK, BLOCK]),
                                 slot_f[:, :].unsqueeze(2).to_broadcast([P, BLOCK, BLOCK]), ALU.is_lt))
            dve.wait_ge(tops_copied, 1)
            for t in range(DVE_TILES):
                link(v.tensor_scalar(junk[:, 0:BLOCKS], tops_all, id_f[:, t:t + 1], None, ALU.is_lt, ALU.add,
                                     accum_out=cnt[:, t:t + 1]))
            take(dve, tops_counted)
            link(v.tensor_scalar(cnt[:, DVE_TILES:], cnt_a[:, DVE_TILES:], float(BLOCKS), 0.5, ALU.add, ALU.mult))
            link(v.tensor_scalar(blk[:, :], cnt[:, :], -1.0, 0.0, ALU.add, ALU.max))
            link(v.tensor_copy(blk_i[:, :], blk[:, :]))
            signal(blk_ready)
            dve.wait_ge(dst_gathered, 16 * T)
            link(v.tensor_copy(dst_f, dst_i))
            link(v.tensor_tensor(below, dst_f, id_f[:, :].unsqueeze(2).to_broadcast([P, T, BLOCK]), ALU.is_lt))
            link(v.tensor_reduce(cnt[:, :], below, AX.X, ALU.add))
            link(v.scalar_tensor_tensor(rp[:, :], blk[:, :], float(BLOCK), cnt[:, :], ALU.mult, ALU.add))
            signal(rp_ready)
            dve.wait_ge(rp1_landed, 16)
            v.tensor_copy(rec[:, :, 0], rp[:, :])
            v.tensor_copy(rec[:, :, 2], id_f[:, :])
            link(v.tensor_tensor(rec[:, :, 1], rp1[:, :], rp[:, :], ALU.subtract))
            link(v.tensor_scalar(key[:, :], rec[:, :, 1], 4095.0, 4096.0, ALU.min, ALU.mult))
            link(v.tensor_tensor(key[:, :], key[:, :], id_f[:, :], ALU.subtract))
            link(v.tensor_scalar(key[:, :], key[:, :], 4095.0, None, ALU.add))
            link(v.tensor_scalar(key_neg[:, :], key[:, :], -1.0, None, ALU.mult))
            signal(key_ready)
            dve.wait_ge(key_landed, 16)
            for t in range(DVE_TILES):
                link(v.tensor_scalar(junk, key_all, key[:, t:t + 1], None, ALU.is_gt, ALU.add, accum_out=rank[:, t:t + 1]))
            take(dve, keys_counted)
            link(v.tensor_scalar(rank[:, DVE_TILES:], rank_a[:, DVE_TILES:], float(NP - 1), 0.5, ALU.add, ALU.mult))
            dve.wait_ge(vec_landed, 16)
            v.tensor_copy(rec[:, :, 3], vec[:, :])
            link(v.tensor_copy(rank_i[:, :], rank[:, :]))
            signal(rec_ready)
            dve.wait_ge(recs_landed, 16)
            signal(deg_ready)
            link(v.tensor_copy(node_i[:, :], recs[:, :, 2]))
            link(v.tensor_copy(first_i[:, :], recs[:, :, 0]))
            link(v.tensor_scalar(tmp_i[:, :], first_i[:, :], 6, None, ALU.arith_shift_right))
            v.memset(first_blk[:, T:], 0.0)
            link(v.tensor_copy(first_blk[:, 0:T], tmp_i[:, :]))
            for b in range(6):
                link(v.tensor_scalar(tmp_i[:, :], first_i[:, :], b, 1, ALU.arith_shift_right, ALU.bitwise_and))
                link(v.tensor_copy(bit[:, b, :], tmp_i[:, :]))
            link(v.tensor_scalar(nbit[:, :, :], bit[:, :, :], -1.0, 1.0, ALU.mult, ALU.add))
            take(dve, deg_maxed)

            def ceil_div(dst, shift):
                link(v.tensor_scalar(chunks_f[:, :], deg_max[:, :], float((1 << shift) - 1), None, ALU.add))
                link(v.tensor_copy(tmp_i[:, :], chunks_f[:, :]))
                link(v.tensor_scalar(dst, tmp_i[:, :], shift, None, ALU.arith_shift_right))

            def starts(dst, counts):
                link(v.tensor_copy(chunks_f[:, :], counts))
                link(v.tensor_tensor_scan(start_f[:, :], zero_t[:, :], chunks_f[:, :], 0.0, ALU.add, ALU.add))
                v.tensor_scalar(cnt[:, 0:1], start_f[:, T - 1:T], (RING - 1) / 2, 1.0 / RING, ALU.add, ALU.mult)
                link(v.tensor_tensor(first_blk_at[:, :], start_f[:, :], chunks_f[:, :], ALU.subtract))
                link(v.tensor_copy(dst, first_blk_at[:, :]))

            ceil_div(blocks_i[:, :], 6)
            link(v.tensor_copy(chunks_f[:, :], blocks_i[:, :]))
            link(v.tensor_scalar(blocks_f[:, :], chunks_f[:, :], 1.0, None, ALU.max))
            link(v.tensor_copy(blocks_i[:, :], blocks_f[:, :]))
            starts(block_start_i[:, :], blocks_i[:, :])
            ceil_div(chunks_i[:, :], SLOTS.bit_length() - 1)
            starts(start_i[:, :], chunks_i[:, :])
            link(v.tensor_scalar(cnt[:, 0:1], cnt[:, 0:1], ROUND, None, ALU.add))
            link(v.tensor_scalar(cnt[:, 0:1], cnt[:, 0:1], -ROUND, None, ALU.add))
            v.tensor_copy(meta[:, 1:2], start_f[:, T - 1:T])
            link(v.tensor_copy(meta[:, 0:1], cnt[:, 0:1]))
            signal(meta_sp)
            signal(meta_pool)
            link(v.memset(tile_no[:, :], 0.0))
            def pick():
                v.tensor_scalar(pick_i[:, 0:1], at_blk[:, :], float(BLOCKS), None, ALU.min)
                link(v.tensor_scalar(pick_i[:, 1:2], at_blk[:, :], 1.0, float(BLOCKS), ALU.add, ALU.min))
                signal(pick_ready)

            link(v.tensor_copy(at_blk[:, :], first_blk[:, 0:1]))
            pick()
            dve.wait_ge(ident_done, 1)
            link(v.tensor_tensor(turn.rearrange("p (t n) -> p t n", n=P), ident[:, :].unsqueeze(1).to_broadcast([P, T, P]),
                                 recs[:, :, 3].unsqueeze(2).to_broadcast([P, T, P]), ALU.mult))
            signal(diag_ready)
            dve.wait_ge(count_zeroed, 16)
            dve.wait_ge(adj_zeroed, 16 * ZERO_FILLS)
            link.reset()
            with dve.Fori(0, T) as t:
                v.tensor_copy(blocks_left[:, :], blocks_f[:, bass.ds(t, 1)])
                link(v.tensor_copy(left[:, :], recs[:, bass.ds(t, 1), 1]))
                blocks = dve.value_load(blocks_i[0:1, bass.ds(t, 1)], min_val=1, max_val=BLOCKS + 1)
                block_start = dve.value_load(block_start_i[0:1, bass.ds(t, 1)], min_val=0, max_val=BLOCKS + T)
                link.reset()
                with dve.Fori(0, blocks) as s:
                    link(v.tensor_scalar(blocks_left[:, :], blocks_left[:, :], -1.0, None, ALU.add))
                    v.tensor_scalar(is_last[:, :], blocks_left[:, :], 0.0, None, ALU.is_le)
                    v.tensor_scalar(next_blk[:, :], at_blk[:, :], 1.0, None, ALU.add)
                    link(v.tensor_scalar(valid[:, :], slot_f[:, :], left[:, 0:1], None, ALU.is_lt))
                    link(v.tensor_tensor(at_blk[:, :], first_blk[:, bass.ds(t + 1, 1)], next_blk[:, :], ALU.subtract))
                    link(v.scalar_tensor_tensor(at_blk[:, :], at_blk[:, :], is_last[:, 0:1], next_blk[:, :], ALU.mult, ALU.add))
                    dve.wait_ge(pair_gathered, (block_start + s) * 32 + 32)
                    signal(ticks["dve"])
                    cur = pair[:, :, :].rearrange("p j n -> p (j n)")
                    for b in range(5, -1, -1):
                        keep = BLOCK + (1 << b) - 1
                        by = 2 << b
                        link(v.tensor_scalar(shift_a[:, 0:2 * keep], cur[:, 0:2 * keep], nbit[:, b, bass.ds(t, 1)], None, ALU.mult))
                        link(v.scalar_tensor_tensor(shift_b[:, 0:2 * keep], cur[:, by:by + 2 * keep], bit[:, b, bass.ds(t, 1)],
                                                    shift_a[:, 0:2 * keep], ALU.mult, ALU.add))
                        if b == 5:
                            pick()
                        cur = shift_b
                    sw_now = shift_b[:, 0:2 * BLOCK].rearrange("p (e c) -> p e c", c=2)
                    take(dve, ell_free_new)
                    v.tensor_tensor(w_valid[:, :], sw_now[:, :, 1], valid[:, :], ALU.mult)
                    link(v.scalar_tensor_tensor(srcv[:, :], sw_now[:, :, 0], float(-PAD), valid[:, :], ALU.add, ALU.mult))
                    v.tensor_scalar(ell_new[:, :, 0:SLOTS], srcv[:, :].rearrange("p (k r) -> p k r", r=SLOTS), float(PAD), None, ALU.add)
                    v.tensor_copy(ell_new[:, :, TILE_AT], tile_no[:, :].to_broadcast([P, PER_BLOCK]))
                    link(v.tensor_tensor(adj_row[:, :], sw_now[:, :, 0], dump[:, :], ALU.subtract))
                    signal(ell_ready)
                    link(v.tensor_tensor(adj_row[:, :], adj_row[:, :], valid[:, :], ALU.mult))
                    link(v.tensor_tensor(adj_row[:, :], adj_row[:, :], dump[:, :], ALU.add))
                    square = [P, BLOCK, BLOCK]
                    link(v.tensor_tensor(same[:, :, :], adj_row[:, :].unsqueeze(1).to_broadcast(square),
                                         adj_row[:, :].unsqueeze(2).to_broadcast(square), ALU.is_equal))
                    link(v.tensor_tensor(same_w, same[:, :, :], w_valid[:, :].unsqueeze(1).to_broadcast(square), ALU.mult))
                    link(v.tensor_reduce(adj_w_new[:, :], same_w, AX.X, ALU.add))
                    link(v.tensor_tensor(same[:, :, :], same[:, :, :], before[:, :, :], ALU.mult))
                    link(v.tensor_reduce(repeats[:, :], same[:, :, :], AX.X, ALU.max))
                    link(v.tensor_tensor(srcv[:, :], dump[:, :], adj_row[:, :], ALU.subtract))
                    link(v.tensor_tensor(srcv[:, :], srcv[:, :], repeats[:, :], ALU.mult))
                    link(v.tensor_tensor(adj_row[:, :], srcv[:, :], adj_row[:, :], ALU.add))
                    link(v.tensor_scalar(adj_row[:, :], adj_row[:, :], float(NA), recs[:, bass.ds(t, 1), 2], ALU.mult, ALU.add))
                    take(dve, post_free)
                    v.tensor_copy(post_i[:, :], adj_row[:, :])
                    v.tensor_copy(post_w[:, :], adj_w_new[:, :])
                    link(v.tensor_scalar(left[:, :], left[:, :], float(-BLOCK), None, ALU.add))
                    signal(post_ready)
                    link.reset()
                link(v.tensor_scalar(tile_no[:, :], tile_no[:, :], 1.0, None, ALU.add))
                link.reset()

            def layernorm(dst, room):
                def spread(s):
                    return s[:, :].unsqueeze(2).to_broadcast([P, T, D])
                link(v.tensor_reduce(ln_a[:, :], x_res[:, :, :], AX.X, ALU.add))
                link(v.tensor_scalar(ln_a[:, :], ln_a[:, :], 1.0 / D, None, ALU.mult))
                centred, square = (room[:, n * T * D:(n + 1) * T * D].rearrange("p (t f) -> p t f", f=D) for n in range(2))
                link(v.tensor_tensor(centred, x_res[:, :, :], spread(ln_a), ALU.subtract))
                link(v.tensor_tensor(square, centred, centred, ALU.mult))
                link(v.tensor_reduce(ln_a[:, :], square, AX.X, ALU.add))
                link(v.tensor_scalar(ln_b[:, :], ln_a[:, :], 1.0 / D, LN_EPS, ALU.mult, ALU.add))
                signal(sqrt_in)
                take(dve, sqrt_done)
                link(v.reciprocal(ln_c[:, :], ln_c[:, :]))
                newton(ln_c[:, :], ln_b[:, :], ln_d[:, :])
                link(v.tensor_tensor(centred, centred, spread(ln_c), ALU.mult))
                link(v.tensor_scalar(dst[:, :, :], centred, 0.0, None, ALU.max))

            def newton(y, sq, tmp):
                link(v.tensor_tensor(tmp, y, y, ALU.mult))
                link(v.tensor_tensor(tmp, tmp, sq, ALU.mult))
                link(v.tensor_scalar(tmp, tmp, -0.5, 1.5, ALU.mult, ALU.add))
                link(v.tensor_tensor(y, y, tmp, ALU.mult))

            dve.wait_ge(x_landed, 32)
            dve.wait_ge(vec_copied, 1)
            layernorm(h_in, turn)
            signal(h_ready)
            dve.wait_ge(weights_landed, 16 * WEIGHTS)
            link(v.tensor_scalar(arg, arg, freqs[:, 0:1], None, ALU.mult))
            link(v.tensor_scalar(turn, arg, 1.0 / TWO_PI, quarter[:, 0:1], ALU.mult, ALU.add))
            link(v.tensor_scalar(turn, turn, ROUND, None, ALU.add))
            link(v.tensor_scalar(turn, turn, -ROUND, None, ALU.add))
            link(v.scalar_tensor_tensor(arg, turn, -PI_HI, arg, ALU.mult, ALU.add))
            link(v.scalar_tensor_tensor(arg, turn, -PI_MID, arg, ALU.mult, ALU.add))
            link(v.scalar_tensor_tensor(arg, turn, -PI_LO, arg, ALU.mult, ALU.add))
            link(v.tensor_scalar(arg, arg, half_pi[:, 0:1], 3.1415925, ALU.add, ALU.min))
            link(v.tensor_scalar(arg, arg, -3.1415925, None, ALU.max))
            link(v.tensor_tensor(te_b2[:, :], te_b2[:, :], init_b[:, :], ALU.add))
            signal(sin_in)
            for l in range(3):
                c = head[l]
                for j in range(kin[l]):
                    rows_w = gat_w[l][:, j, 0:gat_row[l]].rearrange("p (h q) -> p h q", h=HEADS)
                    by_head = x_st[0][:, 0:GAT_OUT[l]].rearrange("p (h c) -> p h c", h=HEADS)
                    for e, to in enumerate((rows_w[:, :, c], gat_w[l][:, j, gat_row[l]:])):
                        link(v.tensor_tensor(by_head, rows_w[:, :, 0:c], att[l][:, e, :].rearrange("p (h c) -> p h c", h=HEADS), ALU.mult))
                        link(v.tensor_reduce(to, by_head, AX.X, ALU.add))
                link(v.tensor_tensor(gat_b[l][:, :], gat_b[l][:, :], adj_b[l][:, :], ALU.add))
            signal(gat_w_ready)
            rounds = dve.value_load(meta[0:1, 0:1], min_val=1, max_val=CHUNKS // RING)
            link.reset()

            def chunk_tile(u):
                return dve.value_load(ell[u][0:1, TILE_AT:TILE_AT + 1], min_val=0, max_val=T - 1)

            def in_turn(first, second):
                first(0, 0)
                link.reset()
                with dve.Fori(0, STEPS // 2) as it:
                    for u in range(2):
                        first(it * 2 + (u + 1), 1 - u)
                        second(it * 2 + u, u)
                    link.reset()
                second(STEPS - 1, 0)
                link.reset()

            def tiles_of(t, step):
                return t[:, bass.ds(step * PAIR, PAIR), :]

            def columns_of(t, k, step):
                return t[:, 0:k, bass.ds(step * (PAIR * P), PAIR * P)]

            def halves(x, k):
                return x[:, 0:k * PAIR * P].rearrange("p (k n) -> p k n", k=k)

            def tile_of(t, tile):
                return plane(t[:, bass.ds(tile, 1), :])

            for l in range(3):
                take(dve, agg_made)
                for n, width in NODE_STRIPS[1::2]:
                    link(v.tensor_copy(agg_sb[:, n:n + width], agg_ps[:, n:n + width]))
                    signal(agg_copied[1])
                for i, (n, width) in enumerate(NODE_STRIPS):
                    tiles, k = slice(n // P, (n + width) // P), width // P
                    take(dve, B_made[i % 2])
                    made = gin_out_ps[i % 2][:, 0:k * D].rearrange("p (k f) -> p k f", f=D)
                    bias = b2[l][:, :].unsqueeze(1).to_broadcast([P, k, D])
                    if l < 2:
                        link(v.tensor_tensor(h_in[:, tiles, :], made, bias, ALU.add))
                        signal(B_free[i % 2])
                        link(v.tensor_scalar(h_in[:, tiles, :], h_in[:, tiles, :], 0.0, None, ALU.max))
                    else:
                        link(v.tensor_tensor(h_in[:, tiles, :], made, bias, ALU.add))
                        signal(B_free[i % 2])
                        link(v.tensor_tensor(x_res[:, tiles, :], x_res[:, tiles, :], h_in[:, tiles, :], ALU.add))
                link.reset()
                signal(h_ready if l < 2 else x1_ready)
            dve.wait_ge(x_gathered, 16 * T)
            layernorm(h_in, rf[:, NP:2 * NP])
            signal(h_ready)
            for i, (n, width) in enumerate(STRIPS):
                dve.wait_ge(x0_made, i + 1)
                link(v.tensor_tensor(x0_t[:, n:n + width], banks[:, 2 + i % 2, 0:width], emb[:, n:n + width], ALU.add))
                signal(x0_added)
            link.reset()
            for l in range(3):
                wide, c, width = GAT_OUT[l], head[l], gat_row[l]
                sums = acc[:, 0:T * width].rearrange("p (t w) -> p t w", w=width)
                sums_h = acc[:, 0:T * width].rearrange("p (t h q) -> p t h q", h=HEADS, q=c + 1)

                def stage(step, u):
                    if l:
                        take(dve, silu_done)
                    link(v.tensor_copy(halves(x_st[u], kin[l]), columns_of(x_t, kin[l], step)))
                    signal(x_staged)

                def keep_rows(step, u):
                    take(dve, row_made, PAIR)
                    v.tensor_copy(tiles_of(sums, step), row_st[u][:, :, 0:width])
                    link(v.tensor_copy(tiles_of(sd, step), row_st[u][:, :, width:width + HEADS]))

                in_turn(stage, keep_rows)
                link(v.tensor_tensor(m_all[:, :, :], sums_h[:, :, :, c], sd[:, :, :], ALU.add))
                v.memset(sums_h[:, :, :, c], 1.0)
                link(v.scalar_tensor_tensor(m_all[:, :, :], m_all[:, :, :], LRELU_SLOPE, m_all[:, :, :], ALU.mult, ALU.max))
                link.reset()
                def shrink_sums(u, tile):
                    at = sums[:, bass.ds(tile, 1), :].rearrange("p a (h q) -> p (a h) q", h=HEADS)
                    return link.mark(v.tensor_tensor(at, at, shrink[u][:, :].unsqueeze(2).to_broadcast([P, HEADS, c + 1]), ALU.mult))

                def add_sums(u, tile, shrunk):
                    link.wait(shrunk)
                    take(dve, sum_made)
                    at = tile_of(sums, tile)
                    return link.mark(v.tensor_tensor(at, at, sum_ps[u % SUMS][:, 0:width], ALU.add))

                def known_tile(u):
                    take(dve, tile_known)
                    return chunk_tile(u)

                def kept_tile(u):
                    return dve.value_load(tile_kept[0:1, u:u + 1], min_val=0, max_val=T - 1)

                v.memset(tile_kept[:, :], T - 1)
                for u in range(RING - LAG, RING):
                    link(v.memset(shrink[u][:, :], 1.0))
                link.reset()
                with dve.Fori(0, rounds) as it:
                    tiles, row_h = [], [rows[u][:, 0:SLOTS * width].rearrange("p (r h q) -> p r h q", h=HEADS, q=c + 1) for u in range(RING)]

                    def weigh(u, tile):
                        dve.wait_ge(rows_landed[u], (it + rounds * l + 1) * GROUP)
                        signal(ticks["dve"])
                        now, before_u = bass.ds(tile, 1), (u - LAG) % RING
                        v.tensor_copy(lrel[:, SLOTS, :], plane(m_all[:, now, :]))
                        scored = link.mark(v.tensor_tensor(score[:, :, :], row_h[u][:, :, :, c],
                                                           sd[:, now, :].to_broadcast([P, SLOTS, HEADS]), ALU.add))
                        was = tiles[u - LAG] if u >= LAG else was_kept[u]
                        shrunk = shrink_sums(before_u, was)
                        link.wait(scored)
                        bent = link.mark(v.scalar_tensor_tensor(lrel[:, 0:SLOTS, :], score[:, :, :], LRELU_SLOPE, score[:, :, :], ALU.mult, ALU.max))
                        if u >= RING - LAG:
                            link.mark(v.tensor_copy(tile_kept[0:1, u:u + 1], ell[u][0:1, TILE_AT:TILE_AT + 1]))
                        added = add_sums(before_u, was, shrunk)
                        link.wait(bent)
                        top = link.mark(v.tensor_reduce(plane(m_all[:, now, :]), lrel[:, :, :].rearrange("p r h -> p h r"), AX.X, ALU.max))
                        link.wait(top)
                        link(v.tensor_tensor(ex_in[:, :, :], lrel[:, :, :], m_all[:, now, :].to_broadcast([P, SLOTS + 1, HEADS]), ALU.subtract))
                        signal(exp_in)
                        signal(ell_free)

                    was_kept = [kept_tile(u) for u in range(RING - LAG, RING)]
                    tiles += [known_tile(0), known_tile(1)]
                    weigh(0, tiles[0])
                    for u in range(RING):
                        take(dve, exp_done)
                        if u + 1 < RING:
                            weigh(u + 1, tiles[u + 1])
                        msg = row_h[u][:, :, :, 0:c]
                        v.tensor_tensor(msg, msg, row_h[u][:, :, :, c].unsqueeze(3).to_broadcast([P, SLOTS, HEADS, c]), ALU.mult)\
                            .then_inc(msg_ready, 1)
                        if u + 2 < RING:
                            tiles.append(known_tile(u + 2))
                    link.reset()
                for u in range(RING - LAG, RING):
                    tile = kept_tile(u)
                    link.wait(add_sums(u, tile, shrink_sums(u, tile)))
                link(v.reciprocal(den[:, :, :], sums_h[:, :, :, c]))

                def stage_means(step, u):
                    link(v.tensor_tensor(x_st[u][:, 0:PAIR * wide].rearrange("p (t c) -> p t c", c=c),
                                         tiles_of(sums, step).rearrange("p t (h q) -> p (t h) q", h=HEADS)[:, :, 0:c],
                                         tiles_of(den, step).rearrange("p t h -> p (t h)").unsqueeze(2).to_broadcast([P, PAIR * HEADS, c]), ALU.mult))
                    signal(x_staged)

                def means_done(step, u):
                    take(dve, means_kept)

                in_turn(stage_means, means_done)
                k = kout[l]
                link(v.tensor_reduce(bn_sum[:, 0:k], bn_parts[:, 0:k, :], AX.X, ALU.add))
                link(v.tensor_scalar(mean[:, 0:k], bn_sum[:, 0:k], -1.0 / N, None, ALU.mult))
                signal(bn_in)
                take(dve, bn_done)
                link(v.tensor_scalar(var[:, 0:k], bn_sq[:, 0:k], 1.0 / N, BN_EPS, ALU.mult, ALU.add))
                signal(sqrt_in)
                take(dve, sqrt_done)
                link(v.reciprocal(rstd[:, 0:k], rtmp[:, 0:k]))
                newton(rstd[:, 0:k], var[:, 0:k], rtmp[:, 0:k])
                link(v.tensor_tensor(scale[:, 0:k], rstd[:, 0:k], bn_g[l][:, :], ALU.mult))
                link(v.tensor_tensor(shift[:, 0:k], mean[:, 0:k], scale[:, 0:k], ALU.mult))
                link(v.tensor_tensor(shift[:, 0:k], shift[:, 0:k], bn_b[l][:, :], ALU.add))
                signal(silu_in)
                if l == 2:
                    link(v.tensor_tensor(x_res[:, :, :], x_res[:, :, :], out_b[:, :].unsqueeze(1).to_broadcast([P, T, D]), ALU.add))
                link.reset()
            def stage_out(step, u):
                take(dve, silu_done)
                link(v.tensor_copy(halves(x_st[u], 1), columns_of(x_t, 1, step)))
                signal(x_staged)

            def add_out(step, u):
                take(dve, A_made)
                at = tiles_of(x_res, step)
                link(v.tensor_tensor(at, at, A_ps[u][0][:, 0:PAIR * D].rearrange("p (t f) -> p t f", f=D), ALU.add))
                signal(fin_ready, PAIR)

            in_turn(stage_out, add_out)


WEIGHTS = 1 + 3 * 4 + 6 + sum(2 + GAT_IN[l] // P + 1 + 4 * (GAT_OUT[l] // P) for l in range(3)) + 2
ZERO_FILLS = TILES + 1
ZERO_FIRST = 12


def kernel(**inputs):
    import concourse.bacc as bacc
    from concourse.bass_utils import run_bass_kernel_spmd

    nc = bacc.Bacc("TRN2", target_bir_lowering=False, num_devices=1)
    arrays = {k: np.asarray(x) for k, x in inputs.items()}

    def padded(x, n, fill):
        y = np.full((n,), fill, x.dtype)
        y[:x.shape[0]] = x
        return y

    arrays["src"] = padded(arrays["src"], EP, 0)
    arrays["dst"] = padded(arrays["dst"], EP, 2 * NP)
    arrays["edge_weight"] = padded(arrays["edge_weight"], EP, 0)
    arrays["node_vec"] = padded(arrays["node_vec"], NP, 0)
    steps = np.arange(HALF, dtype=np.float32) / np.float32(HALF)
    arrays["freqs"] = np.tile(np.float32(1.0 / 10000.0) ** steps, 2)
    aps = {k: nc.dram_tensor(f"in_{k}", x.shape, mybir.dt.from_np(x.dtype), kind="ExternalInput").ap() for k, x in arrays.items()}
    out = nc.dram_tensor("out", (N, D), F32, kind="ExternalOutput").ap()
    program(nc, aps, out, ())
    result = run_bass_kernel_spmd(nc, [{f"in_{k}": x for k, x in arrays.items()}], core_ids=[0])
    return result.results[0]["out"]
```
